# Optimizing a Trainium2 kernel written in Bass

```python
import numpy as np
import jax
import jax.numpy as jnp

def _softmax(x, axis=-1):
    return jax.nn.softmax(x, axis=axis)

def _gelu(x):
    return jax.nn.gelu(x, approximate=True)

def _silu(x):
    return jax.nn.silu(x)

def _sigmoid(x):
    return jax.nn.sigmoid(x)

def _layernorm(x, axis=-1, eps=1e-05):
    m = jnp.mean(x, axis=axis, keepdims=True)
    v = jnp.var(x, axis=axis, keepdims=True)
    return (x - m) / jnp.sqrt(v + eps)

def _scatter_add(tgt, idx, src, axis=0):
    return tgt.at[idx].add(src)

def _segment_sum(src, seg, n):
    return jax.ops.segment_sum(src, seg, n)
kernel_name = 'mk_adj_preln_d2_adj_r2_a92edd'

def setup_inputs(seed: int=0):
    np.random.seed(seed)
    _w = jnp.asarray

    def _rec_inputs():
        import jax
        import jax.numpy as jnp
        _gk = jax.random.key(seed)
        x = 7.22e-05 + 1 * jax.random.normal(jax.random.fold_in(_gk, 1), (16, 512, 128), jnp.float32)
        _a = jax.random.bernoulli(jax.random.fold_in(_gk, 2), 0.0078125, (512, 512))
        _a = jnp.logical_or(_a, jnp.swapaxes(_a, -1, -2))
        _a = jnp.logical_or(_a, jnp.eye(512, dtype=bool))
        _af = _a.astype(jnp.float32)
        _af = _af * jax.random.uniform(jax.random.fold_in(_gk, 3), (512, 512), jnp.float32, 0.05, 0.000976562)
        adj = _af
        return (x, adj)
    x, adj = _rec_inputs()

    def _L0_gnn_setup():
        import jax, jax.numpy as jnp
        import numpy as np
        N_STEPS = 8
        SPATIAL_SCALE = 1.0
        key = jax.random.key(seed)
        ks = jax.random.split(key, 6)
        B, N, D = (32, 512, 128)
        x = jax.random.normal(ks[0], (B, N, D), dtype=jnp.float32)
        adj_mx = jax.random.uniform(ks[1], (N, N), dtype=jnp.float32) / N
        alpha_train = jnp.ones((N,), dtype=jnp.float32)
        w = jnp.eye(D, dtype=jnp.float32) + 0.01 * jax.random.normal(ks[2], (D, D), dtype=jnp.float32)
        d = jax.random.uniform(ks[3], (D,), dtype=jnp.float32)
        fc_in_w = jax.random.normal(ks[4], (D, D), dtype=jnp.float32) * (1.0 / np.sqrt(D))
        fc_in_b = jnp.zeros((D,), dtype=jnp.float32)
        return {'x': x, 'adj_mx': adj_mx, 'alpha_train': alpha_train, 'w': w, 'd': d, 'fc_in_w': fc_in_w, 'fc_in_b': fc_in_b, 'vt': 0}
    _L0_gnn_all = _L0_gnn_setup()
    _L0_gnn_in = {k: v for k, v in _L0_gnn_all.items() if k in ('alpha_train', 'w', 'd', 'fc_in_w', 'fc_in_b')}
    del _L0_gnn_all

    def _L1_gnn_setup():
        import jax, jax.numpy as jnp
        import numpy as np
        BT, N, D, HEADS, E = (512, 64, 128, 4, 256)
        LRELU_SLOPE = 0.2
        EPS = 1e-08
        key = jax.random.key(seed)
        ks = jax.random.split(key, 8)
        d = D
        return {'H': jax.random.normal(ks[0], (BT, N, d), jnp.float32), 'W_lin': jax.random.normal(ks[1], (d, d), jnp.float32) / np.sqrt(d).astype(np.float32), 'W_val': jax.random.normal(ks[2], (d, d), jnp.float32) / np.sqrt(d).astype(np.float32), 'a': jax.random.normal(ks[3], (HEADS, d // HEADS), jnp.float32), 'W_out': jax.random.normal(ks[4], (d, d), jnp.float32) / np.sqrt(d).astype(np.float32), 'A0': jax.random.uniform(ks[5], (N, N), jnp.float32), 'src': jax.random.randint(ks[6], (E,), 0, N, jnp.int32), 'dst': jax.random.randint(ks[7], (E,), 0, N, jnp.int32)}
    _L1_gnn_all = _L1_gnn_setup()
    _L1_gnn_in = {k: v for k, v in _L1_gnn_all.items() if k in ('W_lin', 'W_val', 'a', 'W_out', 'src', 'dst')}
    del _L1_gnn_all
    return {'x': x, 'adj': adj, 'L0_gnn_alpha_train': _L0_gnn_in['alpha_train'], 'L0_gnn_w': _L0_gnn_in['w'], 'L0_gnn_d': _L0_gnn_in['d'], 'L0_gnn_fc_in_w': _L0_gnn_in['fc_in_w'], 'L0_gnn_fc_in_b': _L0_gnn_in['fc_in_b'], 'L1_gnn_W_lin': _L1_gnn_in['W_lin'], 'L1_gnn_W_val': _L1_gnn_in['W_val'], 'L1_gnn_a': _L1_gnn_in['a'], 'L1_gnn_W_out': _L1_gnn_in['W_out'], 'L1_gnn_src': _L1_gnn_in['src'], 'L1_gnn_dst': _L1_gnn_in['dst']}

def reference(x, adj, L0_gnn_alpha_train, L0_gnn_w, L0_gnn_d, L0_gnn_fc_in_w, L0_gnn_fc_in_b, L1_gnn_W_lin, L1_gnn_W_val, L1_gnn_a, L1_gnn_W_out, L1_gnn_src, L1_gnn_dst):
    import jax
    import jax.numpy as jnp

    def _L0_gnn_ref(x, adj_mx, alpha_train, w, d, fc_in_w, fc_in_b, vt):
        import jax, jax.numpy as jnp
        import numpy as np
        N_STEPS = 8
        SPATIAL_SCALE = 1.0
        x0 = jax.lax.stop_gradient(x)
        h = jnp.einsum('bnd,ed->bne', x, fc_in_w) + fc_in_b
        alph = jax.nn.sigmoid(alpha_train)[:, None]
        d_clamped = jnp.clip(d, 0.0, 1.0)
        w_eff = w * d_clamped @ w.T
        dt = jnp.float32(SPATIAL_SCALE / N_STEPS)

        def euler_step(h, _):
            ax = jnp.einsum('nm,bmd->bnd', adj_mx, h)
            f = alph * 0.5 * (ax - h) + h @ w_eff - h + x0
            return (h + dt * f, None)
        h, _ = jax.lax.scan(euler_step, h, None, length=N_STEPS)
        return h

    def _L1_gnn_ref(H, W_lin, W_val, a, W_out, A0, src, dst):
        import jax, jax.numpy as jnp
        import numpy as np
        BT, N, D, HEADS, E = (512, 64, 128, 4, 256)
        LRELU_SLOPE = 0.2
        EPS = 1e-08
        bt, n, d = H.shape
        h, dh = a.shape
        Xq = (H @ W_lin.T).reshape(bt, n, h, dh)
        Xv = (H @ W_val.T).reshape(bt, n, h, dh)
        Qs = Xq[:, src]
        Kt = Xq[:, dst]
        e = jnp.einsum('behd,hd->beh', jax.nn.leaky_relu(Qs + Kt, LRELU_SLOPE), a)
        e = e + jnp.log(A0[src, dst] + EPS)[None, :, None]
        e_t = e.transpose(1, 0, 2)
        m = jax.ops.segment_max(e_t, src, num_segments=n)
        ex = jnp.exp(e_t - m[src])
        denom = jax.ops.segment_sum(ex, src, num_segments=n)
        attn = ex / denom[src]
        Vt = Xv[:, dst].transpose(1, 0, 2, 3)
        Y = jax.ops.segment_sum(attn[..., None] * Vt, src, num_segments=n)
        Y = Y.transpose(1, 0, 2, 3).reshape(bt, n, d)
        return Y @ W_out.T
    h = jnp.maximum(_layernorm(x, axis=-1), 0.0)
    x = x + _L0_gnn_ref(h, adj, L0_gnn_alpha_train, L0_gnn_w, L0_gnn_d, L0_gnn_fc_in_w, L0_gnn_fc_in_b, 0)
    h = jnp.maximum(_layernorm(x, axis=-1), 0.0)
    x = x + _L1_gnn_ref(h, L1_gnn_W_lin, L1_gnn_W_val, L1_gnn_a, L1_gnn_W_out, adj, L1_gnn_src, L1_gnn_dst)
    return x

_drawn_inputs = setup_inputs


def setup_inputs(seed=0):
    import zlib

    import numpy as np

    out = dict(_drawn_inputs(seed))
    spreads = {'L0_gnn_alpha_train': (1.0, 0.2), 'L0_gnn_fc_in_b': (0.0, 0.1)}
    factors = {}
    for name, (base, spread) in spreads.items():
        noise = np.random.default_rng([zlib.crc32(name.encode()), seed]).standard_normal(out[name].shape)
        drawn = base * np.exp(spread * noise) if base else spread * noise
        out[name] = jnp.asarray(drawn.astype(out[name].dtype))
    for name, factor in factors.items():
        out[name] = (out[name] * factor).astype(out[name].dtype)
    return out
```

```python
from contextlib import ExitStack
from math import comb

import concourse.bass as bass
from concourse import mybir

ALU = mybir.AluOpType
ACT = mybir.ActivationFunctionType
AX_X = mybir.AxisListType.X
F32 = mybir.dt.float32
F32R = mybir.dt.float32r
I32 = mybir.dt.int32
U32 = mybir.dt.uint32

P = 128
STEPS = 8
DT = 1.0 / STEPS
POW = 3
LN_EPS = 1e-5
LOG_EPS = 1e-8
SLOPE = 0.2
FAR = -1e30
LEAST = -3e38


def gnn_two_layers(nc, x, adj, alpha, w, d, fc_w, fc_b, W_lin, W_val, a, W_out, src, dst, out):
    B, N, D = x.shape
    E = src.shape[0]
    HEADS, DH = a.shape
    NT = N // P
    ET = E // P
    GB = 4
    NG = B // GB
    W = GB * D
    GH = GB * HEADS
    BLOCKS = (STEPS + POW) // POW
    assert D == P and N == NT * P and E == 2 * P and NT == 4 and BLOCKS == 3 and W == 512

    with ExitStack() as ctx:
        def sb(name, shape, dt=F32, where=ctx):
            return where.enter_context(nc.sbuf_tensor(name, shape, dt))

        def sem(name):
            return ctx.enter_context(nc.semaphore(name))

        X = sb("X", [P, NG, GB, NT, D])
        MT = [sb(f"MT{j}_{k}", [P, NT, N], F32R) for j in (1, 2, 3) for k in ("hi", "lo")]
        M1h, M1l, M2h, M2l, M3h, M3l = MT
        Zh = sb("Zh", [P, POW, BLOCKS * D], F32R)
        Zl = sb("Zl", [P, POW, BLOCKS * D], F32R)
        TB = sb("TB", [P, NT, D])
        gat = sb("gat", [P, NT, 2 * E], F32R)
        scat = sb("scat", [P, ET, N], F32R)
        linh, linl, valh, vall, outh, outl = [
            sb(n, [P, D], F32R) for n in ("linh", "linl", "valh", "vall", "outh", "outl")]
        ident = sb("ident", [P, P])
        identr = sb("identr", [P, P], F32R)
        apad = sb("apad", [P, GB, GH])
        sel = sb("sel", [GH, GB, P])
        lgrow = sb("lgrow", [GH, E])
        far = sb("far", [GH, E + 1])
        same = sb("same", [GH, E + 1])
        mean1 = sb("mean1", [P, NG * GB * NT])
        rstd1 = sb("rstd1", [P, NG * GB * NT])
        stats = sb("stats", [P, GB * NT, 6])
        lnw = sb("lnw", [P, 6, GB * NT])
        nodecol = sb("nodecol", [P, NT])
        scol_col = sb("scol_col", [P, NT])
        ccol = sb("ccol", [P, NT])

        xt = sb("xt", [P, NT * D])
        x0h = sb("x0h", [P, 2, NT, D], F32R)
        x0l = sb("x0l", [P, 2, NT, D], F32R)
        Vh = sb("Vh", [P, 2, POW, N], F32R)
        Vl = sb("Vl", [P, 2, POW, N], F32R)
        vv = sb("vv", [P, GB, E])
        sm = [sb(f"sm{i}", [GH, E]) for i in range(3)]
        with ExitStack() as before:
            lr = sb("lr", [P, 2 * E], F32, before)
            lrt = sb("lrt", [P, 2 * E], F32, before)
        avh = sb("avh", [P, 2, E], F32R)
        avl = sb("avl", [P, 2, E], F32R)

        with ExitStack() as early:
            A = sb("A", [P, NT, N], F32, early)
            Mf = sb("Mf", [P, NT, NT, P], F32, early)
            Mh = sb("Mh", [P, NT, NT, P], F32R, early)
            Ml = sb("Ml", [P, NT, NT, P], F32R, early)
            stack = sb("stack", [P, STEPS + 1, 2 * D + 1], F32, early)
            wraw = sb("wraw", [P, 4, D], F32, early)
            feat = sb("feat", [P, 4, D], F32, early)
            irow = sb("irow", [P, 2, E], I32, early)
        with ExitStack() as middle_scope:
            sb("skip", [P, 3 * NT * W], F32, middle_scope)
            bb = sb("bb", [P, NT, BLOCKS * D], F32, middle_scope)
            tbh = sb("tbh", [P, NT, D], F32R, middle_scope)
            tbl = sb("tbl", [P, NT, D], F32R, middle_scope)
            crow = sb("crow", [POW, BLOCKS * D], F32, middle_scope)
            onesr = sb("onesr", [P, N], F32R, middle_scope)
            rowsel = sb("rowsel", [P, POW, P], F32R, middle_scope)
            ecolb = sb("ecolb", [P, 2, ET, P], F32, middle_scope)
            perm = sb("perm", [P, ET, E], F32, middle_scope)
            rowf = sb("rowf", [P, E], F32, middle_scope)
            keyrow = sb("keyrow", [P, E], F32, middle_scope)
            nrow = sb("nrow", [P, 2, E], F32, middle_scope)
        B2h = sb("B2h", [P, NT, W], F32R)
        B2l = sb("B2l", [P, NT, W], F32R)
        B1 = sb("B1", [P, NT, W])
        Ch = sb("Ch", [P, NT, W], F32R)
        Cl = sb("Cl", [P, NT, W], F32R)
        Gh = sb("Gh", [P, 2, 2 * E], F32R)
        Gl = sb("Gl", [P, 2, 2 * E], F32R)
        wT, wTd, R = feat[:, 0, :], feat[:, 1, :], feat[:, 2, :]
        zt = vv[:, :, :].rearrange("p b e -> p (b e)")
        urow = zt[0:POW, 0:N]
        nodegrid = lrt[:, :]
        egrid = lr[:, 0:E]
        idgrid = lr[:, E:E + P]
        small = sb("small", [P, 64])
        tiny = sb("tiny", [P, 32])
        colf = tiny[:, 0:2 * ET].rearrange("p (t s) -> p t s", s=2)
        keycol, rank = tiny[:, 4:4 + ET], tiny[:, 6:6 + ET]
        ncol = tiny[:, 8:8 + 2 * ET].rearrange("p (t s) -> p t s", s=2)
        hm = tiny[:, 16:16 + 2 * HEADS]
        logb = sb("logb", [P, ET, GH])
        icol = sb("icol", [P, 2, ET], I32)
        flat = sb("flat", [P, ET], U32)
        picked = sb("picked", [P, ET])

        def ztk(k):
            return zt[:, k * D:(k + 1) * D] if k < STEPS else feat[:, 3, :]

        def ccols(i):
            return small[:, 22 + POW * i:22 + POW * (i + 1)]

        bank = [ctx.enter_context(nc.psum_tensor(f"bank{i}", [P, 512], F32)) for i in range(8)]
        PV, PZ, PA, PL = bank[0:2], bank[2:4], bank[4:6], bank[6:8]

        names = """ld_adj ld_alpha ld_w ld_stack ld_cols ld_idx ld_l1 iota_done
            sig_done m_step m_done m_hi m_lo mt_mm mt_hi mt_lo z_step r_mm r_sb st_mm st_sb
            zt_done zt_mm zk_hi zk_lo ln1_step ln1_var ln1_std ln1_done w_mm3 w_hi w_lo id_done
            tb_step tb_mm u_sb bb_sb tb_hi tb_lo tb_out tb_added
            ed_step ed_mm ed_sb ed_flat ed_pick ed_picked ed_log ed_done lg_mm
            x0_t x0_hi x0_lo v_mm v_hi v_lo z_mm z_hi z_lo a1_mm a1_sum c_hi c_lo a2_mm a2_out
            ln2_step ln2_var ln2_std h_t h_hi h_lo g_mm g_hi g_lo u_mm u_t u_lr q_mm q_cp e_mm
            soft_step e_shift e_exp attn_ready bc_mm av_f av_hi av_lo y_mm y_hi y_lo s_mm s_out stored
            """.split()
        S = type("Semaphores", (), {n: sem(n) for n in names})
        x_loaded = [sem(f"x_loaded{g}") for g in range(NG)]

        x_d = x.rearrange("(g b) (p t) d -> g p b t d", b=GB, t=NT)
        out_d = out.rearrange("(g b) (p t) d -> g p b t d", b=GB, t=NT)

        def xg(g, b=None, t=None):
            v = X[:, bass.ds(g, 1), :, :, :]
            if t is None:
                return v[:, :, b, :, :].rearrange("p o t d -> p (o t) d")
            if b is None:
                return v[:, :, :, t, :].rearrange("p o b d -> p (o b) d")
            return v[:, :, b, t, :].rearrange("p o d -> p (o d)")

        def ht(t):
            return (lrt if t % 2 else xt)[:, :]

        def part(t):
            return slice(t * P, (t + 1) * P)

        block = ctx.enter_context(nc.Block())

        @block.sync
        def _(sp):
            sp.dma_start(A[:, :, :], adj.rearrange("(p t) m -> p t m", t=NT)).then_inc(S.ld_adj, 16)
            sp.dma_start(small[:, 0:NT], alpha.rearrange("(p t) -> p t", t=NT)).then_inc(S.ld_alpha, 16)
            sp.dma_start(wraw[:, 0, :], w).then_inc(S.ld_w, 16)
            sp.dma_start(small[:, 4:5], d.rearrange("(p o) -> p o", o=1)).then_inc(S.ld_cols, 16)
            sp.dma_start(small[:, 5:6], a.rearrange("h (e o) -> (h e) o", o=1)).then_inc(S.ld_cols, 16)
            sp.dma_start(stack[:, 0, 0:D], fc_w).then_inc(S.ld_stack, 16)
            sp.dma_start(stack[:, 0, 2 * D:2 * D + 1], fc_b.rearrange("(p o) -> p o", o=1)).then_inc(S.ld_stack, 16)
            for g in range(NG):
                sp.dma_start(X[:, g, :, :, :], x_d[g]).then_inc(x_loaded[g], 16)
            for i, m in enumerate((W_lin, W_val, W_out)):
                sp.dma_start(wraw[:, 1 + i, :], m).then_inc(S.ld_l1, 16)
            for i, e in enumerate((src, dst)):
                sp.dma_start(irow[:, i, :], e.partition_broadcast(P)).then_inc(S.ld_idx, 16)
                sp.dma_start(icol[:, i, :], e.rearrange("(p t) -> p t", t=ET)).then_inc(S.ld_idx, 16)
            with sp.Fori(0, NG) as g:
                sp.wait_ge(S.s_out, g * NT + NT)
                sp.dma_start(out_d[bass.ds(g, 1)].rearrange("o p b t d -> (o p) b t d"),
                             X[:, bass.ds(g, 1), :, :, :].rearrange("p o b t d -> p (o b) t d")).then_inc(S.stored, 16)
            sp.wait_ge(S.stored, 16 * NG)

        @block.gpsimd
        def _(pool):
            exact = dict(allow_small_or_imprecise_dtypes=True)
            pool.iota(idgrid, [[1, P]], base=0, channel_multiplier=-1, **exact).then_inc(S.iota_done, 1)
            pool.iota(nodecol[:, :], [[1, NT]], base=0, channel_multiplier=NT, **exact).then_inc(S.iota_done, 1)
            pool.iota(nodegrid, [[1, NT], [NT, P]], base=0, channel_multiplier=0, **exact).then_inc(S.iota_done, 1)
            pool.iota(egrid, [[1, E]], base=0, channel_multiplier=0, **exact).then_inc(S.iota_done, 1)
            pool.iota(small[:, 8:8 + ET], [[1, ET]], base=0, channel_multiplier=ET, **exact).then_inc(S.iota_done, 1)
            pool.iota(small[:, 12:12 + HEADS], [[-DH, HEADS]], base=0, channel_multiplier=1, **exact).then_inc(S.iota_done, 1)
            pool.iota(sel[:, :, :].rearrange("p b (h e) -> p b h e", h=HEADS), [[HEADS, GB], [1, HEADS], [0, DH]],
                      base=0, channel_multiplier=-1, **exact).then_inc(S.iota_done, 1)
            pool.memset(apad[:, :, :], 0.0).then_inc(S.iota_done, 1)
            pool.wait_ge(S.ed_flat, 1)
            for t in range(ET):
                pool.indirect_dma_start(
                    picked[:, t:t + 1], None, adj.rearrange("n (m o) -> (n m) o", o=1),
                    bass.IndirectOffsetOnAxis(ap=flat[:, t:t + 1], axis=0)).then_inc(S.ed_picked, 16)

        @block.tensor
        def _(pe):
            def product(o, ah, al, bh, bl, start, stop):
                pe.matmul(o, ah, bh, start=start, stop=False)
                pe.matmul(o, ah, bl, start=False, stop=False)
                return pe.matmul(o, al, bh, start=False, stop=stop)

            def setup_features():
                pe.wait_ge(S.id_done, 1)
                pe.wait_ge(S.ld_w, 16)
                pe.transpose(PZ[0][:, 0:P], wraw[:, 0, :], ident[:, :]).then_inc(S.r_mm, 1)
                pe.wait_ge(S.r_sb, 2)
                pe.matmul(PZ[0][:, P:2 * P], wTd, wT, start=True, stop=True).then_inc(S.r_mm, 1)

            def setup_power(i):
                if i == 1:
                    pe.wait_ge(S.ld_stack, 32)
                    pe.wait_ge(S.r_sb, 3)
                else:
                    pe.wait_ge(S.st_sb, i - 1)
                pe.matmul(PZ[1][:, 0:2 * D + 1], R, stack[:, i - 1, :], start=True, stop=True).then_inc(S.st_mm, 1)

            def setup_transposes():
                for c in range(NT):
                    if c == 0:
                        pe.wait_ge(S.m_done, NT)
                    for t in range(NT):
                        mm = pe.transpose((PV + PA)[c][:, part(t)], Mf[:, t, c, :], ident[:, :])
                    mm.then_inc(S.mt_mm, 1)

            def setup_square(j, inh, inl):
                pe.wait_ge(S.m_lo, 1)
                pe.wait_ge(S.mt_lo, NT * (j - 1))
                for c in range(NT):
                    for t in range(NT):
                        mm = product((PV + PA)[c][:, :], Mh[:, t, c, :], Ml[:, t, c, :], inh[:, t, :], inl[:, t, :],
                                     t == 0, t == NT - 1)
                    mm.then_inc(S.mt_mm, 1)

            def setup_z():
                for k in range(STEPS + 1):
                    if k == 0:
                        pe.wait_ge(S.zt_done, 1)
                    if k >= 2:
                        pe.wait_ge(S.zk_lo, k - 1)
                    pe.transpose(PZ[k % 2][:, 0:P], ztk(k), ident[:, :]).then_inc(S.zt_mm, 1)

            def setup_weights():
                pe.wait_ge(S.ld_l1, 48)
                for i in range(3):
                    mm = pe.transpose(PL[0][:, part(i)], wraw[:, 1 + i, :], ident[:, :])
                mm.then_inc(S.w_mm3, 1)

            def setup_bias():
                pe.wait_ge(S.tb_step, 3)
                pe.wait_ge(S.w_lo, 1)
                pe.wait_ge(S.mt_lo, 2 * NT)
                n = 0
                for j, parts in enumerate(([onesr[:, :]], [M1h, M1l], [M2h, M2l])):
                    for m in parts:
                        for t in range(NT if j else 1):
                            rhs = m[:, t, :] if j else onesr[:, :]
                            mm = pe.matmul(PL[0][:, :], rowsel[:, j, :], rhs, start=(n == 0), stop=(n == 4 * NT))
                            n += 1
                mm.then_inc(S.tb_mm, 1)
                for i in range(BLOCKS):
                    mm = pe.transpose(PL[1][0:POW, part(i)], ccols(i), ident[:, :])
                mm.then_inc(S.tb_mm, 1)
                pe.wait_ge(S.u_sb, 2)
                for t in range(NT):
                    if t >= 2:
                        pe.wait_ge(S.bb_sb, t - 1)
                    pe.matmul(PL[t % 2][:, 0:BLOCKS * D], urow[:, part(t)], crow[:, :], start=True, stop=True).then_inc(S.tb_mm, 1)
                pe.wait_ge(S.mt_lo, 3 * NT)
                for r in range(2):
                    pe.wait_ge(S.tb_lo, r + 1)
                    for t in range(NT):
                        for m in range(NT):
                            mm = product(PL[r][:, part(t)], M3h[:, m, part(t)], M3l[:, m, part(t)],
                                         tbh[:, m, :], tbl[:, m, :], m == 0, m == NT - 1)
                    mm.then_inc(S.tb_mm, 1)

            def setup_edges():
                pe.wait_ge(S.ed_step, 5)
                pe.wait_ge(S.tb_out, 1)
                for s in range(2):
                    for t in range(ET):
                        mm = pe.matmul(PL[0][:, s * E:(s + 1) * E], ecolb[:, s, t, :], perm[:, t, :], start=(t == 0), stop=(t == ET - 1))
                for r in range(ET):
                    for t in range(ET):
                        mm = pe.matmul(PL[1][:, 2 * r:2 * r + 2], perm[:, t, part(r)], colf[:, t, :], start=(t == 0), stop=(t == ET - 1))
                mm.then_inc(S.ed_mm, 1)

            def setup_logs():
                pe.wait_ge(S.ed_log, 2)
                for t in range(ET):
                    mm = pe.matmul(PL[0][0:GH, part(t)], logb[:, t, :], ident[:, :], start=True, stop=True)
                mm.then_inc(S.lg_mm, 1)

            def powers(g, b):
                n = g * GB + b
                pe.wait_ge(S.x0_lo, n + 1)
                xs = b % 2
                for j in range(POW):
                    i = g * (GB * POW) + (b * POW + j)
                    o = PV[(b * POW + j) % 2]
                    first = type(g) is int and g == 0 and b == 0
                    if not (first and j < 2):
                        pe.wait_ge(S.v_lo, i - 1)
                    if first and j < 2:
                        pe.wait_ge(S.mt_lo, 3 * NT)
                    for t in range(NT):
                        if j == 0:
                            pe.matmul(o[:, part(t)], x0h[:, xs, t, :], identr[:, :], start=True, stop=False)
                            mm = pe.matmul(o[:, part(t)], x0l[:, xs, t, :], identr[:, :], start=False, stop=True)
                        else:
                            mh, ml = (M1h, M1l) if j == 1 else (M2h, M2l)
                            mm = product(o[:, :], x0h[:, xs, t, :], x0l[:, xs, t, :], mh[:, t, :], ml[:, t, :],
                                         t == 0, t == NT - 1)
                    mm.then_inc(S.v_mm, 1)

            def blocks(g, b):
                for t in range(NT):
                    i = g * (GB * NT) + (b * NT + t)
                    if t == 0:
                        pe.wait_ge(S.v_lo, g * (GB * POW) + (b * POW + POW))
                    if type(g) is int and g == 0 and b == 0 and t < 2:
                        pe.wait_ge(S.zk_lo, STEPS + 1)
                    else:
                        pe.wait_ge(S.z_lo, i - 1)
                    o = PZ[t % 2][:, 0:BLOCKS * D]
                    for j in range(POW):
                        mm = product(o, Vh[:, b % 2, j, part(t)], Vl[:, b % 2, j, part(t)], Zh[:, j, :], Zl[:, j, :],
                                     j == 0, j == POW - 1)
                    mm.then_inc(S.z_mm, 1)

            def cube(g, t, stage):
                if stage == 1:
                    if t == 0:
                        pe.wait_ge(S.z_lo, g * (GB * NT) + GB * NT)
                        if not (type(g) is int and g == 0):
                            pe.wait_ge(S.av_f, g * 2)
                    if t >= 2:
                        pe.wait_ge(S.a1_sum, g * NT + (t - 1))
                    bh, bl = B2h, B2l
                else:
                    if t == 0:
                        pe.wait_ge(S.c_lo, g * NT + NT)
                    if t >= 2:
                        pe.wait_ge(S.a2_out, g * NT + (t - 1))
                    bh, bl = Ch, Cl
                for m in range(NT):
                    mm = product(PA[t % 2][:, :], M3h[:, m, part(t)], M3l[:, m, part(t)], bh[:, m, :], bl[:, m, :],
                                 m == 0, m == NT - 1)
                mm.then_inc(S.a1_mm if stage == 1 else S.a2_mm, 1)

            def gather(g, b):
                if b == 0:
                    pe.wait_ge(S.h_lo, g * NT + NT)
                if b == 2:
                    pe.wait_ge(S.u_lr, g * 2 + 1)
                elif b == 3:
                    pe.wait_ge(S.q_cp, g * 2 + 1)
                o = PL[b % 2][:, :]
                for t in range(NT):
                    pe.matmul(o, Ch[:, t, part(b)], gat[:, t, :], start=(t == 0), stop=False)
                    mm = pe.matmul(o, Cl[:, t, part(b)], gat[:, t, :], start=False, stop=(t == NT - 1))
                mm.then_inc(S.g_mm, 1)

            def project(g, p):
                pe.wait_ge(S.g_lo, g * GB + (2 * p + 2))
                product(PL[0][:, :], linh[:, :], linl[:, :], Gh[:, :, 0:E], Gl[:, :, 0:E], True, True).then_inc(S.u_mm, 1)
                product(PL[1][:, :], valh[:, :], vall[:, :], Gh[:, :, E:2 * E], Gl[:, :, E:2 * E], True, True).then_inc(S.q_mm, 1)

            def scores(g, p):
                pe.wait_ge(S.u_lr, g * 2 + (p + 1))
                if p == 0:
                    pe.wait_ge(S.a2_out, g * NT + NT)
                for b in range(2 * p, 2 * p + 2):
                    mm = pe.matmul(PA[0][0:GH, 0:E], apad[:, b, :], lr[:, (b % 2) * E:(b % 2 + 1) * E],
                                   start=(b == 0), stop=(b == GB - 1))
                mm.then_inc(S.e_mm, 1)

            def spread(g, p):
                if p == 0:
                    pe.wait_ge(S.attn_ready, g + 1)
                for b in range(2 * p, 2 * p + 2):
                    mm = pe.matmul(PA[1 - p][:, (b % 2) * E:(b % 2 + 1) * E], sel[:, b, :], sm[1][:, :], start=True, stop=True)
                mm.then_inc(S.bc_mm, 1)

            def project_out(g, p):
                pe.wait_ge(S.av_lo, g * 2 + (p + 1))
                if p == 0:
                    pe.wait_ge(S.u_lr, g * 2 + 2)
                    pe.wait_ge(S.q_cp, g * 2 + 2)
                for t in range(ET):
                    for b in range(2 * p, 2 * p + 2):
                        mm = product(PL[t][:, part(b)], avh[:, b % 2, part(t)], avl[:, b % 2, part(t)],
                                     outh[:, :], outl[:, :], True, True)
                mm.then_inc(S.y_mm, 1)

            def scatter(g, t):
                if t == 0:
                    pe.wait_ge(S.y_lo, g * ET + ET)
                if t >= 2:
                    pe.wait_ge(S.s_out, g * NT + (t - 1))
                for r in range(ET):
                    pe.matmul(PL[t % 2][:, :], scat[:, r, part(t)], Gh[:, r, :], start=(r == 0), stop=False)
                    mm = pe.matmul(PL[t % 2][:, :], scat[:, r, part(t)], Gl[:, r, :], start=False, stop=(r == ET - 1))
                mm.then_inc(S.s_mm, 1)

            def first_body():
                powers(0, 0)
                powers(0, 1)
                setup_z()
                blocks(0, 0)
                powers(0, 2)
                setup_bias()
                blocks(0, 1)
                powers(0, 3)
                setup_edges()
                blocks(0, 2)
                blocks(0, 3)
                setup_logs()
                pe.wait_ge(S.ed_done, 2)
                for stage in (1, 2):
                    for t in range(NT):
                        cube(0, t, stage)

            def body(g):
                l = g - 1
                powers(g, 0)
                powers(g, 1)
                gather(l, 0)
                gather(l, 1)
                blocks(g, 0)
                project(l, 0)
                powers(g, 2)
                scores(l, 0)
                gather(l, 2)
                gather(l, 3)
                blocks(g, 1)
                project(l, 1)
                powers(g, 3)
                scores(l, 1)
                blocks(g, 2)
                spread(l, 0)
                blocks(g, 3)
                spread(l, 1)
                project_out(l, 0)
                cube(g, 0, 1)
                cube(g, 1, 1)
                project_out(l, 1)
                cube(g, 2, 1)
                cube(g, 3, 1)
                scatter(l, 0)
                scatter(l, 1)
                cube(g, 0, 2)
                scatter(l, 2)
                scatter(l, 3)
                for t in range(1, NT):
                    cube(g, t, 2)

            setup_features()
            setup_power(1)
            setup_transposes()
            for i in range(2, STEPS + 1):
                setup_power(i)
            setup_square(2, M1h, M1l)
            setup_weights()
            setup_square(3, M2h, M2l)
            first_body()
            with pe.Fori(1, NG - 1) as g:
                body(g)
            body(NG - 1)
            l = NG - 1
            for p in range(2):
                gather(l, 2 * p)
                gather(l, 2 * p + 1)
                project(l, p)
                scores(l, p)
            for p in range(2):
                spread(l, p)
                project_out(l, p)
            for t in range(NT):
                scatter(l, t)

        @block.scalar
        def _(act):
            def copy(o, i):
                return act.activation(o, i, ACT.Copy)

            def x0_round(g, b):
                n = g * GB + b
                act.wait_ge(S.x0_t, n + 1)
                if not (type(g) is int and g == 0 and b < 2):
                    act.wait_ge(S.v_mm, n * POW - POW)
                act.activation(x0h[:, b % 2, :, :].rearrange("p t d -> p (t d)"), xt[:, :], ACT.Relu).then_inc(S.x0_hi, 1)

            def powers(g, b):
                n = g * GB + b
                for j in range(POW):
                    act.wait_ge(S.v_mm, g * (GB * POW) + (b * POW + j + 1))
                    if j == 0 and not (type(g) is int and g == 0 and b < 2):
                        act.wait_ge(S.z_mm, n * NT - NT)
                    copy(Vh[:, b % 2, j, :], PV[(b * POW + j) % 2][:, :]).then_inc(S.v_hi, 1)

            def blocks(g, b):
                for t in range(NT):
                    act.wait_ge(S.z_mm, g * (GB * NT) + (b * NT + t + 1))
                    if b == 0 and t == 0:
                        if type(g) is int and g == 0:
                            act.wait_ge(S.mt_mm, 3 * NT)
                            act.wait_ge(S.tb_step, 2)
                            act.wait_ge(S.zt_done, 1)
                        else:
                            act.wait_ge(S.c_lo, g * NT)
                            act.wait_ge(S.a1_mm, g * NT)
                    copy(B1[:, t, part(b)], PZ[t % 2][:, D:2 * D])
                    copy(B2h[:, t, part(b)], PZ[t % 2][:, 2 * D:3 * D]).then_inc(S.z_hi, 1)

            def middle(g, t):
                act.wait_ge(S.a1_sum, g * NT + (t + 1))
                if t == 0 and not (type(g) is int and g == 0):
                    act.wait_ge(S.g_mm, g * GB)
                copy(Ch[:, t, :], B1[:, t, :]).then_inc(S.c_hi, 1)

            def second_norm(g):
                act.wait_ge(S.ln2_var, g + 1)
                act.activation(lnw[:, 4, :], lnw[:, 3, :], ACT.Sqrt).then_inc(S.ln2_std, 1)
                for t in range(NT):
                    act.wait_ge(S.h_t, g * NT + (t + 1))
                    if t == 0:
                        act.wait_ge(S.a2_mm, g * NT + NT)
                    act.activation(Ch[:, t, :], ht(t), ACT.Relu).then_inc(S.h_hi, 1)

            def gather(g, b):
                act.wait_ge(S.g_mm, g * GB + (b + 1))
                if b == 2:
                    act.wait_ge(S.q_mm, g * 2 + 1)
                copy(Gh[:, b % 2, :], PL[b % 2][:, :]).then_inc(S.g_hi, 1)

            def project(g, p):
                act.wait_ge(S.u_mm, g * 2 + (p + 1))
                act.activation(lrt[:, :], PL[0][:, :], ACT.Copy, scale=SLOPE).then_inc(S.u_t, 1)
                act.wait_ge(S.q_mm, g * 2 + (p + 1))
                copy(vv[:, 2 * p:2 * p + 2, :].rearrange("p b e -> p (b e)"), PL[1][:, :]).then_inc(S.q_cp, 1)

            def exponent(g):
                act.wait_ge(S.e_shift, g + 1)
                act.activation(sm[2][:, :], sm[1][:, :], ACT.Exp).then_inc(S.e_exp, 1)

            def weigh(g, p):
                act.wait_ge(S.av_f, g * 2 + (p + 1))
                if p == 1:
                    act.wait_ge(S.y_mm, g * 2 + 1)
                copy(avh[:, :, :].rearrange("p b e -> p (b e)"),
                     vv[:, 2 * p:2 * p + 2, :].rearrange("p b e -> p (b e)")).then_inc(S.av_hi, 1)

            def edge_out(g, t):
                if t == 0:
                    act.wait_ge(S.y_mm, g * 2 + 2)
                copy(Gh[:, t, :], PL[t][:, :]).then_inc(S.y_hi, 1)

            def setup():
                act.wait_ge(S.ld_alpha, 16)
                act.activation(small[:, 16:16 + NT], small[:, 0:NT], ACT.Sigmoid).then_inc(S.sig_done, 1)
                act.wait_ge(S.m_done, NT)
                copy(Mh[:, :, :, :].rearrange("p t c q -> p (t c q)"), Mf[:, :, :, :].rearrange("p t c q -> p (t c q)")).then_inc(S.m_hi, 1)
                for c in range(NT):
                    act.wait_ge(S.mt_mm, c + 1)
                    copy(M1h[:, c, :], (PV + PA)[c][:, :]).then_inc(S.mt_hi, 1)
                act.wait_ge(S.ln1_var, 1)
                act.activation(lnw[:, 4, :], lnw[:, 3, :], ACT.Sqrt).then_inc(S.ln1_std, 1)
                for j, m in ((1, M2h), (2, M3h)):
                    for c in range(NT):
                        act.wait_ge(S.mt_mm, NT * j + c + 1)
                        copy(m[:, c, :], (PV + PA)[c][:, :]).then_inc(S.mt_hi, 1)
                    if j == 1:
                        act.wait_ge(S.w_mm3, 1)
                        for i, m3 in enumerate((linh, valh, outh)):
                            copy(m3[:, :], PL[0][:, part(i)]).then_inc(S.w_hi, 1)
                        for g in range(1, NG):
                            act.wait_ge(S.ln1_var, g + 1)
                            act.activation(lnw[:, 4, :], lnw[:, 3, :], ACT.Sqrt).then_inc(S.ln1_std, 1)
                        x0_round(0, 0)
                        x0_round(0, 1)

            def setup_z():
                for k in range(STEPS + 1):
                    act.wait_ge(S.zt_mm, k + 1)
                    copy(Zh[:, k % POW, part(k // POW)], PZ[k % 2][:, 0:P]).then_inc(S.zk_hi, 1)

            def setup_bias():
                act.wait_ge(S.tb_mm, 1)
                copy(urow, PL[0][0:POW, :]).then_inc(S.u_sb, 1)
                act.wait_ge(S.tb_mm, 2)
                copy(crow[:, :], PL[1][0:POW, 0:BLOCKS * D]).then_inc(S.u_sb, 1)
                for t in range(NT):
                    act.wait_ge(S.tb_mm, 3 + t)
                    copy(bb[:, t, :], PL[t % 2][:, 0:BLOCKS * D]).then_inc(S.bb_sb, 1)
                act.wait_ge(S.bb_sb, NT)
                copy(tbh[:, :, :], bb[:, :, 2 * D:3 * D]).then_inc(S.tb_hi, 1)
                act.wait_ge(S.tb_step, 4)
                copy(tbh[:, :, :], TB[:, :, :]).then_inc(S.tb_hi, 1)

            def setup_logs():
                act.wait_ge(S.ed_log, 1)
                act.activation(picked[:, :], picked[:, :], ACT.Ln).then_inc(S.ed_pick, 1)

            def first_body():
                powers(0, 0)
                x0_round(0, 2)
                powers(0, 1)
                x0_round(0, 3)
                setup_z()
                blocks(0, 0)
                powers(0, 2)
                x0_round(1, 0)
                setup_bias()
                blocks(0, 1)
                powers(0, 3)
                x0_round(1, 1)
                blocks(0, 2)
                blocks(0, 3)
                setup_logs()
                for t in range(NT):
                    middle(0, t)
                second_norm(0)

            def body(g, last):
                l = g - 1
                powers(g, 0)
                x0_round(g, 2)
                powers(g, 1)
                x0_round(g, 3)
                gather(l, 0)
                gather(l, 1)
                blocks(g, 0)
                project(l, 0)
                powers(g, 2)
                if not last:
                    x0_round(g + 1, 0)
                gather(l, 2)
                gather(l, 3)
                blocks(g, 1)
                project(l, 1)
                powers(g, 3)
                if not last:
                    x0_round(g + 1, 1)
                exponent(l)
                blocks(g, 2)
                weigh(l, 0)
                blocks(g, 3)
                weigh(l, 1)
                middle(g, 0)
                middle(g, 1)
                for t in range(ET):
                    edge_out(l, t)
                middle(g, 2)
                middle(g, 3)
                second_norm(g)

            setup()
            first_body()
            with act.Fori(1, NG - 1) as g:
                body(g, False)
            body(NG - 1, True)
            l = NG - 1
            for p in range(2):
                gather(l, 2 * p)
                gather(l, 2 * p + 1)
                project(l, p)
            exponent(l)
            for p in range(2):
                weigh(l, p)
            for t in range(ET):
                edge_out(l, t)

        @block.vector
        def _(dve):
            def tt(o, x_, y_, op):
                return dve.tensor_tensor(o, x_, y_, op)

            def ts(o, x_, s1, s2, op0, op1=None):
                return dve.tensor_scalar(o, x_, s1, s2, op0, op1) if op1 is not None else dve.tensor_scalar(o, x_, s1, s2, op0)

            def stt(o, x_, s, y_, op0, op1):
                return dve.scalar_tensor_tensor(out=o, in0=x_, scalar=s, in1=y_, op0=op0, op1=op1)

            def low(o, v, hi):
                return tt(o, v, hi.bitcast(F32), ALU.subtract)

            def norm_small(g, count, step, var, std, mean_out, rstd_out):
                st = stats[:, :, :]
                me, ve, mo, vo = st[:, :, 1], st[:, :, 2], st[:, :, 4], st[:, :, 5]
                tt(lnw[:, 0, :], me, mo, ALU.add)
                tt(lnw[:, 1, :], me, mo, ALU.subtract)
                tt(lnw[:, 2, :], ve, vo, ALU.add).then_inc(step, 1)
                dve.wait_ge(step, count + 1)
                tt(lnw[:, 1, :], lnw[:, 1, :], lnw[:, 1, :], ALU.mult)
                ts(mean_out, lnw[:, 0, :], 0.5, None, ALU.mult).then_inc(step, 1)
                dve.wait_ge(step, count + 2)
                stt(lnw[:, 2, :], lnw[:, 1, :], D / 4.0, lnw[:, 2, :], ALU.mult, ALU.add).then_inc(step, 1)
                dve.wait_ge(step, count + 3)
                ts(lnw[:, 3, :], lnw[:, 2, :], 1.0 / D, LN_EPS, ALU.mult, ALU.add).then_inc(var, 1)
                dve.wait_ge(std, g + 1)
                dve.reciprocal(lnw[:, 5, :], lnw[:, 4, :]).then_inc(step, 1)
                dve.wait_ge(step, count + 4)
                tt(lnw[:, 0, :], lnw[:, 5, :], lnw[:, 5, :], ALU.mult).then_inc(step, 1)
                dve.wait_ge(step, count + 5)
                tt(lnw[:, 0, :], lnw[:, 0, :], lnw[:, 3, :], ALU.mult).then_inc(step, 1)
                dve.wait_ge(step, count + 6)
                ts(lnw[:, 0, :], lnw[:, 0, :], -0.5, 1.5, ALU.mult, ALU.add).then_inc(step, 1)
                dve.wait_ge(step, count + 7)
                tt(rstd_out, lnw[:, 5, :], lnw[:, 0, :], ALU.mult).then_inc(step, 1)
                dve.wait_ge(step, count + NORM_STEPS)

            NORM_STEPS = 8

            def first_norm(g):
                dve.wait_ge(x_loaded[g], 16)
                for b in range(GB):
                    for t in range(NT):
                        mm = dve.bn_stats(stats[:, b * NT + t, :], X[:, g, b, t, :])
                mm.then_inc(S.ln1_done, 1)
                dve.wait_ge(S.ln1_done, g + 1)
                n = GB * NT
                norm_small(g, g * NORM_STEPS, S.ln1_step, S.ln1_var, S.ln1_std,
                           mean1[:, g * n:(g + 1) * n], rstd1[:, g * n:(g + 1) * n])

            def x0_norm(g, b):
                n = g * GB + b
                if not (type(g) is int and n == 0):
                    dve.wait_ge(S.x0_lo, n)
                if b == 2 and not (type(g) is int and g == 0):
                    dve.wait_ge(S.h_lo, g * NT)
                for t in range(NT):
                    n = g * (GB * NT) + (b * NT + t)
                    mm = ts(xt[:, part(t)], xg(g, b, t), mean1[:, bass.ds(n, 1)], rstd1[:, bass.ds(n, 1)],
                            ALU.subtract, ALU.mult)
                mm.then_inc(S.x0_t, 1)

            def x0_low(g, b):
                dve.wait_ge(S.x0_hi, g * GB + (b + 1))
                stt(x0l[:, b % 2, :, :].rearrange("p t d -> p (t d)"), xt[:, :], 0.0,
                    x0h[:, b % 2, :, :].rearrange("p t d -> p (t d)").bitcast(F32), ALU.max, ALU.subtract).then_inc(S.x0_lo, 1)

            def powers(g, b):
                for j in range(POW):
                    dve.wait_ge(S.v_hi, g * (GB * POW) + (b * POW + j + 1))
                    low(Vl[:, b % 2, j, :], PV[(b * POW + j) % 2][:, :], Vh[:, b % 2, j, :]).then_inc(S.v_lo, 1)

            def blocks(g, b):
                for t in range(NT):
                    dve.wait_ge(S.z_hi, g * (GB * NT) + (b * NT + t + 1))
                    tt(xg(g, b, t), PZ[t % 2][:, 0:D], xg(g, b, t), ALU.add)
                    low(B2l[:, t, part(b)], PZ[t % 2][:, 2 * D:3 * D], B2h[:, t, part(b)]).then_inc(S.z_lo, 1)

            def middle_sum(g, t):
                dve.wait_ge(S.a1_mm, g * NT + (t + 1))
                tt(B1[:, t, :], PA[t % 2][:, :], B1[:, t, :], ALU.add).then_inc(S.a1_sum, 1)

            def middle_low(g, t):
                dve.wait_ge(S.c_hi, g * NT + (t + 1))
                low(Cl[:, t, :], B1[:, t, :], Ch[:, t, :]).then_inc(S.c_lo, 1)

            def first_layer(g, t):
                dve.wait_ge(S.a2_mm, g * NT + (t + 1))
                tt(xg(g, None, t), PA[t % 2][:, :].rearrange("p (b d) -> p b d", b=GB), xg(g, None, t), ALU.add).then_inc(S.a2_out, 1)
                dve.wait_ge(S.a2_out, g * NT + (t + 1))
                tt(xg(g, None, t), xg(g, None, t), TB[:, t:t + 1, :].to_broadcast([P, GB, D]), ALU.add).then_inc(S.tb_added, 1)
                dve.wait_ge(S.tb_added, g * NT + (t + 1))
                dve.memset(small[:, 31:32], 0.0)
                for b in range(GB):
                    mm = dve.bn_stats(stats[:, b * NT + t, :], xg(g, b, t))
                mm.then_inc(S.ln2_step, 1)

            def second_norm(g, x0_made):
                L2 = NT + NORM_STEPS
                dve.wait_ge(S.ln2_step, g * L2 + NT)
                norm_small(g, g * L2 + NT, S.ln2_step, S.ln2_var, S.ln2_std, small[:, 32:48], small[:, 48:64])
                for t in range(NT + 1):
                    if t < NT:
                        if t == 0:
                            dve.wait_ge(S.x0_lo, x0_made)
                        elif t == 1 and not (type(g) is int and g == 0):
                            dve.wait_ge(S.u_lr, g * 2)
                        elif t >= 2:
                            dve.wait_ge(S.h_lo, g * NT + (t - 1))
                        for b in range(GB):
                            n = b * NT + t
                            mm = ts(ht(t)[:, part(b)], xg(g, b, t), small[:, 32 + n:33 + n], small[:, 48 + n:49 + n],
                                    ALU.subtract, ALU.mult)
                        mm.then_inc(S.h_t, 1)
                    if t:
                        dve.wait_ge(S.h_hi, g * NT + t)
                        stt(Cl[:, t - 1, :], ht(t - 1), 0.0, Ch[:, t - 1, :].bitcast(F32),
                            ALU.max, ALU.subtract).then_inc(S.h_lo, 1)

            def gather(g, b):
                dve.wait_ge(S.g_hi, g * GB + (b + 1))
                low(Gl[:, b % 2, :], PL[b % 2][:, :], Gh[:, b % 2, :]).then_inc(S.g_lo, 1)

            def leaky(g, p):
                dve.wait_ge(S.u_t, g * 2 + (p + 1))
                tt(lr[:, :], PL[0][:, :], lrt[:, :], ALU.max).then_inc(S.u_lr, 1)

            SOFT = 6

            def scan(o, mask, v, first, op0, op1):
                return dve.tensor_tensor_scan(o, mask, v, first, op0, op1)

            def softmax(g):
                dve.wait_ge(S.e_mm, g * 2 + 2)
                tt(sm[0][:, :], PA[0][0:GH, 0:E], lgrow[:, :], ALU.add).then_inc(S.soft_step, 1)
                dve.wait_ge(S.soft_step, g * SOFT + 1)
                scan(sm[1][:, :], far[:, 0:E], sm[0][:, :], LEAST, ALU.add, ALU.max).then_inc(S.soft_step, 1)
                dve.wait_ge(S.soft_step, g * SOFT + 2)
                scan(sm[2][:, ::-1], far[:, 1:E + 1][:, ::-1], sm[1][:, ::-1], LEAST, ALU.add, ALU.max).then_inc(S.soft_step, 1)
                dve.wait_ge(S.soft_step, g * SOFT + 3)
                tt(sm[1][:, :], sm[0][:, :], sm[2][:, :], ALU.subtract).then_inc(S.e_shift, 1)

            def softmax_end(g):
                dve.wait_ge(S.e_exp, g + 1)
                scan(sm[0][:, :], same[:, 0:E], sm[2][:, :], 0.0, ALU.mult, ALU.add).then_inc(S.soft_step, 1)
                dve.wait_ge(S.soft_step, g * SOFT + 4)
                scan(sm[1][:, ::-1], same[:, 1:E + 1][:, ::-1], sm[0][:, ::-1], 0.0, ALU.mult, ALU.max).then_inc(S.soft_step, 1)
                dve.wait_ge(S.soft_step, g * SOFT + 5)
                dve.reciprocal(sm[0][:, :], sm[1][:, :]).then_inc(S.soft_step, 1)
                dve.wait_ge(S.soft_step, g * SOFT + 6)
                tt(sm[1][:, :], sm[2][:, :], sm[0][:, :], ALU.mult).then_inc(S.attn_ready, 1)

            def weigh(g, p):
                dve.wait_ge(S.bc_mm, g * 2 + (p + 1))
                v = vv[:, 2 * p:2 * p + 2, :].rearrange("p b e -> p (b e)")
                tt(v, PA[1 - p][:, :], v, ALU.mult).then_inc(S.av_f, 1)

            def weigh_low(g, p):
                dve.wait_ge(S.av_hi, g * 2 + (p + 1))
                low(avl[:, :, :].rearrange("p b e -> p (b e)"), vv[:, 2 * p:2 * p + 2, :].rearrange("p b e -> p (b e)"),
                    avh[:, :, :].rearrange("p b e -> p (b e)")).then_inc(S.av_lo, 1)

            def edge_out(g, t):
                dve.wait_ge(S.y_hi, g * ET + (t + 1))
                low(Gl[:, t, :], PL[t][:, :], Gh[:, t, :]).then_inc(S.y_lo, 1)

            def second_layer(g, t):
                dve.wait_ge(S.s_mm, g * NT + (t + 1))
                tt(xg(g, None, t), PL[t % 2][:, :].rearrange("p (b d) -> p b d", b=GB), xg(g, None, t), ALU.add).then_inc(S.s_out, 1)

            def setup():
                dve.wait_ge(S.iota_done, 8)
                ts(ident[:, :], idgrid, 0.0, None, ALU.is_equal).then_inc(S.id_done, 1)
                ts(stack[:, 0, D:2 * D], idgrid, 0.0, None, ALU.is_equal).then_inc(S.r_sb, 1)
                ts(identr[:, :], idgrid, 0.0, None, ALU.is_equal)
                dve.wait_ge(S.sig_done, 1)
                ts(scol_col[:, :], small[:, 16:16 + NT], DT / 2, None, ALU.mult)
                ts(ccol[:, :], small[:, 16:16 + NT], -DT / 2, 1.0 - DT, ALU.mult, ALU.add).then_inc(S.m_step, 1)
                dve.wait_ge(S.ld_cols, 32)
                ts(small[:, 20:21], small[:, 4:5], 0.0, 1.0, ALU.max, ALU.min).then_inc(S.z_step, 1)
                dve.wait_ge(S.r_mm, 1)
                dve.wait_ge(S.z_step, 1)
                ts(wTd, PZ[0][:, 0:P], small[:, 20:21], DT, ALU.mult, ALU.mult)
                dve.tensor_copy(wT, PZ[0][:, 0:P]).then_inc(S.r_sb, 1)
                dve.wait_ge(S.m_step, 1)
                dve.wait_ge(S.ld_adj, 16)
                for t in range(NT):
                    m = Mf[:, t, :, :].rearrange("p c q -> p (c q)")
                    ts(m, nodegrid, nodecol[:, t:t + 1], ccol[:, t:t + 1], ALU.is_equal, ALU.mult).then_inc(S.m_step, 1)
                for t in range(NT):
                    dve.wait_ge(S.m_step, 2 + t)
                    stt(Mf[:, t, :, :], A[:, t, :].rearrange("p (q c) -> p c q", c=NT), scol_col[:, t:t + 1],
                        Mf[:, t, :, :], ALU.mult, ALU.add).then_inc(S.m_done, 1)
                dve.wait_ge(S.r_mm, 2)
                dve.tensor_copy(R, PZ[0][:, P:2 * P]).then_inc(S.r_sb, 1)
                dve.wait_ge(S.st_mm, 1)
                dve.tensor_copy(stack[:, 1, :], PZ[1][:, 0:2 * D + 1]).then_inc(S.st_sb, 1)
                for c in range(NT):
                    dve.wait_ge(S.mt_hi, c + 1)
                    low(M1l[:, c, :], (PV + PA)[c][:, :], M1h[:, c, :]).then_inc(S.mt_lo, 1)
                dve.wait_ge(S.m_hi, 1)
                low(Ml[:, :, :, :].rearrange("p t c q -> p (t c q)"), Mf[:, :, :, :].rearrange("p t c q -> p (t c q)"),
                    Mh[:, :, :, :].rearrange("p t c q -> p (t c q)")).then_inc(S.m_lo, 1)
                for i in range(2, STEPS + 1):
                    dve.wait_ge(S.st_mm, i)
                    dve.tensor_copy(stack[:, i, :], PZ[1][:, 0:2 * D + 1]).then_inc(S.st_sb, 1)
                first_norm(0)
                for c in range(NT):
                    dve.wait_ge(S.mt_hi, NT + c + 1)
                    low(M2l[:, c, :], (PV + PA)[c][:, :], M2h[:, c, :]).then_inc(S.mt_lo, 1)
                dve.wait_ge(S.w_hi, 3)
                for i, (lo_, hi_) in enumerate(((linl, linh), (vall, valh), (outl, outh))):
                    mm = low(lo_[:, :], PL[0][:, part(i)], hi_[:, :])
                mm.then_inc(S.w_lo, 1)
                for g in range(1, NG):
                    first_norm(g)
                x0_norm(0, 0)
                x0_low(0, 0)
                x0_norm(0, 1)
                x0_low(0, 1)
                for c in range(NT):
                    dve.wait_ge(S.mt_hi, 2 * NT + c + 1)
                    low(M3l[:, c, :], (PV + PA)[c][:, :], M3h[:, c, :]).then_inc(S.mt_lo, 1)

            def setup_zt():
                dve.wait_ge(S.st_sb, STEPS)
                n = 1
                for k in range(STEPS + 1):
                    last = ts(ztk(k), stack[:, STEPS - k, 0:D], float(comb(STEPS, k)), None, ALU.mult)
                    if k == STEPS:
                        last.then_inc(S.z_step, 1)
                n += 1
                for i in range(STEPS):
                    dve.wait_ge(S.z_step, n)
                    for k in range(STEPS - i):
                        last = stt(ztk(k), stack[:, i, D:2 * D], DT * comb(i + k, k), ztk(k), ALU.mult, ALU.add)
                    last.then_inc(S.z_step if i < STEPS - 1 else S.zt_done, 1)
                    n += 1
                for k in range(STEPS + 1):
                    mm = ts(ccols(k // POW)[:, k % POW:k % POW + 1], stack[:, STEPS - k, 2 * D:2 * D + 1],
                            float(comb(STEPS, k)), None, ALU.mult)
                mm.then_inc(S.tb_step, 1)

            def setup_z():
                for k in range(STEPS + 1):
                    dve.wait_ge(S.zk_hi, k + 1)
                    low(Zl[:, k % POW, part(k // POW)], PZ[k % 2][:, 0:P], Zh[:, k % POW, part(k // POW)]).then_inc(S.zk_lo, 1)

            def setup_ones():
                dve.wait_ge(S.tb_step, 1)
                dve.memset(onesr[:, :].bitcast(F32), 1.0)
                for j in range(POW):
                    mm = dve.memset(rowsel[:, j, :].bitcast(F32), 0.0)
                mm.then_inc(S.tb_step, 1)
                for j in range(POW):
                    if j == 0:
                        dve.wait_ge(S.tb_step, 2)
                    mm = dve.memset(rowsel[:, j, j:j + 1].bitcast(F32), 1.0 if j else 1.0 / P)
                mm.then_inc(S.tb_step, 1)

            def setup_bias():
                dve.wait_ge(S.tb_hi, 1)
                low(tbl[:, :, :], bb[:, :, 2 * D:3 * D], tbh[:, :, :]).then_inc(S.tb_lo, 1)
                dve.wait_ge(S.tb_mm, 3 + NT)
                tt(TB[:, :, :], PL[0][:, :].rearrange("p (t d) -> p t d", t=NT), bb[:, :, D:2 * D], ALU.add).then_inc(S.tb_step, 1)
                dve.wait_ge(S.tb_hi, 2)
                low(tbl[:, :, :], TB[:, :, :], tbh[:, :, :]).then_inc(S.tb_lo, 1)
                dve.wait_ge(S.tb_mm, 4 + NT)
                tt(TB[:, :, :], PL[1][:, :].rearrange("p (t d) -> p t d", t=NT), bb[:, :, 0:D], ALU.add).then_inc(S.tb_out, 1)

            def setup_edges_rank():
                dve.wait_ge(S.ld_idx, 64)
                dve.tensor_copy(rowf[:, :], irow[:, 0, :])
                dve.tensor_copy(colf, icol[:, :, :].rearrange("p s t -> p t s")).then_inc(S.ed_step, 1)
                dve.wait_ge(S.ed_step, 1)
                stt(keyrow[:, :], rowf[:, :], float(E), egrid, ALU.mult, ALU.add)
                stt(keycol, colf[:, :, 0], float(E), small[:, 8:8 + ET], ALU.mult, ALU.add).then_inc(S.ed_step, 1)
                dve.wait_ge(S.ed_step, 2)
                for t in range(ET):
                    mm = ts(perm[:, t, :], keyrow[:, :], keycol[:, t:t + 1], None, ALU.is_lt)
                mm.then_inc(S.ed_step, 1)
                dve.wait_ge(S.ed_step, 3)
                for t in range(ET):
                    mm = dve.tensor_reduce(rank[:, t:t + 1], perm[:, t, :], AX_X, ALU.add)
                mm.then_inc(S.ed_step, 1)
                dve.wait_ge(S.ed_step, 4)
                for t in range(ET):
                    ts(perm[:, t, :], egrid, rank[:, t:t + 1], None, ALU.is_equal)
                for s in range(2):
                    for t in range(ET):
                        mm = ts(ecolb[:, s, t, :], ident[:, :], 0.0, colf[:, t, s:s + 1], ALU.mult, ALU.add)
                mm.then_inc(S.ed_step, 1)

            def setup_edges():
                dve.wait_ge(S.ed_mm, 1)
                dve.tensor_copy(nrow[:, :, :].rearrange("p s e -> p (s e)"), PL[0][:, :])
                dve.tensor_copy(ncol, PL[1][:, 0:2 * ET].rearrange("p (t s) -> p t s", s=2)).then_inc(S.ed_sb, 1)
                dve.wait_ge(S.ed_sb, 1)
                stt(flat[:, :], ncol[:, :, 0], float(N), ncol[:, :, 1], ALU.mult, ALU.add).then_inc(S.ed_flat, 1)
                for t in range(NT):
                    mm = ts(gat[:, t, E:2 * E], nrow[:, 1, :], nodecol[:, t:t + 1], None, ALU.is_equal)
                mm.then_inc(S.ed_sb, 1)
                for t in range(ET):
                    ts(scat[:, t, :], nodegrid, ncol[:, t, 0:1], None, ALU.is_equal)
                dve.wait_ge(S.ed_sb, 2)
                for t in range(NT):
                    stt(gat[:, t, 0:E], nrow[:, 0, :], nodecol[:, t:t + 1], gat[:, t, E:2 * E].bitcast(F32), ALU.is_equal, ALU.add)
                tt(same[:, 1:E], nrow[0:GH, 0, 1:E], nrow[0:GH, 0, 0:E - 1], ALU.is_equal)
                dve.memset(same[:, 0:1], 0.0)
                dve.memset(same[:, E:E + 1], 0.0).then_inc(S.ed_sb, 1)
                dve.wait_ge(S.ed_sb, 3)
                ts(far[:, :], same[:, :], -FAR, FAR, ALU.mult, ALU.add)
                ts(hm[:, 0:HEADS], small[:, 12:12 + HEADS], 0.0, None, ALU.is_ge)
                ts(hm[:, HEADS:2 * HEADS], small[:, 12:12 + HEADS], float(DH - 1), small[:, 5:6], ALU.is_le, ALU.mult).then_inc(S.ed_sb, 1)
                dve.wait_ge(S.ed_sb, 4)
                for b in range(GB):
                    tt(apad[:, b, b * HEADS:(b + 1) * HEADS], hm[:, 0:HEADS], hm[:, HEADS:2 * HEADS], ALU.mult)
                ts(sel[:, :, :], sel[:, :, :], 0.0, None, ALU.is_equal).then_inc(S.ed_done, 1)

            def setup_logs():
                dve.wait_ge(S.ed_picked, 16 * ET)
                ts(picked[:, :], picked[:, :], LOG_EPS, None, ALU.add).then_inc(S.ed_log, 1)
                dve.wait_ge(S.ed_pick, 1)
                for t in range(ET):
                    mm = ts(logb[:, t, :], ident[:, 0:GH], 0.0, picked[:, t:t + 1], ALU.mult, ALU.add)
                mm.then_inc(S.ed_log, 1)
                dve.wait_ge(S.lg_mm, 1)
                dve.tensor_copy(lgrow[:, :], PL[0][0:GH, 0:E]).then_inc(S.ed_done, 1)

            def first_body():
                powers(0, 0)
                x0_norm(0, 2)
                x0_low(0, 2)
                powers(0, 1)
                x0_norm(0, 3)
                x0_low(0, 3)
                setup_z()
                blocks(0, 0)
                powers(0, 2)
                x0_norm(1, 0)
                x0_low(1, 0)
                setup_bias()
                setup_edges_rank()
                blocks(0, 1)
                powers(0, 3)
                x0_norm(1, 1)
                x0_low(1, 1)
                setup_edges()
                blocks(0, 2)
                blocks(0, 3)
                setup_logs()
                middle_sum(0, 0)
                for t in range(NT):
                    if t + 1 < NT:
                        middle_sum(0, t + 1)
                    middle_low(0, t)
                for t in range(NT):
                    first_layer(0, t)
                second_norm(0, GB + 2)

            def body(g, last):
                l = g - 1
                powers(g, 0)
                x0_norm(g, 2)
                x0_low(g, 2)
                powers(g, 1)
                x0_norm(g, 3)
                x0_low(g, 3)
                gather(l, 0)
                gather(l, 1)
                blocks(g, 0)
                leaky(l, 0)
                powers(g, 2)
                if not last:
                    x0_norm(g + 1, 0)
                    x0_low(g + 1, 0)
                gather(l, 2)
                gather(l, 3)
                blocks(g, 1)
                leaky(l, 1)
                powers(g, 3)
                if not last:
                    x0_norm(g + 1, 1)
                    x0_low(g + 1, 1)
                softmax(l)
                softmax_end(l)
                blocks(g, 2)
                weigh(l, 0)
                weigh_low(l, 0)
                blocks(g, 3)
                weigh(l, 1)
                weigh_low(l, 1)
                middle_sum(g, 0)
                middle_sum(g, 1)
                middle_low(g, 0)
                middle_low(g, 1)
                for t in range(ET):
                    edge_out(l, t)
                middle_sum(g, 2)
                middle_sum(g, 3)
                middle_low(g, 2)
                middle_low(g, 3)
                second_layer(l, 0)
                second_layer(l, 1)
                first_layer(g, 0)
                second_layer(l, 2)
                second_layer(l, 3)
                for t in range(1, NT):
                    first_layer(g, t)
                second_norm(g, NG * GB if last else g * GB + (GB + 2))

            setup()
            setup_zt()
            setup_ones()
            first_body()
            with dve.Fori(1, NG - 1) as g:
                body(g, False)
            body(NG - 1, True)
            l = NG - 1
            for p in range(2):
                gather(l, 2 * p)
                gather(l, 2 * p + 1)
                leaky(l, p)
            softmax(l)
            softmax_end(l)
            for p in range(2):
                weigh(l, p)
                weigh_low(l, p)
            for t in range(ET):
                edge_out(l, t)
            for t in range(NT):
                second_layer(l, t)


def kernel(x, adj, L0_gnn_alpha_train, L0_gnn_w, L0_gnn_d, L0_gnn_fc_in_w, L0_gnn_fc_in_b,
           L1_gnn_W_lin, L1_gnn_W_val, L1_gnn_a, L1_gnn_W_out, L1_gnn_src, L1_gnn_dst):
    import numpy as np
    import concourse.bacc as bacc
    from concourse.bass_utils import run_bass_kernel_spmd

    given = {"x": x, "adj": adj, "alpha": L0_gnn_alpha_train, "w": L0_gnn_w, "d": L0_gnn_d, "fc_w": L0_gnn_fc_in_w,
             "fc_b": L0_gnn_fc_in_b, "W_lin": L1_gnn_W_lin, "W_val": L1_gnn_W_val, "a": L1_gnn_a,
             "W_out": L1_gnn_W_out, "src": L1_gnn_src, "dst": L1_gnn_dst}
    nc = bacc.Bacc("TRN2", target_bir_lowering=False, num_devices=1)
    arrays, args = {}, []
    for name, value in given.items():
        v = np.ascontiguousarray(value)
        arrays[f"in_{name}"] = v
        args.append(nc.dram_tensor(f"in_{name}", v.shape, mybir.dt.from_np(v.dtype), kind="ExternalInput").ap())
    out = nc.dram_tensor("out", arrays["in_x"].shape, F32, kind="ExternalOutput").ap()
    gnn_two_layers(nc, *args, out)
    return run_bass_kernel_spmd(nc, [arrays], core_ids=[0]).results[0]["out"]
```

```python
from contextlib import ExitStack
from math import comb

import concourse.bass as bass
from concourse import mybir

ALU = mybir.AluOpType
ACT = mybir.ActivationFunctionType
AX_X = mybir.AxisListType.X
F32 = mybir.dt.float32
F32R = mybir.dt.float32r
BF16 = mybir.dt.bfloat16
I32 = mybir.dt.int32
U32 = mybir.dt.uint32

P = 128
STEPS = 8
DT = 1.0 / STEPS
POW = 3
LN_EPS = 1e-5
LOG_EPS = 1e-8
SLOPE = 0.2
FAR = -1e30
LEAST = -3e38


def gnn_two_layers(nc, x, adj, alpha, w, d, fc_w, fc_b, W_lin, W_val, a, W_out, src, dst, out):
    B, N, D = x.shape
    E = src.shape[0]
    HEADS, DH = a.shape
    NT = N // P
    ET = E // P
    GB = 4
    NG = B // GB
    W = GB * D
    GH = GB * HEADS
    BLOCKS = (STEPS + POW) // POW
    assert D == P and N == NT * P and E == 2 * P and NT == 4 and BLOCKS == 3 and W == 512

    with ExitStack() as ctx:
        def sb(name, shape, dt=F32, where=ctx):
            return where.enter_context(nc.sbuf_tensor(name, shape, dt))

        def sem(name):
            return ctx.enter_context(nc.semaphore(name))

        X = sb("X", [P, NG, GB, NT, D])
        MT = [sb(f"MT{j}_{k}", [P, NT, N], F32R) for j in (1, 2, 3) for k in ("hi", "lo")]
        M1h, M1l, M2h, M2l, M3h, M3l = MT
        Zh = sb("Zh", [P, POW, BLOCKS * D], F32R)
        Zl = sb("Zl", [P, POW, BLOCKS * D], F32R)
        TB = sb("TB", [P, NT, D])
        gat = sb("gat", [P, NT, 2 * E], F32R)
        scat = sb("scat", [P, ET, N], F32R)
        linh, linl, valh, vall, outh, outl = [
            sb(n, [P, D], F32R) for n in ("linh", "linl", "valh", "vall", "outh", "outl")]
        ident = sb("ident", [P, P])
        identr = sb("identr", [P, P], F32R)
        apad = sb("apad", [P, GB, GH])
        lgrow = sb("lgrow", [GH, E])
        far = sb("far", [GH, E + 1], BF16)
        same = sb("same", [GH, E + 1], BF16)
        mean1 = sb("mean1", [P, NG * GB * NT])
        rstd1 = sb("rstd1", [P, NG * GB * NT])
        stats = sb("stats", [P, GB * NT, 6])
        lnw = sb("lnw", [P, 6, GB * NT])
        nodecol = sb("nodecol", [P, NT])
        scol_col = sb("scol_col", [P, NT])
        ccol = sb("ccol", [P, NT])

        xt = sb("xt", [P, NT * D])
        x0h = sb("x0h", [P, 2, NT, D], F32R)
        x0l = sb("x0l", [P, 2, NT, D], F32R)
        Vh = sb("Vh", [P, 2, POW, N], F32R)
        Vl = sb("Vl", [P, 2, POW, N], F32R)
        vv = sb("vv", [P, GB, E])
        selr = sb("selr", [GH, GB, P], F32R)
        atth = sb("atth", [GH, E], F32R)
        attl = sb("attl", [GH, E], F32R)
        sm = [sb(f"sm{i}", [GH, E]) for i in range(3)]
        with ExitStack() as before:
            lr = sb("lr", [P, 2 * E], F32, before)
            lrt = sb("lrt", [P, 2 * E], F32, before)
        avh = sb("avh", [P, 2, E], F32R)
        avl = sb("avl", [P, 2, E], F32R)

        with ExitStack() as early:
            A = sb("A", [P, NT, N], F32, early)
            Mf = sb("Mf", [P, NT, NT, P], F32, early)
            Mh = sb("Mh", [P, NT, NT, P], F32R, early)
            Ml = sb("Ml", [P, NT, NT, P], F32R, early)
            stack = sb("stack", [P, STEPS + 1, 2 * D + 1], F32, early)
            wraw = sb("wraw", [P, 4, D], F32, early)
            feat = sb("feat", [P, 4, D], F32, early)
            irow = sb("irow", [P, 2, E], I32, early)
        sel = vv[0:GH, 0:2, :].rearrange("p b (c e) -> p (b c) e", e=P)
        with ExitStack() as middle_scope:
            sb("skip", [P, 3 * NT * W], F32, middle_scope)
            bb = sb("bb", [P, NT, BLOCKS * D], F32, middle_scope)
            tbh = sb("tbh", [P, NT, D], F32R, middle_scope)
            tbl = sb("tbl", [P, NT, D], F32R, middle_scope)
            crow = sb("crow", [POW, BLOCKS * D], F32, middle_scope)
            onesr = sb("onesr", [P, N], F32R, middle_scope)
            rowsel = sb("rowsel", [P, POW, P], F32R, middle_scope)
            ecolb = sb("ecolb", [P, 2, ET, P], F32, middle_scope)
            perm = sb("perm", [P, ET, E], F32, middle_scope)
            rowf = sb("rowf", [P, E], F32, middle_scope)
            keyrow = sb("keyrow", [P, E], F32, middle_scope)
            nrow = sb("nrow", [P, 2, E], F32, middle_scope)
        B2h = sb("B2h", [P, NT, W], F32R)
        B2l = sb("B2l", [P, NT, W], F32R)
        B1 = sb("B1", [P, NT, W])
        Ch = sb("Ch", [P, NT, W], F32R)
        Cl = sb("Cl", [P, NT, W], F32R)
        Gh = sb("Gh", [P, 2, 2 * E], F32R)
        Gl = sb("Gl", [P, 2, 2 * E], F32R)
        wT, wTd, R = feat[:, 0, :], feat[:, 1, :], feat[:, 2, :]
        zt = vv[:, :, :].rearrange("p b e -> p (b e)")
        urow = zt[0:POW, 0:N]
        nodegrid = lrt[:, :]
        egrid = lr[:, 0:E]
        idgrid = lr[:, E:E + P]
        small = lr[:, 3 * P:3 * P + 32]
        tiny = lr[:, 3 * P + 32:3 * P + 64]
        norm2 = sb("norm2", [P, 2, GB * NT])
        carrier = sb("carrier", [P, 1])
        colf = tiny[:, 0:2 * ET].rearrange("p (t s) -> p t s", s=2)
        keycol, rank = tiny[:, 4:4 + ET], tiny[:, 6:6 + ET]
        ncol = tiny[:, 8:8 + 2 * ET].rearrange("p (t s) -> p t s", s=2)
        hm = tiny[:, 16:16 + 2 * HEADS]
        logb = lr[:, 3 * P + 64:3 * P + 64 + ET * GH].rearrange("p (t b) -> p t b", t=ET)
        icol = lr[:, 3 * P + 96:3 * P + 96 + 2 * ET].bitcast(I32).rearrange("p (s t) -> p s t", t=ET)
        flat = lr[:, 3 * P + 104:3 * P + 104 + ET].bitcast(U32)
        picked = lr[:, 3 * P + 108:3 * P + 108 + ET]

        def ztk(k):
            return zt[:, k * D:(k + 1) * D] if k < STEPS else feat[:, 3, :]

        def ccols(i):
            return small[:, 22 + POW * i:22 + POW * (i + 1)]

        bank = [ctx.enter_context(nc.psum_tensor(f"bank{i}", [P, 512], F32)) for i in range(8)]
        PV, PZ, PA, PL = bank[0:2], bank[2:4], bank[4:6], bank[6:8]
        VB = PV + PA[1:2]

        names = """ld_adj ld_alpha ld_w ld_stack ld_cols ld_idx ld_l1 ld_a vv_free iota_done
            sig_done m_step m_done m_hi m_lo mt_mm mt_hi mt_lo z_step r_mm r_sb st_mm st_sb
            zt_done zt_mm zk_hi zk_lo ln1_step ln1_var ln1_std ln1_done w_mm3 w_hi w_lo id_done
            tb_step tb_mm u_sb bb_sb tb_hi tb_lo tb_out tb_added
            ed_step ed_mm ed_sb ed_flat ed_pick ed_picked ed_log ed_done lg_mm
            x0_t x0_hi x0_lo v_mm v_hi v_lo z_mm z_hi z_lo a1_mm a1_sum c_hi c_lo a2_mm a2_out
            ln2_step ln2_var ln2_std h_t h_hi h_lo g_mm g_hi g_lo u_mm u_t u_lr q_mm q_cp e_mm
            soft_step e_shift e_exp att_full att_hi attn_ready bc_mm av_f av_hi av_lo y_mm y_hi y_lo s_mm s_out stored
            """.split()
        S = type("Semaphores", (), {n: sem(n) for n in names})
        x_loaded = [sem(f"x_loaded{g}") for g in range(NG)]

        x_d = x.rearrange("(g b) (p t) d -> g p b t d", b=GB, t=NT)
        out_d = out.rearrange("(g b) (p t) d -> g p b t d", b=GB, t=NT)

        def xg(g, b=None, t=None):
            v = X[:, bass.ds(g, 1), :, :, :]
            if t is None:
                return v[:, :, b, :, :].rearrange("p o t d -> p (o t) d")
            if b is None:
                return v[:, :, :, t, :].rearrange("p o b d -> p (o b) d")
            return v[:, :, b, t, :].rearrange("p o d -> p (o d)")

        def ht(t):
            return (lrt if t % 2 else xt)[:, :]

        def gather_bank(b, last):
            return (PL + PV if last else PL + PL)[b][:, :]

        def gathered(p, last):
            if last:
                return B2h[:, 2 * p:2 * p + 2, :], B2l[:, 2 * p:2 * p + 2, :]
            return Gh[:, :, :], Gl[:, :, :]

        def weighted(p, last):
            return (Ch[:, 0, :], Cl[:, 0, :]) if last and p else (
                avh[:, :, :].rearrange("p b e -> p (b e)"), avl[:, :, :].rearrange("p b e -> p (b e)"))

        def leaked(p, last):
            return B1[:, 0, :] if last and p else lr[:, :]

        def sloped(p, last):
            return B1[:, 1, :] if last and p else lrt[:, :]

        def project_banks(p, last):
            return PV if last and p else PL

        def part(t):
            return slice(t * P, (t + 1) * P)

        block = ctx.enter_context(nc.Block())

        @block.sync
        def _(sp):
            sp.dma_start(A[:, :, :], adj.rearrange("(p t) m -> p t m", t=NT)).then_inc(S.ld_adj, 16)
            for g in range(NG):
                if g == 1:
                    sp.wait_ge(S.ld_stack, 32)
                sp.dma_start(X[:, g, :, :, :], x_d[g]).then_inc(x_loaded[g], 16)
            for i, e in enumerate((src, dst)):
                sp.dma_start(irow[:, i, :], e.partition_broadcast(P)).then_inc(S.ld_idx, 16)
                sp.dma_start(icol[:, i, :], e.rearrange("(p t) -> p t", t=ET)).then_inc(S.ld_idx, 16)
            with sp.Fori(0, NG - 1) as g:
                sp.wait_ge(S.s_out, g * NT + NT)
                sp.dma_start(out_d[bass.ds(g, 1)].rearrange("o p b t d -> (o p) b t d"),
                             X[:, bass.ds(g, 1), :, :, :].rearrange("p o b t d -> p (o b) t d")).then_inc(S.stored, 16)
            for t in range(NT):
                sp.wait_ge(S.s_out, (NG - 1) * NT + t + 1)
                sp.dma_start(out_d[NG - 1][:, :, t, :], X[:, NG - 1, :, t, :]).then_inc(S.stored, 16)
            sp.wait_ge(S.stored, 16 * (NG - 1 + NT))

        @block.gpsimd
        def _(pool):
            exact = dict(allow_small_or_imprecise_dtypes=True)
            pool.iota(idgrid, [[1, P]], base=0, channel_multiplier=-1, **exact).then_inc(S.iota_done, 1)
            pool.iota(nodecol[:, :], [[1, NT]], base=0, channel_multiplier=NT, **exact).then_inc(S.iota_done, 1)
            pool.iota(nodegrid, [[1, NT], [NT, P]], base=0, channel_multiplier=0, **exact).then_inc(S.iota_done, 1)
            pool.iota(egrid, [[1, E]], base=0, channel_multiplier=0, **exact).then_inc(S.iota_done, 1)
            pool.iota(small[:, 8:8 + ET], [[1, ET]], base=0, channel_multiplier=ET, **exact).then_inc(S.iota_done, 1)
            pool.iota(small[:, 12:12 + HEADS], [[-DH, HEADS]], base=0, channel_multiplier=1, **exact).then_inc(S.iota_done, 1)
            pool.iota(sel.rearrange("p b (h e) -> p b h e", h=HEADS), [[HEADS, GB], [1, HEADS], [0, DH]],
                      base=0, channel_multiplier=-1, **exact).then_inc(S.iota_done, 1)
            pool.memset(apad[:, :, :], 0.0).then_inc(S.iota_done, 1)
            pool.wait_ge(S.ed_flat, 1)
            for t in range(ET):
                pool.indirect_dma_start(
                    picked[:, t:t + 1], None, adj.rearrange("n (m o) -> (n m) o", o=1),
                    bass.IndirectOffsetOnAxis(ap=flat[:, t:t + 1], axis=0)).then_inc(S.ed_picked, 16)

            def add_bias(g):
                for t in range(NT):
                    if t == 0:
                        pool.wait_ge(S.z_lo, g * (GB * NT) + GB * NT)
                    pool.tensor_tensor(xg(g, None, t), xg(g, None, t), TB[:, t:t + 1, :].to_broadcast([P, GB, D]),
                                       ALU.add).then_inc(S.tb_added, 1)

            pool.wait_ge(S.tb_out, 1)
            with pool.Fori(0, NG) as g:
                add_bias(g)

        @block.tensor
        def _(pe):
            def product(o, ah, al, bh, bl, start, stop):
                pe.matmul(o, ah, bh, start=start, stop=False)
                pe.matmul(o, ah, bl, start=False, stop=False)
                return pe.matmul(o, al, bh, start=False, stop=stop)

            def setup_features():
                pe.wait_ge(S.id_done, 1)
                pe.wait_ge(S.ld_w, 16)
                pe.transpose(PZ[0][:, 0:P], wraw[:, 0, :], ident[:, :]).then_inc(S.r_mm, 1)
                pe.wait_ge(S.r_sb, 2)
                pe.matmul(PZ[0][:, P:2 * P], wTd, wT, start=True, stop=True).then_inc(S.r_mm, 1)

            def setup_power(i):
                if i == 1:
                    pe.wait_ge(S.ld_stack, 32)
                    pe.wait_ge(S.r_sb, 3)
                else:
                    pe.wait_ge(S.st_sb, i - 1)
                pe.matmul(PZ[1][:, 0:2 * D + 1], R, stack[:, i - 1, :], start=True, stop=True).then_inc(S.st_mm, 1)

            def setup_transposes():
                for c in range(NT):
                    if c == 0:
                        pe.wait_ge(S.m_done, NT)
                    for t in range(NT):
                        mm = pe.transpose((PV + PA)[c][:, part(t)], Mf[:, t, c, :], ident[:, :])
                    mm.then_inc(S.mt_mm, 1)

            def setup_square(j, inh, inl):
                pe.wait_ge(S.m_lo, 1)
                pe.wait_ge(S.mt_lo, NT * (j - 1))
                for c in range(NT):
                    if j == 2:
                        setup_power(2 * c + 2)
                        if c < NT - 1:
                            setup_power(2 * c + 3)
                    elif c == 1:
                        pe.wait_ge(S.v_lo, 2 * POW)
                    for t in range(NT):
                        mm = product((PA + PL)[c][:, :], Mh[:, t, c, :], Ml[:, t, c, :], inh[:, t, :], inl[:, t, :],
                                     t == 0, t == NT - 1)
                    mm.then_inc(S.mt_mm, 1)

            def setup_z():
                for k in range(STEPS + 1):
                    if k == 0:
                        pe.wait_ge(S.zt_done, 1)
                        pe.wait_ge(S.w_lo, 1)
                    if k >= 2:
                        pe.wait_ge(S.zk_lo, k - 1)
                    pe.transpose(PZ[k % 2][:, 0:P], ztk(k), ident[:, :]).then_inc(S.zt_mm, 1)

            def setup_weights():
                pe.wait_ge(S.ld_l1, 48)
                for i in range(3):
                    mm = pe.transpose(PZ[0][:, part(i)], wraw[:, 1 + i, :], ident[:, :])
                mm.then_inc(S.w_mm3, 1)

            def setup_bias_rows():
                pe.wait_ge(S.tb_step, 3)
                pe.wait_ge(S.w_lo, 1)
                pe.wait_ge(S.mt_lo, 2 * NT)
                n = 0
                for j, parts in enumerate(([onesr[:, :]], [M1h, M1l], [M2h, M2l])):
                    for m in parts:
                        for t in range(NT if j else 1):
                            rhs = m[:, t, :] if j else onesr[:, :]
                            mm = pe.matmul(PL[0][:, :], rowsel[:, j, :], rhs, start=(n == 0), stop=(n == 4 * NT))
                            n += 1
                mm.then_inc(S.tb_mm, 1)
                pe.wait_ge(S.mt_lo, 3 * NT)
                for i in range(BLOCKS):
                    mm = pe.transpose(PL[1][0:POW, part(i)], ccols(i), ident[:, :])
                mm.then_inc(S.tb_mm, 1)

            def setup_bias_blocks():
                pe.wait_ge(S.u_sb, 2)
                for t in range(NT):
                    if t >= 2:
                        pe.wait_ge(S.bb_sb, t - 1)
                    pe.matmul(PL[t % 2][:, 0:BLOCKS * D], urow[:, part(t)], crow[:, :], start=True, stop=True).then_inc(S.tb_mm, 1)

            def setup_bias_cube(r):
                if r == 0:
                    pe.wait_ge(S.bb_sb, NT)
                pe.wait_ge(S.tb_lo, r + 1)
                for t in range(NT):
                    for m in range(NT):
                        mm = product(PL[r][:, part(t)], M3h[:, m, part(t)], M3l[:, m, part(t)],
                                     tbh[:, m, :], tbl[:, m, :], m == 0, m == NT - 1)
                mm.then_inc(S.tb_mm, 1)

            def setup_edges():
                pe.wait_ge(S.ed_step, 5)
                pe.wait_ge(S.tb_out, 1)
                for s in range(2):
                    for t in range(ET):
                        mm = pe.matmul(PL[0][:, s * E:(s + 1) * E], ecolb[:, s, t, :], perm[:, t, :], start=(t == 0), stop=(t == ET - 1))
                for r in range(ET):
                    for t in range(ET):
                        mm = pe.matmul(PL[1][:, 2 * r:2 * r + 2], perm[:, t, part(r)], colf[:, t, :], start=(t == 0), stop=(t == ET - 1))
                mm.then_inc(S.ed_mm, 1)

            def setup_logs():
                pe.wait_ge(S.ed_log, 2)
                for t in range(ET):
                    mm = pe.matmul(PL[0][0:GH, part(t)], logb[:, t, :], ident[:, :], start=True, stop=True)
                mm.then_inc(S.lg_mm, 1)

            def powers(g, b):
                n = g * GB + b
                pe.wait_ge(S.x0_lo, n + 1)
                xs = b % 2
                for j in range(POW):
                    i = g * (GB * POW) + (b * POW + j)
                    o = VB[j]
                    if not (type(g) is int and g == 0 and b == 0):
                        pe.wait_ge(S.v_lo, i - 2)
                        if b == 0 and j == 2:
                            pe.wait_ge(S.a2_out, g * NT)
                    elif j == 2:
                        pe.wait_ge(S.mt_lo, 2 * NT)
                    for t in range(NT):
                        if j == 0:
                            pe.matmul(o[:, part(t)], x0h[:, xs, t, :], identr[:, :], start=True, stop=False)
                            mm = pe.matmul(o[:, part(t)], x0l[:, xs, t, :], identr[:, :], start=False, stop=True)
                        else:
                            mh, ml = (M1h, M1l) if j == 1 else (M2h, M2l)
                            mm = product(o[:, :], x0h[:, xs, t, :], x0l[:, xs, t, :], mh[:, t, :], ml[:, t, :],
                                         t == 0, t == NT - 1)
                    mm.then_inc(S.v_mm, 1)

            def blocks(g, b):
                for t in range(NT):
                    i = g * (GB * NT) + (b * NT + t)
                    if t == 0:
                        pe.wait_ge(S.v_lo, g * (GB * POW) + (b * POW + POW))
                    if type(g) is int and g == 0 and b == 0 and t < 2:
                        pe.wait_ge(S.zk_lo, STEPS + 1)
                    else:
                        pe.wait_ge(S.z_lo, i - 1)
                    o = PZ[t % 2][:, 0:BLOCKS * D]
                    for j in range(POW):
                        mm = product(o, Vh[:, b % 2, j, part(t)], Vl[:, b % 2, j, part(t)], Zh[:, j, :], Zl[:, j, :],
                                     j == 0, j == POW - 1)
                    mm.then_inc(S.z_mm, 1)

            def cube(g, t, stage):
                if stage == 1:
                    if t == 0:
                        pe.wait_ge(S.z_lo, g * (GB * NT) + GB * NT)
                        if not (type(g) is int and g == 0):
                            pe.wait_ge(S.soft_step, (g - 1) * 7 + 1)
                    if t >= 2:
                        pe.wait_ge(S.a1_sum, g * NT + (t - 1))
                    bh, bl = B2h, B2l
                else:
                    if t == 0:
                        pe.wait_ge(S.c_lo, g * NT + NT)
                    if t >= 2:
                        pe.wait_ge(S.a2_out, g * NT + (t - 1))
                    bh, bl = Ch, Cl
                for m in range(NT):
                    mm = product(PA[t % 2][:, :], M3h[:, m, part(t)], M3l[:, m, part(t)], bh[:, m, :], bl[:, m, :],
                                 m == 0, m == NT - 1)
                mm.then_inc(S.a1_mm if stage == 1 else S.a2_mm, 1)

            def gather(g, b, last=False):
                if b == 0:
                    pe.wait_ge(S.h_lo, g * NT + NT)
                if b == 2 and not last:
                    pe.wait_ge(S.u_lr, g * 2 + 1)
                elif b == 3 and not last:
                    pe.wait_ge(S.q_cp, g * 2 + 1)
                o = gather_bank(b, last)
                for t in range(NT):
                    pe.matmul(o, Ch[:, t, part(b)], gat[:, t, :], start=(t == 0), stop=False)
                    mm = pe.matmul(o, Cl[:, t, part(b)], gat[:, t, :], start=False, stop=(t == NT - 1))
                mm.then_inc(S.g_mm, 1)

            def project(g, p, last=False):
                pe.wait_ge(S.g_lo, g * GB + (2 * p + 2))
                gh, gl = gathered(p, last)
                ub, qb = project_banks(p, last)
                product(ub[:, :], linh[:, :], linl[:, :], gh[:, :, 0:E], gl[:, :, 0:E], True, True).then_inc(S.u_mm, 1)
                product(qb[:, :], valh[:, :], vall[:, :], gh[:, :, E:2 * E], gl[:, :, E:2 * E], True, True).then_inc(S.q_mm, 1)

            def scores(g, p, last=False):
                pe.wait_ge(S.u_lr, g * 2 + (p + 1))
                if p == 0:
                    pe.wait_ge(S.a2_out, g * NT + NT)
                for b in range(2 * p, 2 * p + 2):
                    mm = pe.matmul(PA[0][0:GH, 0:E], apad[:, b, :], leaked(p, last)[:, (b % 2) * E:(b % 2 + 1) * E],
                                   start=(b == 0), stop=(b == GB - 1))
                mm.then_inc(S.e_mm, 1)

            def spread(g, p, last=False):
                if p == 0:
                    pe.wait_ge(S.attn_ready, g + 1)
                if not last:
                    pe.wait_ge(S.z_lo, (g + 1) * (GB * NT) + (GB * NT - 1 + p))
                for b in range(2 * p, 2 * p + 2):
                    for m in (atth, attl):
                        mm = pe.matmul(PZ[p][:, (b % 2) * E:(b % 2 + 1) * E], selr[:, b, :], m[:, :],
                                       start=(m is atth), stop=(m is attl))
                mm.then_inc(S.bc_mm, 1)

            def project_out(g, p, last=False):
                pe.wait_ge(S.av_lo, g * 2 + (p + 1))
                if p == 0:
                    pe.wait_ge(S.u_lr, g * 2 + 2)
                    pe.wait_ge(S.q_cp, g * 2 + 2)
                vh, vl = weighted(p, last)
                for t in range(ET):
                    for b in range(2 * p, 2 * p + 2):
                        at = slice((b % 2) * E + t * P, (b % 2) * E + (t + 1) * P)
                        mm = product(PL[t][:, part(b)], vh[:, at], vl[:, at],
                                     outh[:, :], outl[:, :], True, True)
                mm.then_inc(S.y_mm, 1)

            def scatter(g, t):
                if t == 0:
                    pe.wait_ge(S.y_lo, g * ET + ET)
                if t >= 2:
                    pe.wait_ge(S.s_out, g * NT + (t - 1))
                for r in range(ET):
                    pe.matmul(PL[t % 2][:, :], scat[:, r, part(t)], Gh[:, r, :], start=(r == 0), stop=False)
                    mm = pe.matmul(PL[t % 2][:, :], scat[:, r, part(t)], Gl[:, r, :], start=False, stop=(r == ET - 1))
                mm.then_inc(S.s_mm, 1)

            def first_body():
                powers(0, 0)
                powers(0, 1)
                setup_square(3, M2h, M2l)
                setup_z()
                blocks(0, 0)
                setup_bias_rows()
                powers(0, 2)
                setup_bias_blocks()
                blocks(0, 1)
                setup_bias_cube(0)
                powers(0, 3)
                setup_bias_cube(1)
                blocks(0, 2)
                setup_edges()
                blocks(0, 3)
                for stage in (1, 2):
                    for t in range(NT):
                        cube(0, t, stage)
                setup_logs()

            def body(g):
                l = g - 1
                powers(g, 0)
                powers(g, 1)
                gather(l, 0)
                gather(l, 1)
                blocks(g, 0)
                project(l, 0)
                powers(g, 2)
                scores(l, 0)
                gather(l, 2)
                gather(l, 3)
                blocks(g, 1)
                project(l, 1)
                powers(g, 3)
                scores(l, 1)
                blocks(g, 2)
                blocks(g, 3)
                cube(g, 0, 1)
                spread(l, 0)
                spread(l, 1)
                cube(g, 1, 1)
                project_out(l, 0)
                cube(g, 2, 1)
                cube(g, 3, 1)
                project_out(l, 1)
                cube(g, 0, 2)
                cube(g, 1, 2)
                scatter(l, 0)
                cube(g, 2, 2)
                scatter(l, 1)
                cube(g, 3, 2)
                scatter(l, 2)
                scatter(l, 3)

            setup_features()
            setup_power(1)
            setup_transposes()
            setup_square(2, M1h, M1l)
            setup_weights()
            first_body()
            with pe.Fori(1, NG - 1) as g:
                body(g)
            body(NG - 1)
            l = NG - 1
            for b in range(GB):
                gather(l, b, True)
            for p in range(2):
                project(l, p, True)
            for p in range(2):
                scores(l, p, True)
            for p in range(2):
                spread(l, p, True)
            for p in range(2):
                project_out(l, p, True)
            for t in range(NT):
                scatter(l, t)

        @block.scalar
        def _(act):
            def copy(o, i):
                return act.activation(o, i, ACT.Copy)

            def x0_round(g, b):
                n = g * GB + b
                act.wait_ge(S.x0_t, n + 1)
                if not (type(g) is int and g == 0 and b < 2):
                    act.wait_ge(S.v_mm, n * POW - POW)
                act.activation(x0h[:, b % 2, :, :].rearrange("p t d -> p (t d)"), xt[:, :], ACT.Relu).then_inc(S.x0_hi, 1)

            def powers(g, b, j0=0, j1=POW):
                n = g * GB + b
                for j in range(j0, j1):
                    act.wait_ge(S.v_mm, g * (GB * POW) + (b * POW + j + 1))
                    if j == 0 and not (type(g) is int and g == 0 and b < 2):
                        act.wait_ge(S.z_mm, n * NT - NT)
                    copy(Vh[:, b % 2, j, :], VB[j][:, :]).then_inc(S.v_hi, 1)

            def blocks(g, b, t0=0, t1=NT):
                for t in range(t0, t1):
                    act.wait_ge(S.z_mm, g * (GB * NT) + (b * NT + t + 1))
                    if b == 0 and t == 0:
                        if type(g) is int and g == 0:
                            act.wait_ge(S.mt_mm, 3 * NT)
                            act.wait_ge(S.tb_step, 2)
                            act.wait_ge(S.zt_done, 1)
                        else:
                            act.wait_ge(S.c_lo, g * NT)
                            act.wait_ge(S.a1_mm, g * NT)
                    copy(B1[:, t, part(b)], PZ[t % 2][:, D:2 * D])
                    copy(B2h[:, t, part(b)], PZ[t % 2][:, 2 * D:3 * D]).then_inc(S.z_hi, 1)

            def middle(g, t):
                act.wait_ge(S.a1_sum, g * NT + (t + 1))
                if t == 0 and not (type(g) is int and g == 0):
                    act.wait_ge(S.g_mm, g * GB)
                copy(Ch[:, t, :], B1[:, t, :]).then_inc(S.c_hi, 1)

            def second_std(g):
                act.wait_ge(S.ln2_var, g + 1)
                act.activation(lnw[:, 4, :], lnw[:, 3, :], ACT.Sqrt).then_inc(S.ln2_std, 1)

            def second_round(g, t):
                act.wait_ge(S.h_t, g * NT + (t + 1))
                if t == 0:
                    act.wait_ge(S.a2_mm, g * NT + NT)
                act.activation(Ch[:, t, :], ht(t), ACT.Relu).then_inc(S.h_hi, 1)

            def gather(g, b, last=False):
                act.wait_ge(S.g_mm, g * GB + (b + 1))
                if b == 2 and not last:
                    act.wait_ge(S.q_mm, g * 2 + 1)
                copy(gathered(b // 2, last)[0][:, b % 2, :], gather_bank(b, last)).then_inc(S.g_hi, 1)

            def project(g, p, last=False):
                act.wait_ge(S.u_mm, g * 2 + (p + 1))
                ub, qb = project_banks(p, last)
                act.activation(sloped(p, last), ub[:, :], ACT.Copy, scale=SLOPE).then_inc(S.u_t, 1)
                act.wait_ge(S.q_mm, g * 2 + (p + 1))
                copy(vv[:, 2 * p:2 * p + 2, :].rearrange("p b e -> p (b e)"), qb[:, :]).then_inc(S.q_cp, 1)

            def exponent(g):
                act.wait_ge(S.e_shift, g + 1)
                act.activation(sm[2][:, :], sm[1][:, :], ACT.Exp).then_inc(S.e_exp, 1)

            def attention_round(g):
                act.wait_ge(S.att_full, g + 1)
                copy(atth[:, :], sm[1][:, :]).then_inc(S.att_hi, 1)

            def weigh(g, p, last=False):
                act.wait_ge(S.av_f, g * 2 + (p + 1))
                if p == 1 and not last:
                    act.wait_ge(S.y_mm, g * 2 + 1)
                copy(weighted(p, last)[0],
                     vv[:, 2 * p:2 * p + 2, :].rearrange("p b e -> p (b e)")).then_inc(S.av_hi, 1)

            def edge_out(g, t):
                if t == 0:
                    act.wait_ge(S.y_mm, g * 2 + 2)
                copy(Gh[:, t, :], PL[t][:, :]).then_inc(S.y_hi, 1)

            def setup():
                act.dma_start(small[:, 0:NT], alpha.rearrange("(p t) -> p t", t=NT)).then_inc(S.ld_alpha, 16)
                act.dma_start(wraw[:, 0, :], w).then_inc(S.ld_w, 16)
                act.dma_start(small[:, 4:5], d.rearrange("(p o) -> p o", o=1)).then_inc(S.ld_cols, 16)
                act.dma_start(stack[:, 0, 0:D], fc_w).then_inc(S.ld_stack, 16)
                act.dma_start(stack[:, 0, 2 * D:2 * D + 1], fc_b.rearrange("(p o) -> p o", o=1)).then_inc(S.ld_stack, 16)
                act.dma_start(small[:, 5:6], a.rearrange("h (e o) -> (h e) o", o=1)).then_inc(S.ld_a, 16)
                for i, m in enumerate((W_lin, W_val, W_out)):
                    act.dma_start(wraw[:, 1 + i, :], m).then_inc(S.ld_l1, 16)
                act.wait_ge(S.ld_alpha, 16)
                act.activation(small[:, 16:16 + NT], small[:, 0:NT], ACT.Sigmoid).then_inc(S.sig_done, 1)
                for c in range(NT):
                    if c == 0:
                        stack_copy(1)
                    act.wait_ge(S.mt_mm, c + 1)
                    copy(M1h[:, c, :], (PV + PA)[c][:, :]).then_inc(S.mt_hi, 1)
                act.wait_ge(S.m_done, NT)
                copy(Mh[:, :, :, :].rearrange("p t c q -> p (t c q)"), Mf[:, :, :, :].rearrange("p t c q -> p (t c q)")).then_inc(S.m_hi, 1)
                stack_copy(2)
                stack_copy(3)
                act.wait_ge(S.ln1_var, 1)
                act.activation(lnw[:, 4, :], lnw[:, 3, :], ACT.Sqrt).then_inc(S.ln1_std, 1)
                for c in range(NT):
                    if c:
                        stack_copy(2 * c + 2)
                        if c < NT - 1:
                            stack_copy(2 * c + 3)
                    square_copy(2, c)
                    if c < 2:
                        x0_round(0, c)
                act.wait_ge(S.w_mm3, 1)
                for i, m3 in enumerate((linh, valh, outh)):
                    copy(m3[:, :], PZ[0][:, part(i)]).then_inc(S.w_hi, 1)

            def stack_copy(i):
                act.wait_ge(S.st_mm, i)
                copy(stack[:, i, :], PZ[1][:, 0:2 * D + 1]).then_inc(S.st_sb, 1)

            def square_copy(j, c):
                act.wait_ge(S.mt_mm, NT * (j - 1) + c + 1)
                copy((M2h if j == 2 else M3h)[:, c, :], (PA + PL)[c][:, :]).then_inc(S.mt_hi, 1)

            def first_std(g):
                act.wait_ge(S.ln1_var, g + 1)
                act.activation(lnw[:, 4, :], lnw[:, 3, :], ACT.Sqrt).then_inc(S.ln1_std, 1)

            def setup_z():
                for k in range(STEPS + 1):
                    act.wait_ge(S.zt_mm, k + 1)
                    copy(Zh[:, k % POW, part(k // POW)], PZ[k % 2][:, 0:P]).then_inc(S.zk_hi, 1)

            def setup_bias_rows():
                act.wait_ge(S.tb_mm, 1)
                copy(urow, PL[0][0:POW, :]).then_inc(S.u_sb, 1)
                act.wait_ge(S.tb_mm, 2)
                copy(crow[:, :], PL[1][0:POW, 0:BLOCKS * D]).then_inc(S.u_sb, 1)

            def setup_bias_blocks():
                for t in range(NT):
                    act.wait_ge(S.tb_mm, 3 + t)
                    copy(bb[:, t, :], PL[t % 2][:, 0:BLOCKS * D]).then_inc(S.bb_sb, 1)
                act.wait_ge(S.bb_sb, NT)
                copy(tbh[:, :, :], bb[:, :, 2 * D:3 * D]).then_inc(S.tb_hi, 1)

            def setup_bias_again():
                act.wait_ge(S.tb_step, 4)
                copy(tbh[:, :, :], TB[:, :, :]).then_inc(S.tb_hi, 1)

            def setup_logs():
                act.wait_ge(S.ed_log, 1)
                act.activation(picked[:, :], picked[:, :], ACT.Ln).then_inc(S.ed_pick, 1)

            def first_body():
                powers(0, 0)
                powers(0, 1)
                for c in range(NT):
                    square_copy(3, c)
                x0_round(0, 2)
                setup_z()
                for t in range(NT):
                    blocks(0, 0, t, t + 1)
                setup_bias_rows()
                first_std(1)
                powers(0, 2)
                x0_round(0, 3)
                setup_bias_blocks()
                blocks(0, 1)
                first_std(2)
                powers(0, 3, 0, 1)
                setup_bias_again()
                powers(0, 3, 1, 3)
                x0_round(1, 0)
                blocks(0, 2)
                first_std(3)
                blocks(0, 3)
                for t in range(NT):
                    middle(0, t)
                x0_round(1, 1)
                setup_logs()
                second_std(0)

            def body(g, last):
                l = g - 1
                powers(g, 0, 0, 1)
                second_round(l, 0)
                powers(g, 0, 1, 2)
                second_round(l, 1)
                powers(g, 0, 2, 3)
                second_round(l, 2)
                powers(g, 1, 0, 1)
                second_round(l, 3)
                powers(g, 1, 1, 3)
                x0_round(g, 2)
                gather(l, 0)
                gather(l, 1)
                blocks(g, 0)
                project(l, 0)
                powers(g, 2)
                x0_round(g, 3)
                gather(l, 2)
                gather(l, 3)
                blocks(g, 1)
                project(l, 1)
                powers(g, 3)
                if not last:
                    x0_round(g + 1, 0)
                blocks(g, 2, 0, 2)
                exponent(l)
                blocks(g, 2, 2, 4)
                blocks(g, 3)
                attention_round(l)
                middle(g, 0)
                weigh(l, 0)
                middle(g, 1)
                weigh(l, 1)
                middle(g, 2)
                middle(g, 3)
                if not last:
                    x0_round(g + 1, 1)
                for t in range(ET):
                    edge_out(l, t)
                second_std(g)

            setup()
            first_body()
            with act.Fori(1, NG - 1) as g:
                body(g, False)
            body(NG - 1, True)
            l = NG - 1
            for t in range(NT):
                second_round(l, t)
            for b in range(GB):
                gather(l, b, True)
            for p in range(2):
                project(l, p, True)
            exponent(l)
            attention_round(l)
            for p in range(2):
                weigh(l, p, True)
            for t in range(ET):
                edge_out(l, t)

        @block.vector
        def _(dve):
            def tt(o, x_, y_, op):
                return dve.tensor_tensor(o, x_, y_, op)

            def ts(o, x_, s1, s2, op0, op1=None):
                return dve.tensor_scalar(o, x_, s1, s2, op0, op1) if op1 is not None else dve.tensor_scalar(o, x_, s1, s2, op0)

            def stt(o, x_, s, y_, op0, op1):
                return dve.scalar_tensor_tensor(out=o, in0=x_, scalar=s, in1=y_, op0=op0, op1=op1)

            def low(o, v, hi):
                return tt(o, v, hi.bitcast(F32), ALU.subtract)

            def norm_mean(count, step, var, mean_out):
                st = stats[:, :, :]
                me, ve, mo, vo = st[:, :, 1], st[:, :, 2], st[:, :, 4], st[:, :, 5]
                tt(lnw[:, 0, :], me, mo, ALU.add)
                tt(lnw[:, 1, :], me, mo, ALU.subtract)
                tt(lnw[:, 2, :], ve, vo, ALU.add).then_inc(step, 1)
                dve.wait_ge(step, count + 1)
                tt(lnw[:, 1, :], lnw[:, 1, :], lnw[:, 1, :], ALU.mult)
                ts(mean_out, lnw[:, 0, :], 0.5, None, ALU.mult).then_inc(step, 1)
                dve.wait_ge(step, count + 2)
                stt(lnw[:, 2, :], lnw[:, 1, :], D / 4.0, lnw[:, 2, :], ALU.mult, ALU.add).then_inc(step, 1)
                dve.wait_ge(step, count + 3)
                ts(lnw[:, 3, :], lnw[:, 2, :], 1.0 / D, LN_EPS, ALU.mult, ALU.add).then_inc(var, 1)

            def norm_rstd(g, count, step, std, rstd_out):
                dve.wait_ge(std, g + 1)
                dve.reciprocal(lnw[:, 5, :], lnw[:, 4, :]).then_inc(step, 1)
                dve.wait_ge(step, count + 4)
                tt(lnw[:, 0, :], lnw[:, 5, :], lnw[:, 5, :], ALU.mult).then_inc(step, 1)
                dve.wait_ge(step, count + 5)
                tt(lnw[:, 0, :], lnw[:, 0, :], lnw[:, 3, :], ALU.mult).then_inc(step, 1)
                dve.wait_ge(step, count + 6)
                ts(lnw[:, 0, :], lnw[:, 0, :], -0.5, 1.5, ALU.mult, ALU.add).then_inc(step, 1)
                dve.wait_ge(step, count + 7)
                tt(rstd_out, lnw[:, 5, :], lnw[:, 0, :], ALU.mult).then_inc(step, 1)
                dve.wait_ge(step, count + NORM_STEPS)

            NORM_STEPS = 8

            def first_stats(g, b):
                if b == 0:
                    dve.wait_ge(x_loaded[g], 16)
                for t in range(NT):
                    mm = dve.bn_stats(stats[:, b * NT + t, :], X[:, g, b, t, :])
                if b == GB - 1:
                    mm.then_inc(S.ln1_done, 1)

            def first_mean(g):
                dve.wait_ge(S.ln1_done, g + 1)
                n = GB * NT
                norm_mean(g * NORM_STEPS, S.ln1_step, S.ln1_var, mean1[:, g * n:(g + 1) * n])

            def first_rstd(g):
                n = GB * NT
                norm_rstd(g, g * NORM_STEPS, S.ln1_step, S.ln1_std, rstd1[:, g * n:(g + 1) * n])

            def x0_norm(g, b):
                n = g * GB + b
                if not (type(g) is int and n == 0):
                    dve.wait_ge(S.x0_lo, n)
                if b == 2 and not (type(g) is int and g == 0):
                    dve.wait_ge(S.h_lo, g * NT)
                for t in range(NT):
                    n = g * (GB * NT) + (b * NT + t)
                    mm = ts(xt[:, part(t)], xg(g, b, t), mean1[:, bass.ds(n, 1)], rstd1[:, bass.ds(n, 1)],
                            ALU.subtract, ALU.mult)
                mm.then_inc(S.x0_t, 1)

            def x0_low(g, b):
                dve.wait_ge(S.x0_hi, g * GB + (b + 1))
                stt(x0l[:, b % 2, :, :].rearrange("p t d -> p (t d)"), xt[:, :], 0.0,
                    x0h[:, b % 2, :, :].rearrange("p t d -> p (t d)").bitcast(F32), ALU.max, ALU.subtract).then_inc(S.x0_lo, 1)

            def powers(g, b, j0=0, j1=POW):
                for j in range(j0, j1):
                    dve.wait_ge(S.v_hi, g * (GB * POW) + (b * POW + j + 1))
                    low(Vl[:, b % 2, j, :], VB[j][:, :], Vh[:, b % 2, j, :]).then_inc(S.v_lo, 1)

            def blocks(g, b, t0=0, t1=NT):
                for t in range(t0, t1):
                    dve.wait_ge(S.z_hi, g * (GB * NT) + (b * NT + t + 1))
                    tt(xg(g, b, t), PZ[t % 2][:, 0:D], xg(g, b, t), ALU.add)
                    low(B2l[:, t, part(b)], PZ[t % 2][:, 2 * D:3 * D], B2h[:, t, part(b)]).then_inc(S.z_lo, 1)

            def middle_sum(g, t):
                dve.wait_ge(S.a1_mm, g * NT + (t + 1))
                tt(B1[:, t, :], PA[t % 2][:, :], B1[:, t, :], ALU.add).then_inc(S.a1_sum, 1)

            def middle_low(g, t):
                dve.wait_ge(S.c_hi, g * NT + (t + 1))
                low(Cl[:, t, :], B1[:, t, :], Ch[:, t, :]).then_inc(S.c_lo, 1)

            def first_layer(g, t):
                dve.wait_ge(S.tb_added, g * NT + (t + 1))
                dve.wait_ge(S.a2_mm, g * NT + (t + 1))
                tt(xg(g, None, t), PA[t % 2][:, :].rearrange("p (b d) -> p b d", b=GB), xg(g, None, t), ALU.add).then_inc(S.a2_out, 1)
                dve.wait_ge(S.a2_out, g * NT + (t + 1))
                dve.memset(carrier[:, :], 0.0)
                for b in range(GB):
                    mm = dve.bn_stats(stats[:, b * NT + t, :], xg(g, b, t))
                mm.then_inc(S.ln2_step, 1)

            L2 = NT + NORM_STEPS

            def second_mean(g):
                dve.wait_ge(S.ln2_step, g * L2 + NT)
                norm_mean(g * L2 + NT, S.ln2_step, S.ln2_var, norm2[:, 0, :])

            def second_rstd(g):
                norm_rstd(g, g * L2 + NT, S.ln2_step, S.ln2_std, norm2[:, 1, :])

            def second_norm(g, t, x0_made):
                if t == 0:
                    dve.wait_ge(S.x0_lo, x0_made)
                elif t >= 2:
                    dve.wait_ge(S.h_lo, g * NT + (t - 1))
                for b in range(GB):
                    n = b * NT + t
                    mm = ts(ht(t)[:, part(b)], xg(g, b, t), norm2[:, 0, n:n + 1], norm2[:, 1, n:n + 1],
                            ALU.subtract, ALU.mult)
                mm.then_inc(S.h_t, 1)

            def second_low(g, t):
                dve.wait_ge(S.h_hi, g * NT + (t + 1))
                stt(Cl[:, t, :], ht(t), 0.0, Ch[:, t, :].bitcast(F32), ALU.max, ALU.subtract).then_inc(S.h_lo, 1)

            def gather(g, b, last=False):
                dve.wait_ge(S.g_hi, g * GB + (b + 1))
                gh, gl = gathered(b // 2, last)
                low(gl[:, b % 2, :], gather_bank(b, last), gh[:, b % 2, :]).then_inc(S.g_lo, 1)

            def leaky(g, p, last=False):
                dve.wait_ge(S.u_t, g * 2 + (p + 1))
                tt(leaked(p, last), project_banks(p, last)[0][:, :], sloped(p, last), ALU.max).then_inc(S.u_lr, 1)

            SOFT = 7

            def scan(o, mask, v, first, op0, op1):
                return dve.tensor_tensor_scan(o, mask, v, first, op0, op1)

            def softmax_max(g):
                dve.wait_ge(S.e_mm, g * 2 + 2)
                tt(sm[0][:, :], PA[0][0:GH, 0:E], lgrow[:, :], ALU.add).then_inc(S.soft_step, 1)
                dve.wait_ge(S.soft_step, g * SOFT + 1)
                scan(sm[1][:, :], far[:, 0:E], sm[0][:, :], LEAST, ALU.add, ALU.max).then_inc(S.soft_step, 1)

            def softmax_shift(g):
                dve.wait_ge(S.soft_step, g * SOFT + 2)
                scan(sm[2][:, ::-1], far[:, 1:E + 1][:, ::-1], sm[1][:, ::-1], LEAST, ALU.add, ALU.max).then_inc(S.soft_step, 1)
                dve.wait_ge(S.soft_step, g * SOFT + 3)
                tt(sm[1][:, :], sm[0][:, :], sm[2][:, :], ALU.subtract).then_inc(S.e_shift, 1)

            def softmax_sum(g, step):
                if step == 0:
                    dve.wait_ge(S.e_exp, g + 1)
                    scan(sm[0][:, :], same[:, 0:E], sm[2][:, :], 0.0, ALU.mult, ALU.add).then_inc(S.soft_step, 1)
                else:
                    dve.wait_ge(S.soft_step, g * SOFT + 4)
                    scan(sm[1][:, ::-1], same[:, 1:E + 1][:, ::-1], sm[0][:, ::-1], 0.0, ALU.mult, ALU.max).then_inc(S.soft_step, 1)

            def softmax_divide(g, half):
                dve.wait_ge(S.soft_step, g * SOFT + 5 + half)
                dve.reciprocal(sm[0][:, half * P:(half + 1) * P], sm[1][:, half * P:(half + 1) * P]).then_inc(S.soft_step, 1)
                if half:
                    dve.wait_ge(S.soft_step, g * SOFT + 7)
                    tt(sm[1][:, :], sm[2][:, :], sm[0][:, :], ALU.mult).then_inc(S.att_full, 1)

            def attention_low(g):
                dve.wait_ge(S.att_hi, g + 1)
                low(attl[:, :], sm[1][:, :], atth[:, :]).then_inc(S.attn_ready, 1)

            def weigh(g, p):
                dve.wait_ge(S.bc_mm, g * 2 + (p + 1))
                v = vv[:, 2 * p:2 * p + 2, :].rearrange("p b e -> p (b e)")
                tt(v, PZ[p][:, :], v, ALU.mult).then_inc(S.av_f, 1)

            def weigh_low(g, p, last=False):
                dve.wait_ge(S.av_hi, g * 2 + (p + 1))
                hi_, lo_ = weighted(p, last)
                low(lo_, vv[:, 2 * p:2 * p + 2, :].rearrange("p b e -> p (b e)"), hi_).then_inc(S.av_lo, 1)

            def edge_out(g, t):
                dve.wait_ge(S.y_hi, g * ET + (t + 1))
                low(Gl[:, t, :], PL[t][:, :], Gh[:, t, :]).then_inc(S.y_lo, 1)

            def second_layer(g, t):
                dve.wait_ge(S.s_mm, g * NT + (t + 1))
                tt(xg(g, None, t), PL[t % 2][:, :].rearrange("p (b d) -> p b d", b=GB), xg(g, None, t), ALU.add).then_inc(S.s_out, 1)

            def setup():
                dve.wait_ge(S.iota_done, 1)
                ts(ident[:, :], idgrid, 0.0, None, ALU.is_equal).then_inc(S.id_done, 1)
                ts(stack[:, 0, D:2 * D], idgrid, 0.0, None, ALU.is_equal).then_inc(S.r_sb, 1)
                ts(identr[:, :], idgrid, 0.0, None, ALU.is_equal)

                dve.wait_ge(S.sig_done, 1)
                ts(scol_col[:, :], small[:, 16:16 + NT], DT / 2, None, ALU.mult)
                ts(ccol[:, :], small[:, 16:16 + NT], -DT / 2, 1.0 - DT, ALU.mult, ALU.add).then_inc(S.m_step, 1)
                dve.wait_ge(S.ld_cols, 16)
                ts(small[:, 20:21], small[:, 4:5], 0.0, 1.0, ALU.max, ALU.min).then_inc(S.z_step, 1)
                dve.wait_ge(S.r_mm, 1)
                dve.wait_ge(S.z_step, 1)
                ts(wTd, PZ[0][:, 0:P], small[:, 20:21], DT, ALU.mult, ALU.mult)
                dve.tensor_copy(wT, PZ[0][:, 0:P]).then_inc(S.r_sb, 1)
                dve.wait_ge(S.iota_done, 3)
                dve.wait_ge(S.m_step, 1)
                dve.wait_ge(S.ld_adj, 16)
                for t in range(NT):
                    m = Mf[:, t, :, :].rearrange("p c q -> p (c q)")
                    ts(m, nodegrid, nodecol[:, t:t + 1], ccol[:, t:t + 1], ALU.is_equal, ALU.mult).then_inc(S.m_step, 1)
                for t in range(NT):
                    dve.wait_ge(S.m_step, 2 + t)
                    stt(Mf[:, t, :, :], A[:, t, :].rearrange("p (q c) -> p c q", c=NT), scol_col[:, t:t + 1],
                        Mf[:, t, :, :], ALU.mult, ALU.add).then_inc(S.m_done, 1)
                dve.wait_ge(S.r_mm, 2)
                dve.tensor_copy(R, PZ[0][:, P:2 * P]).then_inc(S.r_sb, 1)
                for c in range(NT):
                    dve.wait_ge(S.mt_hi, c + 1)
                    low(M1l[:, c, :], (PV + PA)[c][:, :], M1h[:, c, :]).then_inc(S.mt_lo, 1)
                dve.wait_ge(S.m_hi, 1)
                low(Ml[:, :, :, :].rearrange("p t c q -> p (t c q)"), Mf[:, :, :, :].rearrange("p t c q -> p (t c q)"),
                    Mh[:, :, :, :].rearrange("p t c q -> p (t c q)")).then_inc(S.m_lo, 1)
                dve.wait_ge(S.iota_done, 8)
                ts(selr[:, :, :], sel, 0.0, None, ALU.is_equal).then_inc(S.vv_free, 1)
                for b in range(GB):
                    first_stats(0, b)
                first_mean(0)
                first_rstd(0)
                for c in range(NT):
                    if c < 2:
                        x0_norm(0, c)
                    square_low(2, c)
                    if c < 2:
                        x0_low(0, c)
                dve.wait_ge(S.w_hi, 3)
                for i, (lo_, hi_) in enumerate(((linl, linh), (vall, valh), (outl, outh))):
                    mm = low(lo_[:, :], PZ[0][:, part(i)], hi_[:, :])
                mm.then_inc(S.w_lo, 1)

            def square_low(j, c):
                dve.wait_ge(S.mt_hi, (j - 1) * NT + c + 1)
                lo_, hi_ = (M2l, M2h) if j == 2 else (M3l, M3h)
                low(lo_[:, c, :], (PA + PL)[c][:, :], hi_[:, c, :]).then_inc(S.mt_lo, 1)

            def setup_zt(i):
                if i < 0:
                    dve.wait_ge(S.st_sb, STEPS)
                    dve.wait_ge(S.vv_free, 1)
                    for k in range(STEPS + 1):
                        last = ts(ztk(k), stack[:, STEPS - k, 0:D], float(comb(STEPS, k)), None, ALU.mult)
                else:
                    dve.wait_ge(S.z_step, i + 2)
                    for k in range(STEPS - i):
                        last = stt(ztk(k), stack[:, i, D:2 * D], DT * comb(i + k, k), ztk(k), ALU.mult, ALU.add)
                last.then_inc(S.z_step if i < STEPS - 1 else S.zt_done, 1)

            def setup_ccols():
                for k in range(STEPS + 1):
                    mm = ts(ccols(k // POW)[:, k % POW:k % POW + 1], stack[:, STEPS - k, 2 * D:2 * D + 1],
                            float(comb(STEPS, k)), None, ALU.mult)
                mm.then_inc(S.tb_step, 1)

            def setup_z():
                for k in range(STEPS + 1):
                    dve.wait_ge(S.zk_hi, k + 1)
                    low(Zl[:, k % POW, part(k // POW)], PZ[k % 2][:, 0:P], Zh[:, k % POW, part(k // POW)]).then_inc(S.zk_lo, 1)

            def setup_ones():
                dve.wait_ge(S.tb_step, 1)
                dve.memset(onesr[:, :].bitcast(F32), 1.0)
                for j in range(POW):
                    mm = dve.memset(rowsel[:, j, :].bitcast(F32), 0.0)
                mm.then_inc(S.tb_step, 1)
                for j in range(POW):
                    if j == 0:
                        dve.wait_ge(S.tb_step, 2)
                    mm = dve.memset(rowsel[:, j, j:j + 1].bitcast(F32), 1.0 if j else 1.0 / P)
                mm.then_inc(S.tb_step, 1)

            def setup_bias_first():
                dve.wait_ge(S.tb_hi, 1)
                low(tbl[:, :, :], bb[:, :, 2 * D:3 * D], tbh[:, :, :]).then_inc(S.tb_lo, 1)

            def setup_bias_again():
                dve.wait_ge(S.tb_mm, 3 + NT)
                tt(TB[:, :, :], PL[0][:, :].rearrange("p (t d) -> p t d", t=NT), bb[:, :, D:2 * D], ALU.add).then_inc(S.tb_step, 1)
                dve.wait_ge(S.tb_hi, 2)
                low(tbl[:, :, :], TB[:, :, :], tbh[:, :, :]).then_inc(S.tb_lo, 1)

            def setup_bias_last():
                dve.wait_ge(S.tb_mm, 4 + NT)
                tt(TB[:, :, :], PL[1][:, :].rearrange("p (t d) -> p t d", t=NT), bb[:, :, 0:D], ALU.add).then_inc(S.tb_out, 1)

            def setup_edges_rank(step):
                if step == 0:
                    dve.wait_ge(S.ld_idx, 64)
                    dve.tensor_copy(rowf[:, :], irow[:, 0, :])
                    dve.tensor_copy(colf, icol.rearrange("p s t -> p t s")).then_inc(S.ed_step, 1)
                    dve.wait_ge(S.ed_step, 1)
                    stt(keyrow[:, :], rowf[:, :], float(E), egrid, ALU.mult, ALU.add)
                    stt(keycol, colf[:, :, 0], float(E), small[:, 8:8 + ET], ALU.mult, ALU.add).then_inc(S.ed_step, 1)
                elif step == 1:
                    dve.wait_ge(S.ed_step, 2)
                    for t in range(ET):
                        mm = ts(perm[:, t, :], keyrow[:, :], keycol[:, t:t + 1], None, ALU.is_lt)
                    mm.then_inc(S.ed_step, 1)
                elif step == 2:
                    dve.wait_ge(S.ed_step, 3)
                    for t in range(ET):
                        mm = dve.tensor_reduce(rank[:, t:t + 1], perm[:, t, :], AX_X, ALU.add)
                    mm.then_inc(S.ed_step, 1)
                else:
                    dve.wait_ge(S.ed_step, 4)
                    for t in range(ET):
                        ts(perm[:, t, :], egrid, rank[:, t:t + 1], None, ALU.is_equal)
                    for s in range(2):
                        for t in range(ET):
                            mm = ts(ecolb[:, s, t, :], ident[:, :], 0.0, colf[:, t, s:s + 1], ALU.mult, ALU.add)
                    mm.then_inc(S.ed_step, 1)

            def setup_edges(step):
                if step == 0:
                    dve.wait_ge(S.ed_mm, 1)
                    dve.tensor_copy(nrow[:, :, :].rearrange("p s e -> p (s e)"), PL[0][:, :])
                    dve.tensor_copy(ncol, PL[1][:, 0:2 * ET].rearrange("p (t s) -> p t s", s=2)).then_inc(S.ed_sb, 1)
                    dve.wait_ge(S.ed_sb, 1)
                    stt(flat, ncol[:, :, 0], float(N), ncol[:, :, 1], ALU.mult, ALU.add).then_inc(S.ed_flat, 1)
                elif step == 1:
                    tt(same[:, 1:E], nrow[0:GH, 0, 1:E], nrow[0:GH, 0, 0:E - 1], ALU.is_equal)
                    dve.memset(same[:, 0:1], 0.0)
                    dve.memset(same[:, E:E + 1], 0.0).then_inc(S.ed_sb, 1)
                    dve.wait_ge(S.ed_sb, 2)
                    ts(far[:, :], same[:, :], -FAR, FAR, ALU.mult, ALU.add)
                elif step == 2:
                    for t in range(NT):
                        mm = ts(gat[:, t, E:2 * E], nrow[:, 1, :], nodecol[:, t:t + 1], None, ALU.is_equal)
                    mm.then_inc(S.ed_sb, 1)
                elif step == 3:
                    dve.wait_ge(S.ed_sb, 3)
                    for t in range(NT):
                        stt(gat[:, t, 0:E], nrow[:, 0, :], nodecol[:, t:t + 1], gat[:, t, E:2 * E].bitcast(F32), ALU.is_equal, ALU.add)
                else:
                    for t in range(ET):
                        ts(scat[:, t, :], nodegrid, ncol[:, t, 0:1], None, ALU.is_equal)
                    dve.wait_ge(S.ld_a, 16)
                    ts(hm[:, 0:HEADS], small[:, 12:12 + HEADS], 0.0, None, ALU.is_ge)
                    ts(hm[:, HEADS:2 * HEADS], small[:, 12:12 + HEADS], float(DH - 1), small[:, 5:6], ALU.is_le, ALU.mult).then_inc(S.ed_sb, 1)
                    dve.wait_ge(S.ed_sb, 4)
                    for b in range(GB):
                        mm = tt(apad[:, b, b * HEADS:(b + 1) * HEADS], hm[:, 0:HEADS], hm[:, HEADS:2 * HEADS], ALU.mult)
                    mm.then_inc(S.ed_done, 1)

            def setup_logs():
                dve.wait_ge(S.ed_picked, 16 * ET)
                ts(picked[:, :], picked[:, :], LOG_EPS, None, ALU.add).then_inc(S.ed_log, 1)
                dve.wait_ge(S.ed_pick, 1)
                for t in range(ET):
                    mm = ts(logb[:, t, :], ident[:, 0:GH], 0.0, picked[:, t:t + 1], ALU.mult, ALU.add)
                mm.then_inc(S.ed_log, 1)
                dve.wait_ge(S.lg_mm, 1)
                dve.tensor_copy(lgrow[:, :], PL[0][0:GH, 0:E]).then_inc(S.ed_done, 1)

            def first_body():
                setup_zt(-1)
                powers(0, 0, 0, 1)
                setup_zt(0)
                powers(0, 0, 1, 2)
                setup_zt(1)
                powers(0, 0, 2, 3)
                setup_zt(2)
                powers(0, 1, 0, 1)
                setup_zt(3)
                setup_zt(4)
                powers(0, 1, 1, 2)
                setup_zt(5)
                setup_zt(6)
                setup_zt(7)
                setup_ccols()
                powers(0, 1, 2, 3)
                square_low(3, 0)
                square_low(3, 1)
                x0_norm(0, 2)
                square_low(3, 2)
                square_low(3, 3)
                x0_low(0, 2)
                setup_z()
                setup_ones()
                for t in range(NT):
                    blocks(0, 0, t, t + 1)
                    first_stats(1, t)
                first_mean(1)
                powers(0, 2, 0, 1)
                first_rstd(1)
                x0_norm(0, 3)
                powers(0, 2, 1, 2)
                x0_low(0, 3)
                setup_edges_rank(0)
                powers(0, 2, 2, 3)
                setup_edges_rank(1)
                setup_bias_first()
                for t in range(NT):
                    blocks(0, 1, t, t + 1)
                    first_stats(2, t)
                first_mean(2)
                setup_bias_again()
                powers(0, 3, 0, 1)
                first_rstd(2)
                setup_edges_rank(2)
                powers(0, 3, 1, 2)
                setup_edges_rank(3)
                x0_norm(1, 0)
                powers(0, 3, 2, 3)
                x0_low(1, 0)
                setup_bias_last()
                for t in range(NT):
                    blocks(0, 2, t, t + 1)
                    first_stats(3, t)
                first_mean(3)
                setup_edges(0)
                blocks(0, 3, 0, 1)
                first_rstd(3)
                blocks(0, 3, 1, 2)
                setup_edges(1)
                blocks(0, 3, 2, 4)
                middle_sum(0, 0)
                setup_edges(2)
                middle_sum(0, 1)
                middle_low(0, 0)
                setup_edges(3)
                middle_sum(0, 2)
                middle_low(0, 1)
                setup_edges(4)
                middle_sum(0, 3)
                middle_low(0, 2)
                middle_low(0, 3)
                x0_norm(1, 1)
                x0_low(1, 1)
                for t in range(NT):
                    first_layer(0, t)
                second_mean(0)
                setup_logs()

            def middles(g):
                for t in range(NT):
                    middle_sum(g, t)
                    if t:
                        middle_low(g, t - 1)
                middle_low(g, NT - 1)

            def body(g, last):
                l = g - 1
                powers(g, 0, 0, 1)
                second_rstd(l)
                second_norm(l, 0, l * GB + (GB + 2))
                powers(g, 0, 1, 2)
                second_low(l, 0)
                second_norm(l, 1, None)
                powers(g, 0, 2, 3)
                second_low(l, 1)
                second_norm(l, 2, None)
                powers(g, 1, 0, 1)
                second_low(l, 2)
                second_norm(l, 3, None)
                powers(g, 1, 1, 2)
                second_low(l, 3)
                powers(g, 1, 2, 3)
                x0_norm(g, 2)
                x0_low(g, 2)
                gather(l, 0)
                gather(l, 1)
                blocks(g, 0)
                leaky(l, 0)
                powers(g, 2)
                x0_norm(g, 3)
                x0_low(g, 3)
                gather(l, 2)
                gather(l, 3)
                blocks(g, 1)
                leaky(l, 1)
                powers(g, 3)
                if not last:
                    x0_norm(g + 1, 0)
                    x0_low(g + 1, 0)
                blocks(g, 2, 0, 1)
                softmax_max(l)
                blocks(g, 2, 1, 2)
                softmax_shift(l)
                blocks(g, 2, 2, 4)
                softmax_sum(l, 0)
                blocks(g, 3, 0, 1)
                softmax_sum(l, 1)
                blocks(g, 3, 1, 2)
                softmax_divide(l, 0)
                blocks(g, 3, 2, 3)
                softmax_divide(l, 1)
                blocks(g, 3, 3, 4)
                attention_low(l)
                middle_sum(g, 0)
                weigh(l, 0)
                weigh(l, 1)
                weigh_low(l, 0)
                middle_sum(g, 1)
                middle_low(g, 0)
                middle_low(g, 1)
                weigh_low(l, 1)
                middle_sum(g, 2)
                middle_sum(g, 3)
                middle_low(g, 2)
                middle_low(g, 3)
                if not last:
                    x0_norm(g + 1, 1)
                    x0_low(g + 1, 1)
                for t in range(ET):
                    edge_out(l, t)
                first_layer(g, 0)
                first_layer(g, 1)
                second_layer(l, 0)
                first_layer(g, 2)
                second_layer(l, 1)
                first_layer(g, 3)
                second_mean(g)
                second_layer(l, 2)
                second_layer(l, 3)

            setup()
            first_body()
            with dve.Fori(1, NG - 1) as g:
                body(g, False)
            body(NG - 1, True)
            l = NG - 1
            second_rstd(l)
            for t in range(NT):
                second_norm(l, t, NG * GB)
                if t:
                    second_low(l, t - 1)
            second_low(l, NT - 1)
            for b in range(GB):
                gather(l, b, True)
            for p in range(2):
                leaky(l, p, True)
            softmax_max(l)
            softmax_shift(l)
            for h in range(2):
                softmax_sum(l, h)
            for h in range(2):
                softmax_divide(l, h)
            attention_low(l)
            for p in range(2):
                weigh(l, p)
            for p in range(2):
                weigh_low(l, p, True)
            for t in range(ET):
                edge_out(l, t)
            for t in range(NT):
                second_layer(l, t)


def kernel(x, adj, L0_gnn_alpha_train, L0_gnn_w, L0_gnn_d, L0_gnn_fc_in_w, L0_gnn_fc_in_b,
           L1_gnn_W_lin, L1_gnn_W_val, L1_gnn_a, L1_gnn_W_out, L1_gnn_src, L1_gnn_dst):
    import numpy as np
    import concourse.bacc as bacc
    from concourse.bass_utils import run_bass_kernel_spmd

    given = {"x": x, "adj": adj, "alpha": L0_gnn_alpha_train, "w": L0_gnn_w, "d": L0_gnn_d, "fc_w": L0_gnn_fc_in_w,
             "fc_b": L0_gnn_fc_in_b, "W_lin": L1_gnn_W_lin, "W_val": L1_gnn_W_val, "a": L1_gnn_a,
             "W_out": L1_gnn_W_out, "src": L1_gnn_src, "dst": L1_gnn_dst}
    nc = bacc.Bacc("TRN2", target_bir_lowering=False, num_devices=1)
    arrays, args = {}, []
    for name, value in given.items():
        v = np.ascontiguousarray(value)
        arrays[f"in_{name}"] = v
        args.append(nc.dram_tensor(f"in_{name}", v.shape, mybir.dt.from_np(v.dtype), kind="ExternalInput").ap())
    out = nc.dram_tensor("out", arrays["in_x"].shape, F32, kind="ExternalOutput").ap()
    gnn_two_layers(nc, *args, out)
    return run_bass_kernel_spmd(nc, [arrays], core_ids=[0]).results[0]["out"]
```

```python
from contextlib import ExitStack
from math import comb

import concourse.bass as bass
from concourse import mybir

ALU = mybir.AluOpType
ACT = mybir.ActivationFunctionType
AX_X = mybir.AxisListType.X
F32 = mybir.dt.float32
F32R = mybir.dt.float32r
BF16 = mybir.dt.bfloat16
I32 = mybir.dt.int32
U32 = mybir.dt.uint32

P = 128
STEPS = 8
DT = 1.0 / STEPS
POW = 3
LN_EPS = 1e-5
LOG_EPS = 1e-8
SLOPE = 0.2
FAR = -1e30
LEAST = -3e38


def gnn_two_layers(nc, x, adj, alpha, w, d, fc_w, fc_b, W_lin, W_val, a, W_out, src, dst, out):
    B, N, D = x.shape
    E = src.shape[0]
    HEADS, DH = a.shape
    NT = N // P
    ET = E // P
    GB = 4
    NG = B // GB
    W = GB * D
    GH = GB * HEADS
    HALF = GB // 2 * NT
    SOFT = 7
    BLOCKS = (STEPS + POW) // POW
    Q = 32
    assert D == P and N == NT * P and E == 2 * P and NT == 4 and BLOCKS == 3 and W == 512

    with ExitStack() as ctx:
        def sb(name, shape, dt=F32, where=ctx):
            return where.enter_context(nc.sbuf_tensor(name, shape, dt))

        def sem(name):
            return ctx.enter_context(nc.semaphore(name))

        X = sb("X", [P, NG, GB, NT, D])
        MT = [sb(f"MT{j}_{k}", [P, NT, N], F32R) for j in (1, 2, 3) for k in ("hi", "lo")]
        M1h, M1l, M2h, M2l, M3h, M3l = MT
        Zh = sb("Zh", [P, POW, BLOCKS * D], F32R)
        Zl = sb("Zl", [P, POW, BLOCKS * D], F32R)
        TB = sb("TB", [P, NT, D])
        gat = sb("gat", [P, NT, 2 * E], F32R)
        scat = sb("scat", [P, ET, N], F32R)
        linh, linl, valh, vall, outh, outl = [
            sb(n, [P, D], F32R) for n in ("linh", "linl", "valh", "vall", "outh", "outl")]
        ident = sb("ident", [P, P])
        apad = sb("apad", [P, GB, GH])
        lgrow = sb("lgrow", [GH, E])
        far = sb("far", [GH, E + 1], BF16)
        same = sb("same", [GH, E + 1], BF16)
        mean1 = sb("mean1", [P, NG * GB * NT])
        rstd1 = sb("rstd1", [P, NG * GB * NT])
        stats = sb("stats", [P, GB * NT, 6])
        lnw = sb("lnw", [P, 6, GB * NT])
        nodecol = sb("nodecol", [P, NT])
        scol_col = sb("scol_col", [P, NT])
        ccol = sb("ccol", [P, NT])

        xt = sb("xt", [P, NT * D])
        x0h = sb("x0h", [P, 2, NT, D], F32R)
        x0l = sb("x0l", [P, 2, NT, D], F32R)
        Vh = sb("Vh", [P, 2, POW, N], F32R)
        Vl = sb("Vl", [P, 2, POW, N], F32R)
        vv = sb("vv", [P, GB, E])
        selr = sb("selr", [GH, GB, P], F32R)
        atth = sb("atth", [GH, E], F32R)
        attl = sb("attl", [GH, E], F32R)
        sm = [sb(f"sm{i}", [GH, E]) for i in range(3)]
        with ExitStack() as before:
            lr = sb("lr", [P, 2 * E], F32, before)
            lrt = sb("lrt", [P, 2 * E], F32, before)
        avh = sb("avh", [P, 2, E], F32R)
        avl = sb("avl", [P, 2, E], F32R)

        with ExitStack() as early:
            A = sb("A", [P, NT, N], F32, early)
            Mf = sb("Mf", [P, NT, NT, P], F32, early)
            Mh = sb("Mh", [P, NT, NT, P], F32R, early)
            Ml = sb("Ml", [P, NT, NT, P], F32R, early)
            stack = sb("stack", [P, STEPS + 1, 2 * D + 1], F32, early)
            wraw = sb("wraw", [P, 4, D], F32, early)
            feat = sb("feat", [P, 4, D], F32, early)
            irow = sb("irow", [P, 2, E], I32, early)
        sel = vv[0:GH, 0:2, :].rearrange("p b (c e) -> p (b c) e", e=P)
        with ExitStack() as middle_scope:
            sb("skip", [P, 3 * NT * W + 2160], F32, middle_scope)
            Uh = sb("Uh", [P, NT, Q * BLOCKS], F32R, middle_scope)
            Ul = sb("Ul", [P, NT, Q * BLOCKS], F32R, middle_scope)
            onesr = sb("onesr", [P, N], F32R, middle_scope)
            rowsel = sb("rowsel", [P, POW, 4], F32R, middle_scope)
            urow = sb("urow", [Q * BLOCKS, N], F32, middle_scope)
            crow = sb("crow", [Q * BLOCKS, D], F32, middle_scope)
            ecolb = sb("ecolb", [P, 2, ET, P], F32, middle_scope)
            perm = sb("perm", [P, ET, E], F32, middle_scope)
            rowf = sb("rowf", [P, E], F32, middle_scope)
            keyrow = sb("keyrow", [P, E], F32, middle_scope)
            nrow = sb("nrow", [P, 2, E], F32, middle_scope)
        B2h = sb("B2h", [P, NT, W], F32R)
        B2l = sb("B2l", [P, NT, W], F32R)
        B1 = sb("B1", [P, NT, W])
        Ch = sb("Ch", [P, NT, W], F32R)
        Cl = sb("Cl", [P, NT, W], F32R)
        Gh = sb("Gh", [P, 2, 2 * E], F32R)
        Gl = sb("Gl", [P, 2, 2 * E], F32R)
        wT, wTd, R = feat[:, 0, :], feat[:, 1, :], feat[:, 2, :]
        zt = vv[:, :, :].rearrange("p b e -> p (b e)")
        nodegrid = lrt[:, :]
        egrid = lr[:, 0:E]
        idgrid = lr[:, E:E + P]
        small = lr[:, 3 * P:3 * P + 32]
        tiny = lr[:, 3 * P + 32:3 * P + 64]
        norm2 = sb("norm2", [P, 2, GB * NT])
        carrier = sb("carrier", [P, 1])
        colf = tiny[:, 0:2 * ET].rearrange("p (t s) -> p t s", s=2)
        keycol, rank = tiny[:, 4:4 + ET], tiny[:, 6:6 + ET]
        ncol = tiny[:, 8:8 + 2 * ET].rearrange("p (t s) -> p t s", s=2)
        hm = tiny[:, 16:16 + 2 * HEADS]
        logb = lr[:, 3 * P + 64:3 * P + 64 + ET * GH].rearrange("p (t b) -> p t b", t=ET)
        icol = lr[:, 3 * P + 96:3 * P + 96 + 2 * ET].bitcast(I32).rearrange("p (s t) -> p s t", t=ET)
        flat = lr[:, 3 * P + 104:3 * P + 104 + ET].bitcast(U32)
        picked = lr[:, 3 * P + 108:3 * P + 108 + ET]

        def ztk(k):
            return zt[:, k * D:(k + 1) * D] if k < STEPS else feat[:, 3, :]

        ccols = TB[:, 0, 0:Q * BLOCKS]

        bank = [ctx.enter_context(nc.psum_tensor(f"bank{i}", [P, 512], F32)) for i in range(8)]
        PV, PZ, PA, PL = bank[0:2], bank[2:4], bank[4:6], bank[6:8]
        VB = PV + PA[1:2]

        names = """ld_alpha ld_w ld_stack ld_cols ld_idx ld_l1 ld_a vv_free iota_done sig_done m_step m_done m_hi
            m_lo_first m_lo_rest mt_mm mt_hi mt_lo z_step r_mm r_sb st_mm st_sb zt_done zt_mm zk_hi zk_lo
            ln1_step ln1_var ln1_std ln1_done w_mm3 w_hi w_lo id_done tb_step tb_mm u_sb tb_hi tb_lo tb_out
            tb_added ed_step ed_mm ed_sb ed_flat ed_pick ed_picked ed_log ed_done lg_mm x0_c x0_t x0_hi
            x0_lo v_mm v_hi v_lo z_mm z_hi z_lo a1_mm a1_sum c_hi c_lo a2_mm a2_out ln2_step ln2_var ln2_std
            h_t h_hi h_lo g_mm g_hi g_lo u_mm u_t u_lr q_mm q_cp e_mm soft_step e_shift e_exp att_full
            att_hi attn_ready bc_mm av_f av_hi av_lo y_mm y_hi y_lo s_mm s_out stored
            """.split()
        S = type("Semaphores", (), {n: sem(n) for n in names})
        ld_adj = [sem(f"ld_adj{h}") for h in range(2)]
        End = type("EndSemaphores", (), {n: sem("end_" + n) for n in
                                        "a_mm x1 h_t h_c h_p h_hi h_lo y_hi y_lo s_mm s_out".split()})
        end_ln, end_var, end_std, end_steps, end_shift, end_exp, end_full = [
            [sem(f"end_{n}{h}") for h in range(2)] for n in "ln var std soft shift exp full".split()]
        x_loaded = [sem(f"x_loaded{g}") for g in range(NG)]

        x_d = x.rearrange("(g b) (p t) d -> g p b t d", b=GB, t=NT)
        out_d = out.rearrange("(g b) (p t) d -> g p b t d", b=GB, t=NT)

        def xg(g, b=None, t=None):
            v = X[:, bass.ds(g, 1), :, :, :]
            if t is None:
                return v[:, :, b, :, :].rearrange("p o t d -> p (o t) d")
            if b is None:
                return v[:, :, :, t, :].rearrange("p o b d -> p (o b) d")
            return v[:, :, b, t, :].rearrange("p o d -> p (o d)")

        def xn(g, b):
            if b != 1:
                return xt[:, :]
            return A[:, 0, :] if type(g) is int and g == 0 else B1[:, NT - 1, :]

        def ht(t):
            return (lrt if t % 2 else lr)[:, :]

        HW = W // 2

        def half(h):
            return slice(h * HW, (h + 1) * HW)

        def xh(h, t):
            return X[:, NG - 1, 2 * h:2 * h + 2, t, :]

        def pairs(v):
            return v.rearrange("p (b d) -> p b d", b=2)

        def end_cube_bank(t):
            return (PA + PV)[t]

        def end_scatter_bank(h, t):
            return (PA + (PV if h else PL))[t]

        def end_ht(t):
            return (lr, lrt)[t // 2][:, (t % 2) * HW:(t % 2 + 1) * HW]

        def end_softmax(h):
            if h == 0:
                return sm[0][:, :], sm[1][:, :], sm[2][:, :], atth[:, :], attl[:, :]
            return (B1[0:GH, 0, 0:E], B1[0:GH, 0, E:2 * E], B1[0:GH, 1, 0:E],
                    Ch[0:GH, 1, 0:E], Cl[0:GH, 1, 0:E])

        def gather_bank(b, last):
            return (PA + PV if last else PL + PL)[b][:, :]

        def gathered(p, last):
            if last:
                return B2h[:, 2 * p:2 * p + 2, :], B2l[:, 2 * p:2 * p + 2, :]
            return Gh[:, :, :], Gl[:, :, :]

        def weighted(p, last):
            if p == 0:
                return avh[:, :, :].rearrange("p b e -> p (b e)"), avl[:, :, :].rearrange("p b e -> p (b e)")
            return (Ch[:, 0, :], Cl[:, 0, :]) if last else (Gh[:, 0, :], Gl[:, 0, :])

        def leaked(p, last):
            return B1[:, 2 * p, :] if last else lr[:, :]

        def sloped(p, last):
            return B1[:, 2 * p + 1, :] if last else lrt[:, :]

        def project_banks(p, last):
            return PZ if last and p else PL

        def spread_bank(p, last):
            return (PV if last else PZ)[p]

        def scatter_bank(t, spare):
            return (PL + (PZ if spare else PL))[t]

        def part(t):
            return slice(t * P, (t + 1) * P)

        NORM_STEPS = 8
        L2 = NT + NORM_STEPS

        block = ctx.enter_context(nc.Block())

        @block.sync
        def _(sp):
            for t in range(0, NT, 2):
                sp.dma_start(A[:, t:t + 2, :], adj.rearrange("(p t) m -> p t m", t=NT)[:, t:t + 2, :]).then_inc(ld_adj[t // 2], 16)
            sp.wait_ge(S.ld_alpha, 16)
            sp.dma_start(X[:, 0, :, :, :], x_d[0]).then_inc(x_loaded[0], 16)
            for i, m in enumerate((W_lin, W_val, W_out)):
                sp.dma_start(wraw[:, 1 + i, :], m).then_inc(S.ld_l1, 16)
            sp.dma_start(small[:, 5:6], a.rearrange("h (e o) -> (h e) o", o=1)).then_inc(S.ld_a, 16)
            for g in range(1, NG):
                sp.dma_start(X[:, g, :, :, :], x_d[g]).then_inc(x_loaded[g], 16)
            for i, e in enumerate((src, dst)):
                sp.dma_start(irow[:, i, :], e.partition_broadcast(P)).then_inc(S.ld_idx, 16)
                sp.dma_start(icol[:, i, :], e.rearrange("(p t) -> p t", t=ET)).then_inc(S.ld_idx, 16)
            with sp.Fori(0, NG - 1) as g:
                sp.wait_ge(S.s_out, g * NT + NT)
                sp.dma_start(out_d[bass.ds(g, 1)].rearrange("o p b t d -> (o p) b t d"),
                             X[:, bass.ds(g, 1), :, :, :].rearrange("p o b t d -> p (o b) t d")).then_inc(S.stored, 16)
            sp.wait_ge(End.s_out, NT)
            sp.dma_start(out_d[NG - 1][:, 0:2], X[:, NG - 1, 0:2, :, :]).then_inc(S.stored, 16)
            for t in range(2, NT + 1, 2):
                sp.wait_ge(End.s_out, NT + t)
                sp.dma_start(out_d[NG - 1][:, 2:4, t - 2:t, :], X[:, NG - 1, 2:4, t - 2:t, :]).then_inc(S.stored, 16)
            sp.wait_ge(S.stored, 16 * (NG - 1 + 3))

        @block.gpsimd
        def _(pool):
            exact = dict(allow_small_or_imprecise_dtypes=True)
            pool.iota(idgrid, [[1, P]], base=0, channel_multiplier=-1, **exact).then_inc(S.iota_done, 1)
            pool.iota(nodecol[:, :], [[1, NT]], base=0, channel_multiplier=NT, **exact).then_inc(S.iota_done, 1)
            pool.iota(nodegrid, [[1, NT], [NT, P]], base=0, channel_multiplier=0, **exact).then_inc(S.iota_done, 1)
            pool.iota(egrid, [[1, E]], base=0, channel_multiplier=0, **exact).then_inc(S.iota_done, 1)
            pool.iota(small[:, 8:8 + ET], [[1, ET]], base=0, channel_multiplier=ET, **exact).then_inc(S.iota_done, 1)
            pool.iota(small[:, 12:12 + HEADS], [[-DH, HEADS]], base=0, channel_multiplier=1, **exact).then_inc(S.iota_done, 1)
            pool.iota(sel.rearrange("p b (h e) -> p b h e", h=HEADS), [[HEADS, GB], [1, HEADS], [0, DH]],
                      base=0, channel_multiplier=-1, **exact).then_inc(S.iota_done, 1)
            pool.memset(apad[:, :, :], 0.0).then_inc(S.iota_done, 1)
            for t in range(2):
                pool.wait_ge(S.m_hi, t + 1)
                pool.tensor_tensor(Ml[:, t, :, :], Mf[:, t, :, :], Mh[:, t, :, :].bitcast(F32), ALU.subtract).then_inc(S.m_lo_first, 1)
            pool.wait_ge(S.ed_flat, 1)
            for t in range(ET):
                pool.indirect_dma_start(
                    picked[:, t:t + 1], None, adj.rearrange("n (m o) -> (n m) o", o=1),
                    bass.IndirectOffsetOnAxis(ap=flat[:, t:t + 1], axis=0)).then_inc(S.ed_picked, 16)

            def add_bias(g):
                for t in range(NT):
                    if t == 0:
                        pool.wait_ge(S.z_lo, g * (GB * NT) + GB * NT)
                    pool.tensor_tensor(xg(g, None, t), xg(g, None, t), TB[:, t:t + 1, :].to_broadcast([P, GB, D]),
                                       ALU.add).then_inc(S.tb_added, 1)

            def x0_norm(g, b):
                pool.wait_ge(S.x0_lo, g * GB + b)
                if b == 1:
                    pool.wait_ge(S.c_lo, g * NT)
                else:
                    last = g * GB + (0 if b == 2 else b - 1)
                    pool.wait_ge(S.v_mm, last * POW + 1)
                n = g * (GB * NT) + b * NT
                xb = xg(g, b)
                xo = xn(g, b).rearrange("p (t d) -> p t d", t=NT)
                pool.tensor_tensor(xo, xb, mean1[:, bass.ds(n, NT), None].to_broadcast([P, NT, D]), ALU.subtract).then_inc(S.x0_c, 1)
                pool.wait_ge(S.x0_c, n_made(g, b))
                pool.tensor_tensor(xo, xo, rstd1[:, bass.ds(n, NT), None].to_broadcast([P, NT, D]), ALU.mult).then_inc(S.x0_t, 1)

            def n_made(g, b):
                return g * GB + b - (GB + 1)

            def end_norm(h, t):
                if t == 2:
                    pool.wait_ge(end_ln[h], L2)
                if h:
                    pool.wait_ge(End.h_lo, t + 1)
                mean, rstd = [norm2[:, k, HALF * h:HALF * h + HALF].rearrange("p (b t) -> p b t", t=NT)[:, :, t:t + 1].to_broadcast([P, 2, D])
                              for k in range(2)]
                o = pairs(end_ht(t))
                pool.tensor_tensor(o, xh(h, t), mean, ALU.subtract).then_inc(End.h_c, 1)
                pool.wait_ge(End.h_c, 2 * h + t - 1)
                pool.tensor_tensor(o, o, rstd, ALU.mult).then_inc(End.h_p, 1)

            def body(g, last):
                x0_norm(g, 2)
                x0_norm(g, 3)
                if not last:
                    x0_norm(g + 1, 0)
                add_bias(g)
                if not last:
                    x0_norm(g + 1, 1)

            pool.wait_ge(S.tb_out, 1)
            add_bias(0)
            with pool.Fori(1, NG - 1) as g:
                body(g, False)
            body(NG - 1, True)
            for h in range(2):
                for t in (2, 3):
                    end_norm(h, t)

        @block.tensor
        def _(pe):
            def product(o, ah, al, bh, bl, start, stop):
                pe.matmul(o, ah, bh, start=start, stop=False)
                pe.matmul(o, ah, bl, start=False, stop=False)
                return pe.matmul(o, al, bh, start=False, stop=stop)

            def setup_features():
                pe.wait_ge(S.id_done, 1)
                pe.wait_ge(S.ld_w, 16)
                pe.transpose(PZ[0][:, 0:P], wraw[:, 0, :], ident[:, :]).then_inc(S.r_mm, 1)
                setup_transposes(0, 2)
                pe.wait_ge(S.r_sb, 2)
                pe.matmul(PZ[0][:, P:2 * P], wTd, wT, start=True, stop=True).then_inc(S.r_mm, 1)

            def setup_power(i):
                if i == 1:
                    pe.wait_ge(S.ld_stack, 32)
                    pe.wait_ge(S.r_sb, 3)
                else:
                    pe.wait_ge(S.st_sb, i - 1)
                pe.matmul(PZ[1][:, 0:2 * D + 1], R, stack[:, i - 1, :], start=True, stop=True).then_inc(S.st_mm, 1)

            def setup_transposes(t0, t1):
                for t in range(t0, t1):
                    pe.wait_ge(S.m_done, t + 1)
                    for c in range(NT):
                        mm = pe.transpose((PV + PA)[c][:, part(t)], Mf[:, t, c, :], ident[:, :])
                        if t == NT - 1:
                            mm.then_inc(S.mt_mm, 1)

            def setup_square(j, c0, c1):
                inh, inl = (M1h, M1l) if j == 2 else (M2h, M2l)
                for c in range(c0, c1):
                    if j == 3 and c == 3:
                        pe.wait_ge(S.v_lo, 2 * POW)
                    for t in range(NT):
                        if j == 2 and t % 2 == 0:
                            setup_power(2 * c + t // 2 + 1)
                        if c == 0:
                            if j == 2:
                                pe.wait_ge(S.m_lo_rest if t // 2 else S.m_lo_first, t % 2 + 1)
                            pe.wait_ge(S.mt_lo, NT * (j - 2) + t + 1)
                        mm = product((PL + PA)[c][:, :], Mh[:, t, c, :], Ml[:, t, c, :], inh[:, t, :], inl[:, t, :],
                                     t == 0, t == NT - 1)
                    mm.then_inc(S.mt_mm, 1)

            def setup_z():
                for i in range(BLOCKS):
                    if i == 0:
                        pe.wait_ge(S.zt_done, 1)
                        pe.wait_ge(S.w_lo, 1)
                    for j in range(POW):
                        mm = pe.transpose((PZ + PV)[i][:, part(j)], ztk(POW * i + j), ident[:, :])
                    mm.then_inc(S.zt_mm, 1)

            def setup_weights():
                pe.wait_ge(S.ld_l1, 48)
                for i in range(3):
                    mm = pe.transpose(PZ[0][:, part(i)], wraw[:, 1 + i, :], ident[:, :])
                mm.then_inc(S.w_mm3, 1)

            def setup_bias_first():
                pe.wait_ge(S.tb_step, 4)
                pe.wait_ge(S.mt_lo, 2 * NT)
                n = 0
                for j, parts in enumerate(([onesr[:, :]], [M1h, M1l], [M2h, M2l])):
                    for m in parts:
                        for t in range(NT if j else 1):
                            rhs = m[:, t, :] if j else onesr[:, :]
                            mm = pe.matmul(PL[0][0:4, :], rowsel[:, j, :], rhs, start=(n == 0), stop=(n == 4 * NT))
                            n += 1
                mm.then_inc(S.tb_mm, 1)
                pe.wait_ge(S.mt_lo, 3 * NT)
                pe.transpose(PL[1][0:Q * BLOCKS, 0:D], ccols, ident[:, :]).then_inc(S.tb_mm, 1)

            def setup_bias_columns(i):
                pe.wait_ge(S.u_sb, i + 2)
                rows = slice(Q * i, Q * i + 4)
                for t in range(NT):
                    mm = pe.transpose(PL[1][:, 4 * t:4 * t + 4], urow[rows, part(t)], ident[rows, rows])
                mm.then_inc(S.tb_mm, 1)

            def setup_bias_cube(i):
                pe.wait_ge(S.tb_lo, i)
                for m in range(NT):
                    mm = product(PL[0][0:Q * i + 4, :], Uh[:, m, 0:Q * i + 4], Ul[:, m, 0:Q * i + 4],
                                 M3h[:, m, :], M3l[:, m, :], m == 0, m == NT - 1)
                mm.then_inc(S.tb_mm, 1)

            def setup_bias_sum():
                pe.wait_ge(S.u_sb, BLOCKS + 1)
                for t in range(NT):
                    mm = pe.matmul(PL[0][:, part(t)], urow[:, part(t)], crow[:, :], start=True, stop=True)
                mm.then_inc(S.tb_mm, 1)

            def setup_edges():
                pe.wait_ge(S.ed_step, 5)
                pe.wait_ge(S.tb_out, 1)
                for s in range(2):
                    for t in range(ET):
                        mm = pe.matmul(PL[0][:, s * E:(s + 1) * E], ecolb[:, s, t, :], perm[:, t, :], start=(t == 0), stop=(t == ET - 1))
                for r in range(ET):
                    for t in range(ET):
                        mm = pe.matmul(PL[1][:, 2 * r:2 * r + 2], perm[:, t, part(r)], colf[:, t, :], start=(t == 0), stop=(t == ET - 1))
                mm.then_inc(S.ed_mm, 1)

            def setup_logs():
                pe.wait_ge(S.ed_log, 2)
                for t in range(ET):
                    mm = pe.matmul(PL[0][0:GH, part(t)], logb[:, t, :], ident[:, :], start=True, stop=True)
                mm.then_inc(S.lg_mm, 1)

            def powers(g, b, j0=0, j1=POW):
                n = g * GB + b
                xs = b % 2
                for j in range(j0, j1):
                    i = g * (GB * POW) + (b * POW + j)
                    o = VB[j]
                    if not (type(g) is int and g == 0 and b == 0):
                        pe.wait_ge(S.v_lo, i - 2)
                        if b == 0 and j == 2:
                            pe.wait_ge(S.a2_out, g * NT)
                    elif j == 2:
                        pe.wait_ge(S.mt_lo, 2 * NT)
                    if j < 2:
                        pe.wait_ge(S.x0_lo if j else S.x0_t, n + 1)
                    for t in range(NT):
                        if j == 0:
                            mm = pe.transpose(o[:, part(t)], xn(g, b)[:, part(t)], ident[:, :])
                        else:
                            mh, ml = (M1h, M1l) if j == 1 else (M2h, M2l)
                            mm = product(o[:, :], x0h[:, xs, t, :], x0l[:, xs, t, :], mh[:, t, :], ml[:, t, :],
                                         t == 0, t == NT - 1)
                    mm.then_inc(S.v_mm, 1)

            def blocks(g, b):
                for t in range(NT):
                    i = g * (GB * NT) + (b * NT + t)
                    if type(g) is int and g == 0 and b == 0 and t < 2:
                        pe.wait_ge(S.zk_lo, BLOCKS)
                    else:
                        pe.wait_ge(S.z_lo, i - 1)
                    o = PZ[t % 2][:, 0:BLOCKS * D]
                    for j in range(POW):
                        if t == 0:
                            pe.wait_ge(S.v_lo, g * (GB * POW) + (b * POW + j + 1))
                        mm = product(o, Vh[:, b % 2, j, part(t)], Vl[:, b % 2, j, part(t)], Zh[:, j, :], Zl[:, j, :],
                                     j == 0, j == POW - 1)
                    mm.then_inc(S.z_mm, 1)

            def cube(g, t, stage):
                if stage == 1:
                    if t == 0 and not (type(g) is int and g == 0):
                        pe.wait_ge(S.soft_step, (g - 1) * SOFT + 1)
                    if t >= 2:
                        pe.wait_ge(S.a1_sum, g * NT + (t - 1))
                    bh, bl = B2h, B2l
                else:
                    if t == 0:
                        pe.wait_ge(S.a1_sum, g * NT + NT - 1)
                    if t >= 2:
                        pe.wait_ge(S.a2_out, g * NT + (t - 1))
                    bh, bl = Ch, Cl
                for m in range(NT):
                    if t == 0 and stage == 1:
                        pe.wait_ge(S.z_lo, g * (GB * NT) + ((GB - 1) * NT + m + 1))
                    elif t == 0:
                        pe.wait_ge(S.c_lo, g * NT + (m + 1))
                    mm = product(PA[t % 2][:, :], M3h[:, m, part(t)], M3l[:, m, part(t)], bh[:, m, :], bl[:, m, :],
                                 m == 0, m == NT - 1)
                mm.then_inc(S.a1_mm if stage == 1 else S.a2_mm, 1)

            def gather(g, b, last=False):
                if last:
                    pe.wait_ge(End.x1, NT + b + 1)
                if b == 2 and not last:
                    pe.wait_ge(S.u_lr, g * 2 + 1)
                elif b == 3 and not last:
                    pe.wait_ge(S.q_cp, g * 2 + 1)
                o = gather_bank(b, last)
                for t in range(NT):
                    if last and b % 2 == 0:
                        pe.wait_ge(End.h_lo, NT * (b // 2) + t + 1)
                    elif b == 0:
                        pe.wait_ge(S.h_lo, g * NT + (t + 1))
                    pe.matmul(o, Ch[:, t, part(b)], gat[:, t, :], start=(t == 0), stop=False)
                    mm = pe.matmul(o, Cl[:, t, part(b)], gat[:, t, :], start=False, stop=(t == NT - 1))
                mm.then_inc(S.g_mm, 1)

            def project(g, p, last=False):
                if last:
                    pe.wait_ge(S.s_out, g * NT - 2 + 2 * p)
                pe.wait_ge(S.g_lo, g * GB + (2 * p + 2))
                gh, gl = gathered(p, last)
                ub, qb = project_banks(p, last)
                product(ub[:, :], linh[:, :], linl[:, :], gh[:, :, 0:E], gl[:, :, 0:E], True, True).then_inc(S.u_mm, 1)
                product(qb[:, :], valh[:, :], vall[:, :], gh[:, :, E:2 * E], gl[:, :, E:2 * E], True, True).then_inc(S.q_mm, 1)

            def scores(g, p, last=False):
                pe.wait_ge(S.u_lr, g * 2 + (p + 1))
                if p == 0 and not last:
                    pe.wait_ge(S.a2_out, g * NT + NT)
                for b in range(2 * p, 2 * p + 2):
                    mm = pe.matmul(PA[p if last else 0][0:GH, 0:E], apad[:, b, :], leaked(p, last)[:, (b % 2) * E:(b % 2 + 1) * E],
                                   start=(b == 0 or (last and b == 2)), stop=(b == GB - 1 or (last and b == 1)))
                mm.then_inc(S.e_mm, 1)

            def spread(g, p, last=False):
                if last or p == 0:
                    pe.wait_ge(S.attn_ready, g + 1 + p)
                if not last:
                    pe.wait_ge(S.z_lo, (g + 1) * (GB * NT) + (GB * NT - 1 + p))
                for b in range(2 * p, 2 * p + 2):
                    for i, m in enumerate(end_softmax(p)[3:] if last else (atth[:, :], attl[:, :])):
                        mm = pe.matmul(spread_bank(p, last)[:, (b % 2) * E:(b % 2 + 1) * E], selr[:, b, :], m,
                                       start=(i == 0), stop=(i == 1))
                mm.then_inc(S.bc_mm, 1)

            def project_out(g, p, last=False):
                pe.wait_ge(S.av_lo, g * 2 + (p + 1))
                if last or p == 0:
                    pe.wait_ge(S.u_lr, g * 2 + (p + 1 if last else 2))
                    pe.wait_ge(S.q_cp, g * 2 + (p + 1 if last else 2))
                vh, vl = weighted(p, last)
                for t in range(ET):
                    for b in range(2 * p, 2 * p + 2):
                        at = slice((b % 2) * E + t * P, (b % 2) * E + (t + 1) * P)
                        mm = product(project_banks(p, last)[t][:, part(b)], vh[:, at], vl[:, at],
                                     outh[:, :], outl[:, :], True, True)
                mm.then_inc(S.y_mm, 1)

            def scatter(g, t, spare):
                if t >= 2 and not spare:
                    pe.wait_ge(S.s_out, g * NT + (t - 1))
                if t == 1:
                    pe.wait_ge(S.y_lo, g * ET + 2)
                for r in range(ET):
                    if t == 0:
                        pe.wait_ge(S.y_lo, g * ET + (r + 1))
                    o = scatter_bank(t, spare)[:, :]
                    pe.matmul(o, scat[:, r, part(t)], Gh[:, r, :], start=(r == 0), stop=False)
                    mm = pe.matmul(o, scat[:, r, part(t)], Gl[:, r, :], start=False, stop=(r == ET - 1))
                mm.then_inc(S.s_mm, 1)

            def end_cube(h):
                for t in range(NT):
                    if h == 0 and t == 0:
                        pe.wait_ge(S.a1_sum, NG * NT - 1)
                        pe.wait_ge(S.v_lo, NG * GB * POW)
                    if h:
                        pe.wait_ge(End.x1, t + 1)
                    for m in range(NT):
                        if h == 0 and t == 0:
                            pe.wait_ge(S.c_lo, (NG - 1) * NT + m + 1)
                        mm = product(end_cube_bank(t)[:, 0:HW], M3h[:, m, part(t)], M3l[:, m, part(t)],
                                     Ch[:, m, half(h)], Cl[:, m, half(h)], m == 0, m == NT - 1)
                    mm.then_inc(End.a_mm, 1)

            def end_scatter(h, t0, t1):
                for t in range(t0, t1):
                    o = end_scatter_bank(h, t)[:, 0:HW]
                    if h and t < 2:
                        pe.wait_ge(End.s_out, t + 1)
                    for r in range(ET):
                        if t == 0 or (t == 2 and h == 0):
                            pe.wait_ge(End.y_lo, h * ET + r + 1)
                        pe.matmul(o, scat[:, r, part(t)], Gh[:, r, half(h)], start=(r == 0), stop=False)
                        mm = pe.matmul(o, scat[:, r, part(t)], Gl[:, r, half(h)], start=False, stop=(r == ET - 1))
                    mm.then_inc(End.s_mm, 1)

            def first_body():
                powers(0, 0)
                powers(0, 1)
                setup_square(3, 0, NT - 1)
                setup_z()
                setup_square(3, NT - 1, NT)
                blocks(0, 0)
                setup_bias_first()
                powers(0, 2, 0, 2)
                setup_bias_columns(0)
                powers(0, 2, 2, 3)
                setup_bias_cube(1)
                blocks(0, 1)
                setup_bias_columns(1)
                powers(0, 3, 0, 2)
                setup_bias_cube(2)
                powers(0, 3, 2, 3)
                setup_bias_sum()
                blocks(0, 2)
                setup_edges()
                blocks(0, 3)
                for stage in (1, 2):
                    for t in range(NT):
                        cube(0, t, stage)
                        if stage == 2 and t == 1:
                            setup_logs()

            def body(g, last):
                l = g - 1
                powers(g, 0)
                powers(g, 1)
                blocks(g, 0)
                powers(g, 2, 0, 2)
                gather(l, 0)
                gather(l, 1)
                powers(g, 2, 2, 3)
                project(l, 0)
                blocks(g, 1)
                scores(l, 0)
                gather(l, 2)
                gather(l, 3)
                powers(g, 3)
                project(l, 1)
                blocks(g, 2)
                scores(l, 1)
                blocks(g, 3)
                cube(g, 0, 1)
                cube(g, 1, 1)
                cube(g, 2, 1)
                spread(l, 0)
                spread(l, 1)
                cube(g, 3, 1)
                project_out(l, 0)
                project_out(l, 1)
                if last:
                    end_cube(0)
                    end_cube(1)
                for t in range(NT):
                    if not last:
                        cube(g, t, 2)
                        if t:
                            scatter(l, t - 1, False)
                for t in range(0 if last else NT - 1, NT):
                    scatter(l, t, last)

            setup_features()
            setup_transposes(2, NT)
            setup_square(2, 0, NT)
            setup_weights()
            first_body()
            with pe.Fori(1, NG - 1) as g:
                body(g, False)
            body(NG - 1, True)
            l = NG - 1
            for p in range(2):
                gather(l, 2 * p, True)
                gather(l, 2 * p + 1, True)
                project(l, p, True)
                scores(l, p, True)
            spread(l, 0, True)
            project_out(l, 0, True)
            spread(l, 1, True)
            end_scatter(0, 0, 3)
            project_out(l, 1, True)
            end_scatter(0, 3, NT)
            end_scatter(1, 0, NT)

        @block.scalar
        def _(act):
            def copy(o, i):
                return act.activation(o, i, ACT.Copy)

            def x0_round(g, b):
                n = g * GB + b
                act.wait_ge(S.x0_t, n + 1)
                if not (type(g) is int and g == 0 and b < 2):
                    act.wait_ge(S.v_mm, n * POW - POW)
                act.activation(x0h[:, b % 2, :, :].rearrange("p t d -> p (t d)"), xn(g, b), ACT.Relu).then_inc(S.x0_hi, 1)

            def powers(g, b, j0=0, j1=POW):
                n = g * GB + b
                for j in range(j0, j1):
                    act.wait_ge(S.v_mm, g * (GB * POW) + (b * POW + j + 1))
                    if j == 0 and not (type(g) is int and g == 0 and b < 2):
                        act.wait_ge(S.z_mm, n * NT - NT)
                    act.activation(Vh[:, b % 2, j, :], VB[j][:, :], ACT.Copy if j else ACT.Relu).then_inc(S.v_hi, 1)

            def blocks(g, b, t0=0, t1=NT):
                for t in range(t0, t1):
                    act.wait_ge(S.z_mm, g * (GB * NT) + (b * NT + t + 1))
                    if b == 0 and t == 0:
                        if type(g) is int and g == 0:
                            act.wait_ge(S.mt_mm, 3 * NT)
                            act.wait_ge(S.tb_step, 2)
                            act.wait_ge(S.zt_done, 1)
                        else:
                            act.wait_ge(S.c_lo, g * NT)
                            act.wait_ge(S.a1_mm, g * NT)
                    copy(B1[:, t, part(b)], PZ[t % 2][:, D:2 * D])
                    copy(B2h[:, t, part(b)], PZ[t % 2][:, 2 * D:3 * D]).then_inc(S.z_hi, 1)

            def middle(g, t):
                act.wait_ge(S.a1_sum, g * NT + (t + 1))
                if t == 0 and not (type(g) is int and g == 0):
                    act.wait_ge(S.g_mm, g * GB)
                copy(Ch[:, t, :], B1[:, t, :]).then_inc(S.c_hi, 1)

            def second_std(g):
                act.wait_ge(S.ln2_var, g + 1)
                act.activation(lnw[:, 4, :], lnw[:, 3, :], ACT.Sqrt).then_inc(S.ln2_std, 1)

            def second_round(g, t):
                act.wait_ge(S.h_t, g * NT + (t + 1))
                if t == 0:
                    act.wait_ge(S.a2_mm, g * NT + NT)
                act.activation(Ch[:, t, :], ht(t), ACT.Relu).then_inc(S.h_hi, 1)

            def gather(g, b, last=False):
                act.wait_ge(S.g_mm, g * GB + (b + 1))
                if b == 2 and not last:
                    act.wait_ge(S.q_mm, g * 2 + 1)
                copy(gathered(b // 2, last)[0][:, b % 2, :], gather_bank(b, last)).then_inc(S.g_hi, 1)

            def project(g, p, last=False):
                act.wait_ge(S.u_mm, g * 2 + (p + 1))
                ub, qb = project_banks(p, last)
                act.activation(sloped(p, last), ub[:, :], ACT.Copy, scale=SLOPE).then_inc(S.u_t, 1)
                act.wait_ge(S.q_mm, g * 2 + (p + 1))
                copy(vv[:, 2 * p:2 * p + 2, :].rearrange("p b e -> p (b e)"), qb[:, :]).then_inc(S.q_cp, 1)

            def exponent(g):
                act.wait_ge(S.e_shift, g + 1)
                act.activation(sm[2][:, :], sm[1][:, :], ACT.Exp).then_inc(S.e_exp, 1)

            def attention_round(g):
                act.wait_ge(S.att_full, g + 1)
                copy(atth[:, :], sm[1][:, :]).then_inc(S.att_hi, 1)

            def weigh(g, p, last=False):
                act.wait_ge(S.av_f, g * 2 + (p + 1))
                copy(weighted(p, last)[0],
                     vv[:, 2 * p:2 * p + 2, :].rearrange("p b e -> p (b e)")).then_inc(S.av_hi, 1)

            def edge_out(g, t):
                if t == 0:
                    act.wait_ge(S.y_mm, g * 2 + 2)
                copy(Gh[:, t, :], PL[t][:, :]).then_inc(S.y_hi, 1)

            def end_round(h, t):
                act.wait_ge(End.h_p if t >= 2 else End.h_t, 2 * h + t % 2 + 1)
                act.activation(Ch[:, t, half(h)], end_ht(t), ACT.Relu).then_inc(End.h_hi, 1)

            def end_sqrt(h):
                act.wait_ge(end_var[h], 1)
                act.activation(lnw[:, 4, HALF * h:HALF * h + HALF], lnw[:, 3, HALF * h:HALF * h + HALF], ACT.Sqrt).then_inc(end_std[h], 1)

            def end_exponent(h):
                _, shifted, raised, _, _ = end_softmax(h)
                act.wait_ge(end_shift[h], 1)
                act.activation(raised, shifted, ACT.Exp).then_inc(end_exp[h], 1)

            def end_attention(h):
                _, full, _, hi_, _ = end_softmax(h)
                act.wait_ge(end_full[h], 1)
                copy(hi_, full).then_inc(S.att_hi, 1)

            def end_edges(h):
                for t in range(ET):
                    if t == 0:
                        act.wait_ge(S.y_mm, (NG - 1) * 2 + h + 1)
                    copy(Gh[:, t, half(h)], project_banks(h, True)[t][:, half(h)]).then_inc(End.y_hi, 1)

            def setup():
                act.dma_start(small[:, 0:NT], alpha.rearrange("(p t) -> p t", t=NT)).then_inc(S.ld_alpha, 16)
                act.dma_start(wraw[:, 0, :], w).then_inc(S.ld_w, 16)
                act.dma_start(small[:, 4:5], d.rearrange("(p o) -> p o", o=1)).then_inc(S.ld_cols, 16)
                act.dma_start(stack[:, 0, 0:D], fc_w).then_inc(S.ld_stack, 16)
                act.dma_start(stack[:, 0, 2 * D:2 * D + 1], fc_b.rearrange("(p o) -> p o", o=1)).then_inc(S.ld_stack, 16)
                act.wait_ge(S.ld_alpha, 16)
                act.activation(small[:, 16:16 + NT], small[:, 0:NT], ACT.Sigmoid).then_inc(S.sig_done, 1)
                for t in range(NT):
                    act.wait_ge(S.m_done, t + 1)
                    copy(Mh[:, t, :, :], Mf[:, t, :, :]).then_inc(S.m_hi, 1)
                for c in range(NT):
                    act.wait_ge(S.mt_mm, c + 1)
                    copy(M1h[:, c, :], (PV + PA)[c][:, :]).then_inc(S.mt_hi, 1)
                    if c == 1:
                        stack_copy(1)
                stack_copy(2)
                square_copy(2, 0)
                stack_copy(3)
                stack_copy(4)
                first_std(0)
                square_copy(2, 1)
                stack_copy(5)
                stack_copy(6)
                square_copy(2, 2)
                x0_round(0, 0)
                stack_copy(7)
                stack_copy(8)
                square_copy(2, 3)
                x0_round(0, 1)
                act.wait_ge(S.w_mm3, 1)
                for i, m3 in enumerate((linh, valh, outh)):
                    copy(m3[:, :], PZ[0][:, part(i)]).then_inc(S.w_hi, 1)

            def stack_copy(i):
                act.wait_ge(S.st_mm, i)
                copy(stack[:, i, :], PZ[1][:, 0:2 * D + 1]).then_inc(S.st_sb, 1)

            def square_copy(j, c):
                act.wait_ge(S.mt_mm, NT * (j - 1) + c + 1)
                copy((M2h if j == 2 else M3h)[:, c, :], (PL + PA)[c][:, :]).then_inc(S.mt_hi, 1)

            def first_std(g):
                act.wait_ge(S.ln1_var, g + 1)
                act.activation(lnw[:, 4, :], lnw[:, 3, :], ACT.Sqrt).then_inc(S.ln1_std, 1)

            def setup_z():
                for i in range(BLOCKS):
                    act.wait_ge(S.zt_mm, i + 1)
                    copy(Zh[:, :, part(i)], (PZ + PV)[i][:, 0:POW * D].rearrange("p (j d) -> p j d", j=POW)).then_inc(S.zk_hi, 1)

            def setup_bias_rows(i):
                act.wait_ge(S.tb_mm, 1 + 2 * i + (i > 0))
                rows = slice(Q * i, Q * i + 4)
                copy(urow[rows, :], PL[0][rows, :]).then_inc(S.u_sb, 1)
                if i == 0:
                    act.wait_ge(S.tb_mm, 2)
                    copy(crow[:, :], PL[1][0:Q * BLOCKS, 0:D]).then_inc(S.u_sb, 1)

            def setup_bias_columns(i):
                act.wait_ge(S.tb_mm, 3 + 2 * i)
                copy(Uh[:, :, Q * (i + 1):Q * (i + 1) + 4], PL[1][:, 0:4 * NT].rearrange("p (t j) -> p t j", t=NT)).then_inc(S.tb_hi, 1)

            def setup_bias_sum():
                act.wait_ge(S.tb_mm, 2 * BLOCKS + 1)
                copy(TB[:, :, :], PL[0][:, :].rearrange("p (t d) -> p t d", t=NT)).then_inc(S.tb_out, 1)

            def setup_logs():
                act.wait_ge(S.ed_log, 1)
                act.activation(picked[:, :], picked[:, :], ACT.Ln).then_inc(S.ed_pick, 1)

            def first_body():
                powers(0, 0)
                powers(0, 1)
                for c in range(NT - 1):
                    square_copy(3, c)
                x0_round(0, 2)
                setup_z()
                square_copy(3, NT - 1)
                for t in range(NT):
                    blocks(0, 0, t, t + 1)
                setup_bias_rows(0)
                first_std(1)
                powers(0, 2, 0, 2)
                setup_bias_columns(0)
                powers(0, 2, 2, 3)
                x0_round(0, 3)
                setup_bias_rows(1)
                blocks(0, 1)
                setup_bias_columns(1)
                first_std(2)
                powers(0, 3, 0, 2)
                setup_bias_rows(2)
                powers(0, 3, 2, 3)
                setup_bias_sum()
                x0_round(1, 0)
                blocks(0, 2)
                first_std(3)
                blocks(0, 3)
                for t in range(NT):
                    middle(0, t)
                setup_logs()
                x0_round(1, 1)
                second_std(0)

            def body(g, last):
                l = g - 1
                powers(g, 0, 0, 2)
                second_round(l, 0)
                powers(g, 0, 2, 3)
                second_round(l, 1)
                powers(g, 1, 0, 1)
                x0_round(g, 2)
                powers(g, 1, 1, 3)
                blocks(g, 0, 0, 2)
                second_round(l, 2)
                blocks(g, 0, 2, 4)
                second_round(l, 3)
                powers(g, 2, 0, 2)
                gather(l, 0)
                x0_round(g, 3)
                gather(l, 1)
                powers(g, 2, 2, 3)
                project(l, 0)
                blocks(g, 1)
                gather(l, 2)
                gather(l, 3)
                powers(g, 3)
                project(l, 1)
                blocks(g, 2)
                if not last:
                    x0_round(g + 1, 0)
                blocks(g, 3, 0, 1)
                exponent(l)
                blocks(g, 3, 1, 4)
                middle(g, 0)
                attention_round(l)
                middle(g, 1)
                middle(g, 2)
                weigh(l, 0)
                weigh(l, 1)
                middle(g, 3)
                if not last:
                    x0_round(g + 1, 1)
                for t in range(ET):
                    edge_out(l, t)
                if not last:
                    second_std(g)

            setup()
            first_body()
            with act.Fori(1, NG - 1) as g:
                body(g, False)
            body(NG - 1, True)
            l = NG - 1
            end_sqrt(0)
            for t in range(NT):
                end_round(0, t)
            gather(l, 0, True)
            end_sqrt(1)
            gather(l, 1, True)
            end_round(1, 0)
            end_round(1, 1)
            project(l, 0, True)
            end_round(1, 2)
            end_round(1, 3)
            gather(l, 2, True)
            end_exponent(0)
            gather(l, 3, True)
            project(l, 1, True)
            end_attention(0)
            end_exponent(1)
            weigh(l, 0, True)
            end_attention(1)
            end_edges(0)
            weigh(l, 1, True)
            end_edges(1)

        @block.vector
        def _(dve):
            def tt(o, x_, y_, op):
                return dve.tensor_tensor(o, x_, y_, op)

            def ts(o, x_, s1, s2, op0, op1=None):
                return dve.tensor_scalar(o, x_, s1, s2, op0, op1) if op1 is not None else dve.tensor_scalar(o, x_, s1, s2, op0)

            def stt(o, x_, s, y_, op0, op1):
                return dve.scalar_tensor_tensor(out=o, in0=x_, scalar=s, in1=y_, op0=op0, op1=op1)

            def low(o, v, hi):
                return tt(o, v, hi.bitcast(F32), ALU.subtract)

            def norm_mean(count, step, var, mean_out, cols=slice(0, GB * NT)):
                st = stats[:, cols, :]
                me, ve, mo, vo = st[:, :, 1], st[:, :, 2], st[:, :, 4], st[:, :, 5]
                tt(lnw[:, 0, cols], me, mo, ALU.add)
                tt(lnw[:, 1, cols], me, mo, ALU.subtract)
                tt(lnw[:, 2, cols], ve, vo, ALU.add).then_inc(step, 1)
                dve.wait_ge(step, count + 1)
                tt(lnw[:, 1, cols], lnw[:, 1, cols], lnw[:, 1, cols], ALU.mult)
                ts(mean_out, lnw[:, 0, cols], 0.5, None, ALU.mult).then_inc(step, 1)
                dve.wait_ge(step, count + 2)
                stt(lnw[:, 2, cols], lnw[:, 1, cols], D / 4.0, lnw[:, 2, cols], ALU.mult, ALU.add).then_inc(step, 1)
                dve.wait_ge(step, count + 3)
                ts(lnw[:, 3, cols], lnw[:, 2, cols], 1.0 / D, LN_EPS, ALU.mult, ALU.add).then_inc(var, 1)

            def norm_rstd(g, count, step, std, rstd_out, cols=slice(0, GB * NT)):
                dve.wait_ge(std, g + 1)
                dve.reciprocal(lnw[:, 5, cols], lnw[:, 4, cols]).then_inc(step, 1)
                dve.wait_ge(step, count + 4)
                tt(lnw[:, 0, cols], lnw[:, 5, cols], lnw[:, 5, cols], ALU.mult).then_inc(step, 1)
                dve.wait_ge(step, count + 5)
                tt(lnw[:, 0, cols], lnw[:, 0, cols], lnw[:, 3, cols], ALU.mult).then_inc(step, 1)
                dve.wait_ge(step, count + 6)
                ts(lnw[:, 0, cols], lnw[:, 0, cols], -0.5, 1.5, ALU.mult, ALU.add).then_inc(step, 1)
                dve.wait_ge(step, count + 7)
                tt(rstd_out, lnw[:, 5, cols], lnw[:, 0, cols], ALU.mult).then_inc(step, 1)
                dve.wait_ge(step, count + NORM_STEPS)

            def first_stats(g, b):
                if b == 0:
                    dve.wait_ge(x_loaded[g], 16)
                for t in range(NT):
                    mm = dve.bn_stats(stats[:, b * NT + t, :], X[:, g, b, t, :])
                if b == GB - 1:
                    mm.then_inc(S.ln1_done, 1)

            def first_mean(g):
                dve.wait_ge(S.ln1_done, g + 1)
                n = GB * NT
                norm_mean(g * NORM_STEPS, S.ln1_step, S.ln1_var, mean1[:, g * n:(g + 1) * n])

            def first_rstd(g):
                n = GB * NT
                norm_rstd(g, g * NORM_STEPS, S.ln1_step, S.ln1_std, rstd1[:, g * n:(g + 1) * n])

            def x0_norm(g, b):
                n = g * GB + b
                if not (type(g) is int and n == 0):
                    dve.wait_ge(S.x0_lo, n)
                if b == 1 and g:
                    dve.wait_ge(S.c_lo, g * NT)
                elif b != 1 and n:
                    dve.wait_ge(S.v_mm, (n - (2 if b == 2 else 1)) * POW + 1)
                for t in range(NT):
                    n = g * (GB * NT) + (b * NT + t)
                    mm = ts(xn(g, b)[:, part(t)], xg(g, b, t), mean1[:, bass.ds(n, 1)], rstd1[:, bass.ds(n, 1)],
                            ALU.subtract, ALU.mult)
                mm.then_inc(S.x0_t, 1)

            def x0_low(g, b):
                dve.wait_ge(S.x0_hi, g * GB + (b + 1))
                stt(x0l[:, b % 2, :, :].rearrange("p t d -> p (t d)"), xn(g, b), 0.0,
                    x0h[:, b % 2, :, :].rearrange("p t d -> p (t d)").bitcast(F32), ALU.max, ALU.subtract).then_inc(S.x0_lo, 1)

            def powers(g, b, j0=0, j1=POW):
                for j in range(j0, j1):
                    dve.wait_ge(S.v_hi, g * (GB * POW) + (b * POW + j + 1))
                    if j == 0:
                        mm = stt(Vl[:, b % 2, 0, :], VB[0][:, :], 0.0, Vh[:, b % 2, 0, :].bitcast(F32), ALU.max, ALU.subtract)
                    else:
                        mm = low(Vl[:, b % 2, j, :], VB[j][:, :], Vh[:, b % 2, j, :])
                    mm.then_inc(S.v_lo, 1)

            def blocks(g, b, t0=0, t1=NT):
                for t in range(t0, t1):
                    dve.wait_ge(S.z_hi, g * (GB * NT) + (b * NT + t + 1))
                    tt(xg(g, b, t), PZ[t % 2][:, 0:D], xg(g, b, t), ALU.add)
                    low(B2l[:, t, part(b)], PZ[t % 2][:, 2 * D:3 * D], B2h[:, t, part(b)]).then_inc(S.z_lo, 1)

            def middle_sum(g, t):
                dve.wait_ge(S.a1_mm, g * NT + (t + 1))
                tt(B1[:, t, :], PA[t % 2][:, :], B1[:, t, :], ALU.add).then_inc(S.a1_sum, 1)

            def middle_low(g, t):
                dve.wait_ge(S.c_hi, g * NT + (t + 1))
                low(Cl[:, t, :], B1[:, t, :], Ch[:, t, :]).then_inc(S.c_lo, 1)

            def first_layer(g, t):
                dve.wait_ge(S.tb_added, g * NT + (t + 1))
                dve.wait_ge(S.a2_mm, g * NT + (t + 1))
                tt(xg(g, None, t), PA[t % 2][:, :].rearrange("p (b d) -> p b d", b=GB), xg(g, None, t), ALU.add).then_inc(S.a2_out, 1)
                dve.wait_ge(S.a2_out, g * NT + (t + 1))
                dve.memset(carrier[:, :], 0.0)
                for b in range(GB):
                    mm = dve.bn_stats(stats[:, b * NT + t, :], xg(g, b, t))
                mm.then_inc(S.ln2_step, 1)

            def second_mean(g):
                dve.wait_ge(S.ln2_step, g * L2 + NT)
                norm_mean(g * L2 + NT, S.ln2_step, S.ln2_var, norm2[:, 0, :])

            def second_rstd(g):
                norm_rstd(g, g * L2 + NT, S.ln2_step, S.ln2_std, norm2[:, 1, :])

            def second_norm(g, t):
                if t >= 2:
                    dve.wait_ge(S.h_lo, g * NT + (t - 1))
                for b in range(GB):
                    n = b * NT + t
                    mm = ts(ht(t)[:, part(b)], xg(g, b, t), norm2[:, 0, n:n + 1], norm2[:, 1, n:n + 1],
                            ALU.subtract, ALU.mult)
                mm.then_inc(S.h_t, 1)

            def second_low(g, t):
                dve.wait_ge(S.h_hi, g * NT + (t + 1))
                stt(Cl[:, t, :], ht(t), 0.0, Ch[:, t, :].bitcast(F32), ALU.max, ALU.subtract).then_inc(S.h_lo, 1)

            def gather(g, b, last=False):
                dve.wait_ge(S.g_hi, g * GB + (b + 1))
                gh, gl = gathered(b // 2, last)
                low(gl[:, b % 2, :], gather_bank(b, last), gh[:, b % 2, :]).then_inc(S.g_lo, 1)

            def leaky(g, p, last=False):
                dve.wait_ge(S.u_t, g * 2 + (p + 1))
                tt(leaked(p, last), project_banks(p, last)[0][:, :], sloped(p, last), ALU.max).then_inc(S.u_lr, 1)

            def scan(o, mask, v, first, op0, op1):
                return dve.tensor_tensor_scan(o, mask, v, first, op0, op1)

            def softmax_max(g):
                dve.wait_ge(S.e_mm, g * 2 + 2)
                tt(sm[0][:, :], PA[0][0:GH, 0:E], lgrow[:, :], ALU.add).then_inc(S.soft_step, 1)
                dve.wait_ge(S.soft_step, g * SOFT + 1)
                scan(sm[1][:, :], far[:, 0:E], sm[0][:, :], LEAST, ALU.add, ALU.max).then_inc(S.soft_step, 1)

            def softmax_shift(g):
                dve.wait_ge(S.soft_step, g * SOFT + 2)
                scan(sm[2][:, ::-1], far[:, 1:E + 1][:, ::-1], sm[1][:, ::-1], LEAST, ALU.add, ALU.max).then_inc(S.soft_step, 1)
                dve.wait_ge(S.soft_step, g * SOFT + 3)
                tt(sm[1][:, :], sm[0][:, :], sm[2][:, :], ALU.subtract).then_inc(S.e_shift, 1)

            def softmax_sum(g, step):
                if step == 0:
                    dve.wait_ge(S.e_exp, g + 1)
                    scan(sm[0][:, :], same[:, 0:E], sm[2][:, :], 0.0, ALU.mult, ALU.add).then_inc(S.soft_step, 1)
                else:
                    dve.wait_ge(S.soft_step, g * SOFT + 4)
                    scan(sm[1][:, ::-1], same[:, 1:E + 1][:, ::-1], sm[0][:, ::-1], 0.0, ALU.mult, ALU.max).then_inc(S.soft_step, 1)

            def softmax_divide(g, half):
                dve.wait_ge(S.soft_step, g * SOFT + 5 + half)
                dve.reciprocal(sm[0][:, half * P:(half + 1) * P], sm[1][:, half * P:(half + 1) * P]).then_inc(S.soft_step, 1)
                if half:
                    dve.wait_ge(S.soft_step, g * SOFT + 7)
                    tt(sm[1][:, :], sm[2][:, :], sm[0][:, :], ALU.mult).then_inc(S.att_full, 1)

            def attention_low(g):
                dve.wait_ge(S.att_hi, g + 1)
                low(attl[:, :], sm[1][:, :], atth[:, :]).then_inc(S.attn_ready, 1)

            def weigh(g, p, last=False):
                dve.wait_ge(S.bc_mm, g * 2 + (p + 1))
                v = vv[:, 2 * p:2 * p + 2, :].rearrange("p b e -> p (b e)")
                tt(v, spread_bank(p, last)[:, :], v, ALU.mult).then_inc(S.av_f, 1)

            def weigh_low(g, p, last=False):
                dve.wait_ge(S.av_hi, g * 2 + (p + 1))
                hi_, lo_ = weighted(p, last)
                low(lo_, vv[:, 2 * p:2 * p + 2, :].rearrange("p b e -> p (b e)"), hi_).then_inc(S.av_lo, 1)

            def edge_out(g, t):
                dve.wait_ge(S.y_hi, g * ET + (t + 1))
                low(Gl[:, t, :], PL[t][:, :], Gh[:, t, :]).then_inc(S.y_lo, 1)

            def second_layer(g, t, spare=False):
                dve.wait_ge(S.s_mm, g * NT + (t + 1))
                tt(xg(g, None, t), scatter_bank(t, spare)[:, :].rearrange("p (b d) -> p b d", b=GB), xg(g, None, t), ALU.add).then_inc(S.s_out, 1)

            def end_first(h, t):
                if h == 0:
                    dve.wait_ge(S.tb_added, (NG - 1) * NT + t + 1)
                dve.wait_ge(End.a_mm, h * NT + t + 1)
                tt(xh(h, t), pairs(end_cube_bank(t)[:, 0:HW]), xh(h, t), ALU.add).then_inc(End.x1, 1)
                dve.wait_ge(End.x1, h * NT + t + 1)
                for b in range(2 * h, 2 * h + 2):
                    mm = dve.bn_stats(stats[:, b * NT + t, :], X[:, NG - 1, b, t, :])
                mm.then_inc(end_ln[h], 1)

            def end_mean(h):
                dve.wait_ge(end_ln[h], NT)
                norm_mean(NT, end_ln[h], end_var[h], norm2[:, 0, HALF * h:HALF * h + HALF], slice(HALF * h, HALF * h + HALF))

            def end_rstd(h):
                norm_rstd(0, NT, end_ln[h], end_std[h], norm2[:, 1, HALF * h:HALF * h + HALF], slice(HALF * h, HALF * h + HALF))

            def end_norm(h, t):
                if h:
                    dve.wait_ge(End.h_lo, t + 1)
                for i in range(2):
                    n = (2 * h + i) * NT + t
                    mm = ts(end_ht(t)[:, part(i)], X[:, NG - 1, 2 * h + i, t, :], norm2[:, 0, n:n + 1], norm2[:, 1, n:n + 1],
                            ALU.subtract, ALU.mult)
                mm.then_inc(End.h_t, 1)

            def end_low(h, t):
                dve.wait_ge(End.h_hi, h * NT + t + 1)
                stt(Cl[:, t, half(h)], end_ht(t), 0.0, Ch[:, t, half(h)].bitcast(F32), ALU.max, ALU.subtract).then_inc(End.h_lo, 1)

            def end_soft(h, step):
                r0, r1, r2, hi_, lo_ = end_softmax(h)
                done = end_steps[h]
                if step == 0:
                    dve.wait_ge(S.e_mm, (NG - 1) * 2 + h + 1)
                    tt(r0, PA[h][0:GH, 0:E], lgrow[:, :], ALU.add).then_inc(done, 1)
                elif step == 1:
                    dve.wait_ge(done, 1)
                    scan(r1, far[:, 0:E], r0, LEAST, ALU.add, ALU.max).then_inc(done, 1)
                elif step == 2:
                    dve.wait_ge(done, 2)
                    scan(r2[:, ::-1], far[:, 1:E + 1][:, ::-1], r1[:, ::-1], LEAST, ALU.add, ALU.max).then_inc(done, 1)
                elif step == 3:
                    dve.wait_ge(done, 3)
                    tt(r1, r0, r2, ALU.subtract).then_inc(end_shift[h], 1)
                elif step == 4:
                    dve.wait_ge(end_exp[h], 1)
                    scan(r0, same[:, 0:E], r2, 0.0, ALU.mult, ALU.add).then_inc(done, 1)
                elif step == 5:
                    dve.wait_ge(done, 4)
                    scan(r1[:, ::-1], same[:, 1:E + 1][:, ::-1], r0[:, ::-1], 0.0, ALU.mult, ALU.max).then_inc(done, 1)
                elif step == 6:
                    dve.wait_ge(done, 5)
                    dve.reciprocal(r0, r1).then_inc(done, 1)
                elif step == 7:
                    dve.wait_ge(done, 6)
                    tt(r1, r2, r0, ALU.mult).then_inc(end_full[h], 1)
                else:
                    dve.wait_ge(S.att_hi, NG - 1 + h + 1)
                    low(lo_, r1, hi_).then_inc(S.attn_ready, 1)

            def end_edges(h):
                for t in range(ET):
                    dve.wait_ge(End.y_hi, h * ET + t + 1)
                    low(Gl[:, t, half(h)], project_banks(h, True)[t][:, half(h)], Gh[:, t, half(h)]).then_inc(End.y_lo, 1)

            def end_second(h, t):
                dve.wait_ge(End.s_mm, h * NT + t + 1)
                tt(xh(h, t), pairs(end_scatter_bank(h, t)[:, 0:HW]), xh(h, t), ALU.add).then_inc(End.s_out, 1)

            def setup():
                dve.wait_ge(S.iota_done, 1)
                ts(ident[:, :], idgrid, 0.0, None, ALU.is_equal).then_inc(S.id_done, 1)
                ts(stack[:, 0, D:2 * D], idgrid, 0.0, None, ALU.is_equal).then_inc(S.r_sb, 1)

                dve.wait_ge(S.sig_done, 1)
                ts(scol_col[:, :], small[:, 16:16 + NT], DT / 2, None, ALU.mult)
                ts(ccol[:, :], small[:, 16:16 + NT], -DT / 2, 1.0 - DT, ALU.mult, ALU.add).then_inc(S.m_step, 1)
                for t in range(NT):
                    if t == 2:
                        dve.wait_ge(S.r_mm, 1)
                        dve.wait_ge(S.z_step, 1)
                        ts(wTd, PZ[0][:, 0:P], small[:, 20:21], DT, ALU.mult, ALU.mult)
                        dve.tensor_copy(wT, PZ[0][:, 0:P]).then_inc(S.r_sb, 1)
                    if t == 0:
                        dve.wait_ge(S.m_step, 1)
                    dve.wait_ge(ld_adj[t // 2], 16)
                    ts(Mf[:, t, :, :], A[:, t, :].rearrange("p (q c) -> p c q", c=NT), scol_col[:, t:t + 1], None, ALU.mult).then_inc(S.m_step, 1)
                    if t == 0:
                        dve.wait_ge(S.ld_cols, 16)
                        ts(small[:, 20:21], small[:, 4:5], 0.0, 1.0, ALU.max, ALU.min).then_inc(S.z_step, 1)
                    if t % 2:
                        for u in (t - 1, t):
                            dve.wait_ge(S.m_step, 2 + u)
                            stt(Mf[:, u, u, :], ident[:, :], ccol[:, u:u + 1], Mf[:, u, u, :], ALU.mult, ALU.add).then_inc(S.m_done, 1)
                dve.wait_ge(S.r_mm, 2)
                dve.tensor_copy(R, PZ[0][:, P:2 * P]).then_inc(S.r_sb, 1)
                for t in (2, 3):
                    dve.wait_ge(S.m_hi, t + 1)
                    low(Ml[:, t, :, :], Mf[:, t, :, :], Mh[:, t, :, :]).then_inc(S.m_lo_rest, 1)
                for c in range(NT):
                    dve.wait_ge(S.mt_hi, c + 1)
                    low(M1l[:, c, :], (PV + PA)[c][:, :], M1h[:, c, :]).then_inc(S.mt_lo, 1)
                dve.wait_ge(S.iota_done, 8)
                ts(selr[:, :, :], sel, 0.0, None, ALU.is_equal).then_inc(S.vv_free, 1)
                first_stats(0, 0)
                first_stats(0, 1)
                square_low(2, 0)
                first_stats(0, 2)
                first_stats(0, 3)
                first_mean(0)
                first_rstd(0)
                square_low(2, 1)
                x0_norm(0, 0)
                square_low(2, 2)
                x0_low(0, 0)
                x0_norm(0, 1)
                square_low(2, 3)
                x0_low(0, 1)
                dve.wait_ge(S.w_hi, 3)
                for i, (lo_, hi_) in enumerate(((linl, linh), (vall, valh), (outl, outh))):
                    mm = low(lo_[:, :], PZ[0][:, part(i)], hi_[:, :])
                mm.then_inc(S.w_lo, 1)

            def square_low(j, c):
                dve.wait_ge(S.mt_hi, (j - 1) * NT + c + 1)
                lo_, hi_ = (M2l, M2h) if j == 2 else (M3l, M3h)
                low(lo_[:, c, :], (PL + PA)[c][:, :], hi_[:, c, :]).then_inc(S.mt_lo, 1)

            def setup_zt(i):
                if i < 0:
                    dve.wait_ge(S.st_sb, STEPS)
                    dve.wait_ge(S.vv_free, 1)
                    for k in range(STEPS + 1):
                        last = ts(ztk(k), stack[:, STEPS - k, 0:D], float(comb(STEPS, k)), None, ALU.mult)
                else:
                    dve.wait_ge(S.z_step, i + 2)
                    for k in range(STEPS - i):
                        last = stt(ztk(k), stack[:, i, D:2 * D], DT * comb(i + k, k), ztk(k), ALU.mult, ALU.add)
                last.then_inc(S.z_step if i < STEPS - 1 else S.zt_done, 1)

            def setup_ccols():
                dve.memset(ccols, 0.0).then_inc(S.tb_step, 1)
                dve.wait_ge(S.tb_step, 1)
                for k in range(STEPS + 1):
                    n = Q * (k // POW) + k % POW
                    mm = ts(ccols[:, n:n + 1], stack[:, STEPS - k, 2 * D:2 * D + 1], float(comb(STEPS, k)), None, ALU.mult)
                mm.then_inc(S.tb_step, 1)

            def setup_z():
                for i in range(BLOCKS):
                    dve.wait_ge(S.zk_hi, i + 1)
                    low(Zl[:, :, part(i)], (PZ + PV)[i][:, 0:POW * D].rearrange("p (j d) -> p j d", j=POW), Zh[:, :, part(i)]).then_inc(S.zk_lo, 1)

            def setup_ones():
                dve.wait_ge(S.tb_step, 2)
                dve.memset(onesr[:, :].bitcast(F32), 1.0)
                dve.memset(urow[:, :], 0.0)
                dve.memset(Uh[:, :, :].bitcast(F32), 0.0)
                dve.memset(Ul[:, :, :].bitcast(F32), 0.0)
                dve.memset(rowsel[:, :, :].bitcast(F32), 0.0).then_inc(S.tb_step, 1)
                for j in range(POW):
                    if j == 0:
                        dve.wait_ge(S.tb_step, 3)
                    mm = dve.memset(rowsel[:, j, j:j + 1].bitcast(F32), 1.0 if j else 1.0 / P)
                mm.then_inc(S.tb_step, 1)

            def setup_bias_low(i):
                dve.wait_ge(S.tb_hi, i + 1)
                cols = slice(Q * (i + 1), Q * (i + 1) + 4)
                low(Ul[:, :, cols], PL[1][:, 0:4 * NT].rearrange("p (t j) -> p t j", t=NT), Uh[:, :, cols]).then_inc(S.tb_lo, 1)

            def setup_edges_rank(step):
                if step == 0:
                    dve.wait_ge(S.ld_idx, 64)
                    dve.tensor_copy(rowf[:, :], irow[:, 0, :])
                    dve.tensor_copy(colf, icol.rearrange("p s t -> p t s")).then_inc(S.ed_step, 1)
                    dve.wait_ge(S.ed_step, 1)
                    stt(keyrow[:, :], rowf[:, :], float(E), egrid, ALU.mult, ALU.add)
                    stt(keycol, colf[:, :, 0], float(E), small[:, 8:8 + ET], ALU.mult, ALU.add).then_inc(S.ed_step, 1)
                elif step == 1:
                    dve.wait_ge(S.ed_step, 2)
                    for t in range(ET):
                        mm = ts(perm[:, t, :], keyrow[:, :], keycol[:, t:t + 1], None, ALU.is_lt)
                    mm.then_inc(S.ed_step, 1)
                elif step == 2:
                    dve.wait_ge(S.ed_step, 3)
                    for t in range(ET):
                        mm = dve.tensor_reduce(rank[:, t:t + 1], perm[:, t, :], AX_X, ALU.add)
                    mm.then_inc(S.ed_step, 1)
                else:
                    dve.wait_ge(S.ed_step, 4)
                    for t in range(ET):
                        ts(perm[:, t, :], egrid, rank[:, t:t + 1], None, ALU.is_equal)
                    for s in range(2):
                        for t in range(ET):
                            mm = ts(ecolb[:, s, t, :], ident[:, :], 0.0, colf[:, t, s:s + 1], ALU.mult, ALU.add)
                    mm.then_inc(S.ed_step, 1)

            def setup_edges(step):
                if step == 0:
                    dve.wait_ge(S.ed_mm, 1)
                    dve.tensor_copy(nrow[:, :, :].rearrange("p s e -> p (s e)"), PL[0][:, :])
                    dve.tensor_copy(ncol, PL[1][:, 0:2 * ET].rearrange("p (t s) -> p t s", s=2)).then_inc(S.ed_sb, 1)
                    dve.wait_ge(S.ed_sb, 1)
                    stt(flat, ncol[:, :, 0], float(N), ncol[:, :, 1], ALU.mult, ALU.add).then_inc(S.ed_flat, 1)
                elif step == 1:
                    tt(same[:, 1:E], nrow[0:GH, 0, 1:E], nrow[0:GH, 0, 0:E - 1], ALU.is_equal)
                    dve.memset(same[:, 0:1], 0.0)
                    dve.memset(same[:, E:E + 1], 0.0).then_inc(S.ed_sb, 1)
                    dve.wait_ge(S.ed_sb, 2)
                    ts(far[:, :], same[:, :], -FAR, FAR, ALU.mult, ALU.add)
                elif step == 2:
                    for t in range(NT):
                        mm = ts(gat[:, t, E:2 * E], nrow[:, 1, :], nodecol[:, t:t + 1], None, ALU.is_equal)
                    mm.then_inc(S.ed_sb, 1)
                elif step == 3:
                    dve.wait_ge(S.ed_sb, 3)
                    for t in range(NT):
                        stt(gat[:, t, 0:E], nrow[:, 0, :], nodecol[:, t:t + 1], gat[:, t, E:2 * E].bitcast(F32), ALU.is_equal, ALU.add)
                else:
                    for t in range(ET):
                        ts(scat[:, t, :], nodegrid, ncol[:, t, 0:1], None, ALU.is_equal)
                    dve.wait_ge(S.ld_a, 16)
                    ts(hm[:, 0:HEADS], small[:, 12:12 + HEADS], 0.0, None, ALU.is_ge)
                    ts(hm[:, HEADS:2 * HEADS], small[:, 12:12 + HEADS], float(DH - 1), small[:, 5:6], ALU.is_le, ALU.mult).then_inc(S.ed_sb, 1)
                    dve.wait_ge(S.ed_sb, 4)
                    for b in range(GB):
                        mm = tt(apad[:, b, b * HEADS:(b + 1) * HEADS], hm[:, 0:HEADS], hm[:, HEADS:2 * HEADS], ALU.mult)
                    mm.then_inc(S.ed_done, 1)

            def setup_logs():
                dve.wait_ge(S.ed_picked, 16 * ET)
                ts(picked[:, :], picked[:, :], LOG_EPS, None, ALU.add).then_inc(S.ed_log, 1)
                dve.wait_ge(S.ed_pick, 1)
                for t in range(ET):
                    mm = ts(logb[:, t, :], ident[:, 0:GH], 0.0, picked[:, t:t + 1], ALU.mult, ALU.add)
                mm.then_inc(S.ed_log, 1)

            def setup_logs_out():
                dve.wait_ge(S.lg_mm, 1)
                dve.tensor_copy(lgrow[:, :], PL[0][0:GH, 0:E]).then_inc(S.ed_done, 1)

            def first_body():
                setup_zt(-1)
                powers(0, 0, 0, 1)
                setup_zt(0)
                powers(0, 0, 1, 2)
                setup_zt(1)
                powers(0, 0, 2, 3)
                setup_zt(2)
                powers(0, 1, 0, 1)
                setup_zt(3)
                setup_zt(4)
                powers(0, 1, 1, 2)
                setup_zt(5)
                setup_zt(6)
                setup_zt(7)
                setup_ccols()
                powers(0, 1, 2, 3)
                square_low(3, 0)
                square_low(3, 1)
                x0_norm(0, 2)
                square_low(3, 2)
                x0_low(0, 2)
                setup_z()
                square_low(3, 3)
                setup_ones()
                for t in range(NT):
                    blocks(0, 0, t, t + 1)
                    first_stats(1, t)
                first_mean(1)
                powers(0, 2, 0, 1)
                first_rstd(1)
                powers(0, 2, 1, 2)
                setup_bias_low(0)
                x0_norm(0, 3)
                setup_edges_rank(0)
                powers(0, 2, 2, 3)
                x0_low(0, 3)
                setup_edges_rank(1)
                for t in range(NT):
                    blocks(0, 1, t, t + 1)
                    first_stats(2, t)
                setup_bias_low(1)
                first_mean(2)
                powers(0, 3, 0, 1)
                first_rstd(2)
                setup_edges_rank(2)
                powers(0, 3, 1, 2)
                setup_edges_rank(3)
                x0_norm(1, 0)
                powers(0, 3, 2, 3)
                x0_low(1, 0)
                for t in range(NT):
                    blocks(0, 2, t, t + 1)
                    first_stats(3, t)
                first_mean(3)
                setup_edges(0)
                blocks(0, 3, 0, 1)
                first_rstd(3)
                blocks(0, 3, 1, 2)
                setup_edges(1)
                blocks(0, 3, 2, 4)
                middle_sum(0, 0)
                setup_edges(2)
                middle_sum(0, 1)
                middle_low(0, 0)
                setup_edges(3)
                middle_sum(0, 2)
                middle_low(0, 1)
                setup_edges(4)
                middle_sum(0, 3)
                middle_low(0, 2)
                middle_low(0, 3)
                setup_logs()
                x0_norm(1, 1)
                first_layer(0, 0)
                x0_low(1, 1)
                setup_logs_out()
                for t in range(1, NT):
                    first_layer(0, t)
                second_mean(0)

            def body(g, last):
                l = g - 1
                powers(g, 0, 0, 1)
                second_rstd(l)
                powers(g, 0, 1, 2)
                second_norm(l, 0)
                powers(g, 0, 2, 3)
                second_low(l, 0)
                second_norm(l, 1)
                powers(g, 1, 0, 1)
                second_low(l, 1)
                powers(g, 1, 1, 2)
                x0_low(g, 2)
                powers(g, 1, 2, 3)
                blocks(g, 0, 0, 1)
                second_norm(l, 2)
                blocks(g, 0, 1, 2)
                second_low(l, 2)
                blocks(g, 0, 2, 3)
                second_norm(l, 3)
                blocks(g, 0, 3, 4)
                second_low(l, 3)
                powers(g, 2, 0, 2)
                gather(l, 0)
                x0_low(g, 3)
                gather(l, 1)
                powers(g, 2, 2, 3)
                blocks(g, 1, 0, 1)
                leaky(l, 0)
                blocks(g, 1, 1, 4)
                gather(l, 2)
                gather(l, 3)
                powers(g, 3)
                blocks(g, 2, 0, 1)
                leaky(l, 1)
                blocks(g, 2, 1, 4)
                if not last:
                    x0_low(g + 1, 0)
                softmax_max(l)
                softmax_shift(l)
                blocks(g, 3, 0, 2)
                softmax_sum(l, 0)
                blocks(g, 3, 2, 3)
                softmax_sum(l, 1)
                blocks(g, 3, 3, 4)
                softmax_divide(l, 0)
                middle_sum(g, 0)
                softmax_divide(l, 1)
                middle_low(g, 0)
                middle_sum(g, 1)
                attention_low(l)
                middle_low(g, 1)
                middle_sum(g, 2)
                weigh(l, 0)
                weigh(l, 1)
                middle_low(g, 2)
                weigh_low(l, 0)
                middle_sum(g, 3)
                weigh_low(l, 1)
                middle_low(g, 3)
                if not last:
                    x0_low(g + 1, 1)
                for t in range(ET):
                    edge_out(l, t)
                if not last:
                    for t in range(NT):
                        first_layer(g, t)
                        if t:
                            second_layer(l, t - 1)
                    second_mean(g)
                    second_layer(l, NT - 1)

            setup()
            first_body()
            with dve.Fori(1, NG - 1) as g:
                body(g, False)
            body(NG - 1, True)
            l = NG - 1
            for t in range(NT):
                end_first(0, t)
            end_mean(0)
            end_first(1, 0)
            end_rstd(0)
            end_norm(0, 0)
            end_norm(0, 1)
            end_low(0, 0)
            end_first(1, 1)
            end_low(0, 1)
            end_low(0, 2)
            end_first(1, 2)
            end_low(0, 3)
            second_layer(l - 1, 0, True)
            end_first(1, 3)
            end_mean(1)
            second_layer(l - 1, 1, True)
            gather(l, 0, True)
            end_rstd(1)
            gather(l, 1, True)
            end_norm(1, 0)
            end_norm(1, 1)
            end_low(1, 0)
            leaky(l, 0, True)
            end_low(1, 1)
            end_low(1, 2)
            end_soft(0, 0)
            end_low(1, 3)
            end_soft(0, 1)
            second_layer(l - 1, 2, True)
            end_soft(0, 2)
            gather(l, 2, True)
            end_soft(0, 3)
            second_layer(l - 1, 3, True)
            end_soft(0, 4)
            gather(l, 3, True)
            end_soft(0, 5)
            end_soft(0, 6)
            leaky(l, 1, True)
            end_soft(0, 7)
            end_soft(1, 0)
            end_soft(0, 8)
            end_soft(1, 1)
            end_soft(1, 2)
            end_soft(1, 3)
            weigh(l, 0, True)
            end_soft(1, 4)
            weigh_low(l, 0, True)
            end_soft(1, 5)
            end_soft(1, 6)
            end_soft(1, 7)
            end_soft(1, 8)
            end_edges(0)
            weigh(l, 1, True)
            end_second(0, 0)
            weigh_low(l, 1, True)
            end_second(0, 1)
            end_edges(1)
            end_second(0, 2)
            end_second(0, 3)
            for t in range(NT):
                end_second(1, t)


def kernel(x, adj, L0_gnn_alpha_train, L0_gnn_w, L0_gnn_d, L0_gnn_fc_in_w, L0_gnn_fc_in_b,
           L1_gnn_W_lin, L1_gnn_W_val, L1_gnn_a, L1_gnn_W_out, L1_gnn_src, L1_gnn_dst):
    import numpy as np
    import concourse.bacc as bacc
    from concourse.bass_utils import run_bass_kernel_spmd

    given = {"x": x, "adj": adj, "alpha": L0_gnn_alpha_train, "w": L0_gnn_w, "d": L0_gnn_d, "fc_w": L0_gnn_fc_in_w,
             "fc_b": L0_gnn_fc_in_b, "W_lin": L1_gnn_W_lin, "W_val": L1_gnn_W_val, "a": L1_gnn_a,
             "W_out": L1_gnn_W_out, "src": L1_gnn_src, "dst": L1_gnn_dst}
    nc = bacc.Bacc("TRN2", target_bir_lowering=False, num_devices=1)
    arrays, args = {}, []
    for name, value in given.items():
        v = np.ascontiguousarray(value)
        arrays[f"in_{name}"] = v
        args.append(nc.dram_tensor(f"in_{name}", v.shape, mybir.dt.from_np(v.dtype), kind="ExternalInput").ap())
    out = nc.dram_tensor("out", arrays["in_x"].shape, F32, kind="ExternalOutput").ap()
    gnn_two_layers(nc, *args, out)
    return run_bass_kernel_spmd(nc, [arrays], core_ids=[0]).results[0]["out"]
```
